# Optimizing a Trainium2 kernel written in Bass

```python
import numpy as np
import jax
import jax.numpy as jnp

def _softmax(x, axis=-1):
    return jax.nn.softmax(x, axis=axis)

def _gelu(x):
    return jax.nn.gelu(x, approximate=True)

def _silu(x):
    return jax.nn.silu(x)

def _sigmoid(x):
    return jax.nn.sigmoid(x)

def _layernorm(x, axis=-1, eps=1e-05):
    m = jnp.mean(x, axis=axis, keepdims=True)
    v = jnp.var(x, axis=axis, keepdims=True)
    return (x - m) / jnp.sqrt(v + eps)

def _scatter_add(tgt, idx, src, axis=0):
    return tgt.at[idx].add(src)

def _segment_sum(src, seg, n):
    return jax.ops.segment_sum(src, seg, n)
kernel_name = 'mk_gnn_ffn_d1_gnn_r64_79c2c3'

def setup_inputs(seed: int=0):
    np.random.seed(seed)
    _w = jnp.asarray

    def _rec_inputs():
        import jax
        import jax.numpy as jnp
        _gk = jax.random.key(seed)
        x = -8.776e-05 + 1 * jax.random.normal(jax.random.fold_in(_gk, 1), (20000, 256), jnp.float32)
        src = jax.random.randint(jax.random.fold_in(_gk, 2), (10000,), 0, 20000, jnp.int32)
        dst = jax.random.randint(jax.random.fold_in(_gk, 3), (10000,), 0, 20000, jnp.int32)
        _o = jnp.argsort(dst, stable=True)
        src = src[_o]
        dst = dst[_o]
        return (x, src, dst)
    x, src, dst = _rec_inputs()

    def _L0_gnn_setup():
        import jax, jax.numpy as jnp
        import numpy as np
        N = 20000
        E = 5000
        IN = 256
        HID = 512
        OUT = 256
        H = 4
        C1 = HID // 2 // H
        NEG_SLOPE = 0.2

        def gat_conv(x, src, dst, W, a_s, a_d, b, heads, ch):
            h = (x @ W).reshape(-1, heads, ch)
            al_s = jnp.einsum('nhc,hc->nh', h, a_s)
            al_d = jnp.einsum('nhc,hc->nh', h, a_d)
            e = jax.nn.leaky_relu(al_s[src] + al_d[dst], NEG_SLOPE)
            m = jax.ops.segment_max(e, dst, num_segments=N)
            ex = jnp.exp(e - m[dst])
            denom = jax.ops.segment_sum(ex, dst, num_segments=N)
            alpha = ex / denom[dst]
            out = jax.ops.segment_sum(alpha[:, :, None] * h[src], dst, num_segments=N)
            return out.reshape(-1, heads * ch) + b
        key = jax.random.key(seed)
        ks = jax.random.split(key, 10)
        s = 0.1
        return {'x': jax.random.normal(ks[0], (N, IN), jnp.float32), 'edge_index': jax.random.randint(ks[1], (2, E), 0, N, dtype=jnp.int64), 'W1': jax.random.normal(ks[2], (IN, H * C1), jnp.float32) * s, 'att_src1': jax.random.normal(ks[3], (H, C1), jnp.float32) * s, 'att_dst1': jax.random.normal(ks[4], (H, C1), jnp.float32) * s, 'b1': jax.random.normal(ks[5], (H * C1,), jnp.float32) * s, 'W2': jax.random.normal(ks[6], (H * C1, OUT), jnp.float32) * s, 'att_src2': jax.random.normal(ks[7], (1, OUT), jnp.float32) * s, 'att_dst2': jax.random.normal(ks[8], (1, OUT), jnp.float32) * s, 'b2': jax.random.normal(ks[9], (OUT,), jnp.float32) * s}
    _L0_gnn_all = _L0_gnn_setup()
    _L0_gnn_in = {k: v for k, v in _L0_gnn_all.items() if k in ('W1', 'att_src1', 'att_dst1', 'b1', 'W2', 'att_src2', 'att_dst2', 'b2')}
    del _L0_gnn_all

    def _L0_ffn_setup():
        import jax, jax.numpy as jnp
        import numpy as np
        BN_EPS = 0.001

        def _bn(h, g, b, m, v):
            return g * (h - m) * jax.lax.rsqrt(v + BN_EPS) + b
        key = jax.random.key(seed)
        ks = jax.random.split(key, 8)
        B, F, Df = (256, 64, 256)
        E, H, D = (8, 256, 256)
        s1 = 1.0 / np.sqrt(Df)
        s2 = 1.0 / np.sqrt(H)
        return {'x': jax.random.normal(ks[0], (B, F, Df), jnp.float32), 'Wr': jax.random.normal(ks[1], (Df, E), jnp.float32) * s1, 'br': jnp.zeros((E,), jnp.float32), 'W1': jax.random.normal(ks[2], (E, Df, H), jnp.float32) * s1, 'b1': jnp.zeros((E, H), jnp.float32), 'g1': jnp.ones((E, H), jnp.float32), 'be1': jnp.zeros((E, H), jnp.float32), 'm1': jnp.zeros((E, H), jnp.float32), 'v1': jnp.ones((E, H), jnp.float32), 'W2': jax.random.normal(ks[3], (E, H, H), jnp.float32) * s2, 'b2': jnp.zeros((E, H), jnp.float32), 'g2': jnp.ones((E, H), jnp.float32), 'be2': jnp.zeros((E, H), jnp.float32), 'm2': jnp.zeros((E, H), jnp.float32), 'v2': jnp.ones((E, H), jnp.float32), 'Wo': jax.random.normal(ks[4], (E, H, D), jnp.float32) * s2, 'bo': jnp.zeros((E, D), jnp.float32)}
    _L0_ffn_all = _L0_ffn_setup()
    _L0_ffn_in = {k: v for k, v in _L0_ffn_all.items() if k in ('Wr', 'br', 'W1', 'b1', 'g1', 'be1', 'm1', 'v1', 'W2', 'b2', 'g2', 'be2', 'm2', 'v2', 'Wo', 'bo')}
    del _L0_ffn_all
    return {'x': x, 'src': src, 'dst': dst, 'L0_gnn_W1': _L0_gnn_in['W1'], 'L0_gnn_att_src1': _L0_gnn_in['att_src1'], 'L0_gnn_att_dst1': _L0_gnn_in['att_dst1'], 'L0_gnn_b1': _L0_gnn_in['b1'], 'L0_gnn_W2': _L0_gnn_in['W2'], 'L0_gnn_att_src2': _L0_gnn_in['att_src2'], 'L0_gnn_att_dst2': _L0_gnn_in['att_dst2'], 'L0_gnn_b2': _L0_gnn_in['b2'], 'L0_ffn_Wr': _L0_ffn_in['Wr'], 'L0_ffn_br': _L0_ffn_in['br'], 'L0_ffn_W1': _L0_ffn_in['W1'], 'L0_ffn_b1': _L0_ffn_in['b1'], 'L0_ffn_g1': _L0_ffn_in['g1'], 'L0_ffn_be1': _L0_ffn_in['be1'], 'L0_ffn_m1': _L0_ffn_in['m1'], 'L0_ffn_v1': _L0_ffn_in['v1'], 'L0_ffn_W2': _L0_ffn_in['W2'], 'L0_ffn_b2': _L0_ffn_in['b2'], 'L0_ffn_g2': _L0_ffn_in['g2'], 'L0_ffn_be2': _L0_ffn_in['be2'], 'L0_ffn_m2': _L0_ffn_in['m2'], 'L0_ffn_v2': _L0_ffn_in['v2'], 'L0_ffn_Wo': _L0_ffn_in['Wo'], 'L0_ffn_bo': _L0_ffn_in['bo']}

def reference(x, src, dst, L0_gnn_W1, L0_gnn_att_src1, L0_gnn_att_dst1, L0_gnn_b1, L0_gnn_W2, L0_gnn_att_src2, L0_gnn_att_dst2, L0_gnn_b2, L0_ffn_Wr, L0_ffn_br, L0_ffn_W1, L0_ffn_b1, L0_ffn_g1, L0_ffn_be1, L0_ffn_m1, L0_ffn_v1, L0_ffn_W2, L0_ffn_b2, L0_ffn_g2, L0_ffn_be2, L0_ffn_m2, L0_ffn_v2, L0_ffn_Wo, L0_ffn_bo):
    import jax
    import jax.numpy as jnp

    def _L0_gnn_ref(x, edge_index, W1, att_src1, att_dst1, b1, W2, att_src2, att_dst2, b2):
        import jax, jax.numpy as jnp
        import numpy as np
        N = 20000
        E = 5000
        IN = 256
        HID = 512
        OUT = 256
        H = 4
        C1 = HID // 2 // H
        NEG_SLOPE = 0.2

        def gat_conv(x, src, dst, W, a_s, a_d, b, heads, ch):
            h = (x @ W).reshape(-1, heads, ch)
            al_s = jnp.einsum('nhc,hc->nh', h, a_s)
            al_d = jnp.einsum('nhc,hc->nh', h, a_d)
            e = jax.nn.leaky_relu(al_s[src] + al_d[dst], NEG_SLOPE)
            m = jax.ops.segment_max(e, dst, num_segments=N)
            ex = jnp.exp(e - m[dst])
            denom = jax.ops.segment_sum(ex, dst, num_segments=N)
            alpha = ex / denom[dst]
            out = jax.ops.segment_sum(alpha[:, :, None] * h[src], dst, num_segments=N)
            return out.reshape(-1, heads * ch) + b
        loop = jnp.arange(N, dtype=edge_index.dtype)
        src = jnp.concatenate([edge_index[0], loop])
        dst = jnp.concatenate([edge_index[1], loop])
        h1 = jax.nn.relu(gat_conv(x, src, dst, W1, att_src1, att_dst1, b1, H, C1))
        return gat_conv(h1, src, dst, W2, att_src2, att_dst2, b2, 1, OUT)

    def _L0_ffn_ref(x, Wr, br, W1, b1, g1, be1, m1, v1, W2, b2, g2, be2, m2, v2, Wo, bo):
        import jax, jax.numpy as jnp
        import numpy as np
        BN_EPS = 0.001

        def _bn(h, g, b, m, v):
            return g * (h - m) * jax.lax.rsqrt(v + BN_EPS) + b
        feat = jnp.mean(x, axis=0)
        w = jax.nn.softmax(feat @ Wr + br, axis=-1)
        h = jnp.einsum('bfd,edh->bfeh', x, W1) + b1
        h = jax.nn.relu(_bn(h, g1, be1, m1, v1))
        h = jnp.einsum('bfeh,ehk->bfek', h, W2) + b2
        h = jax.nn.relu(_bn(h, g2, be2, m2, v2))
        y = jnp.einsum('bfeh,ehd->bfed', h, Wo) + bo
        return jnp.einsum('bfed,fe->bfd', y, w)
    edge_index = jnp.stack([src, dst])
    x = x + _L0_gnn_ref(_layernorm(x, axis=-1), edge_index, L0_gnn_W1, L0_gnn_att_src1, L0_gnn_att_dst1, L0_gnn_b1, L0_gnn_W2, L0_gnn_att_src2, L0_gnn_att_dst2, L0_gnn_b2)
    x = x + _L0_ffn_ref(_layernorm(x, axis=-1)[None], L0_ffn_Wr, L0_ffn_br, L0_ffn_W1, L0_ffn_b1, L0_ffn_g1, L0_ffn_be1, L0_ffn_m1, L0_ffn_v1, L0_ffn_W2, L0_ffn_b2, L0_ffn_g2, L0_ffn_be2, L0_ffn_m2, L0_ffn_v2, L0_ffn_Wo, L0_ffn_bo)[0]
    return x

_drawn_inputs = setup_inputs


def setup_inputs(seed=0):
    import zlib

    import numpy as np

    out = dict(_drawn_inputs(seed))
    spreads = {'L0_ffn_br': (0.0, 0.497),
     'L0_ffn_b1': (0.0, 0.63),
     'L0_ffn_g1': (1.0, 0.6),
     'L0_ffn_be1': (0.0, 0.648),
     'L0_ffn_m1': (0.0, 0.644),
     'L0_ffn_v1': (1.0, 0.6),
     'L0_ffn_b2': (0.0, 0.446),
     'L0_ffn_g2': (1.0, 0.589),
     'L0_ffn_be2': (0.0, 0.471),
     'L0_ffn_m2': (0.0, 0.454),
     'L0_ffn_v2': (1.0, 0.6),
     'L0_ffn_bo': (0.0, 0.328)}
    factors = {}
    for name, (base, spread) in spreads.items():
        noise = np.random.default_rng([zlib.crc32(name.encode()), seed]).standard_normal(out[name].shape)
        drawn = base * np.exp(spread * noise) if base else spread * noise
        out[name] = jnp.asarray(drawn.astype(out[name].dtype))
    for name, factor in factors.items():
        out[name] = (out[name] * factor).astype(out[name].dtype)
    return out
```

```python
import numpy as np
import concourse.bass as bass
from concourse import mybir
from contextlib import ExitStack

F32 = mybir.dt.float32
F32R = mybir.dt.float32r
BF16 = mybir.dt.bfloat16
I32 = mybir.dt.int32
ALU = mybir.AluOpType
ACT = mybir.ActivationFunctionType
AX = mybir.AxisListType

P = 128
LN_EPS = 1e-5
BN_EPS = 1e-3
SLOPE = 0.2
BIG = 3e38
NOWHERE = 1 << 20
TILE = 128
GROUP = 8
SUPER = 4


def ring(eng, count, front, back):
    front(0, 0, 0)
    for i in range(2):
        front(i + 1, (i + 1) % 2, (i + 1) // 2)
        back(i, i % 2, i // 2)
    turns = (count - 1) // 2
    with eng.Fori(1, turns) as k:
        front(2 * k + 1, 1, k)
        back(2 * k, 0, k)
        front(2 * k + 2, 0, k + 1)
        back(2 * k + 1, 1, k)
    for i in range(2 * turns, count):
        if i + 1 < count:
            front(i + 1, (i + 1) % 2, (i + 1) // 2)
        back(i, i % 2, i // 2)


def wait_count(eng, sem, count):
    if isinstance(count, int) and count <= 0:
        return
    eng.wait_ge(sem, count)


def hold(eng, sem, count, passed):
    eng.wait_ge(sem, count)
    eng.sem_inc(passed, 1)


def stores_later(store, count):
    def back(i, b, k):
        if isinstance(i, int) and i == 0:
            return
        store(i - 1, 1 - b, k - 1 + b)
        if isinstance(i, int) and i == count - 1:
            store(i, b, k)
    return back


class Chain:

    def __init__(self, eng, sem, per_round):
        self.eng, self.sem, self.per_round, self.n, self.base = eng, sem, per_round, 0, 0

    def round(self, i):
        self.base, self.n = i * self.per_round, 0

    def link(self, ins):
        self.n += 1
        ins.then_inc(self.sem, 1)
        self.eng.wait_ge(self.sem, self.base + self.n)

    def close(self):
        assert self.n == self.per_round, (self.n, self.per_round)


def gnn_ffn(nc, x, src, dst, W1, as1, ad1, b1, W2, as2, ad2, b2, Wr, br,
            fW1, fb1, g1, be1, m1, v1, fW2, fb2, g2, be2, m2, v2, Wo, bo, out):
    N, D = x.shape
    E = src.shape[0]
    HEADS, CH = as1.shape
    HID = HEADS * CH
    NE, _, FH = fW1.shape
    KD = D // P
    KH = FH // P
    SROWS = P * SUPER
    NSUPER = -(-N // SROWS)
    TAIL = N - (NSUPER - 1) * SROWS
    NT = NSUPER * SROWS // TILE
    NG = NT // GROUP
    NPAD = NT * TILE
    EROWS = 125
    ECOLS = E // EROWS
    assert EROWS * ECOLS == E and NT % GROUP == 0 and TAIL % SUPER == 0 and TAIL <= P
    W1COLS = HID + 2 * HEADS
    W2COLS = D + 2
    top = ExitStack()

    def dram(name, shape, dt=F32):
        return nc.dram_tensor(name, shape, dt, kind="Internal").ap()

    edge_list = dram("edge_list", [E + TILE, 2], I32)
    h1_table = dram("h1_table", [NPAD, W1COLS])
    own1_table = dram("own1_table", [NPAD, W1COLS])
    h2_table = dram("h2_table", [NPAD, W2COLS])
    own2_table = dram("own2_table", [NPAD, W2COLS])
    x2_table = dram("x2_table", [NPAD, D])
    softmax_state = dram("softmax_state", [NPAD, 2 * HEADS])

    def sem(name, ctx=top):
        return ctx.enter_context(nc.semaphore(name))

    def sb(ctx, name, shape, dt=F32):
        return ctx.enter_context(nc.sbuf_tensor(name, shape, dt))

    def ps(ctx, name, shape, dt=F32):
        return ctx.enter_context(nc.psum_tensor(name, shape, dt))

    with top:
        ident = sb(top, "ident", [P, P])
        iota_row = sb(top, "iota_row", [P, TILE])
        tile_base = sb(top, "tile_base", [P, NT])
        eps_half = sb(top, "eps_half", [P, 16])
        windows = sb(top, "windows", [P, NT, 2], I32)
        place = sb(top, "place", [P, NT])
        starts = sb(top, "starts", [P, NT + 1])
        starts_i = sb(top, "starts_i", [1, NT], I32)
        bad = sb(top, "bad", [P, 1])
        bad_i = sb(top, "bad_i", [1, 1], I32)
        W1x = sb(top, "W1x", [P, KD, W1COLS])
        W2x = sb(top, "W2x", [P, HID // P, W2COLS])
        b1_col = sb(top, "b1_col", [P, HID // P])
        b2_row = sb(top, "b2_row", [P, D])
        wh = {n: sb(top, f"{n}_hi", [P, NE, KD, FH], F32R) for n in ("fW1", "fW2", "Wo")}
        wl = {n: sb(top, f"{n}_lo", [P, NE, KD, FH], F32R) for n in ("fW1", "fW2", "Wo")}
        scale = [sb(top, f"bn_scale{n}", [P, NE, KH]) for n in (1, 2)]
        shift = [sb(top, f"bn_shift{n}", [P, NE, KH]) for n in (1, 2)]
        Wr_hi = sb(top, "Wr_hi", [P, KD, NE], F32R)
        Wr_lo = sb(top, "Wr_lo", [P, KD, NE], F32R)
        br_row = sb(top, "br_row", [P, NE])
        bo_sb = sb(top, "bo_sb", [NE, D])

        phase_edges_and_layer1(locals())
        phase_edge_by_edge(locals(), 1)
        phase_aggregate(locals(), 1)
        phase_edge_by_edge(locals(), 2)
        phase_aggregate(locals(), 2)
        phase_experts(locals())


def row_view(table, i, rows=P * SUPER, per=SUPER):
    return table[bass.ds(i * P * SUPER, rows), :].rearrange("(p j) d -> p j d", j=per)


def phase_edges_and_layer1(v):
    nc, sem, sb, ps = v["nc"], v["sem"], v["sb"], v["ps"]
    N, D, E, HEADS, CH, HID, NE, FH = (v[n] for n in ("N", "D", "E", "HEADS", "CH", "HID", "NE", "FH"))
    KD, KH, NSUPER, TAIL, NT, EROWS, ECOLS, NPAD = (v[n] for n in ("KD", "KH", "NSUPER", "TAIL", "NT", "EROWS", "ECOLS", "NPAD"))
    W1COLS, W2COLS = v["W1COLS"], v["W2COLS"]
    ident, iota_row, tile_base, windows = v["ident"], v["iota_row"], v["tile_base"], v["windows"]
    starts, starts_i, bad, bad_i = v["starts"], v["starts_i"], v["bad"], v["bad_i"]
    W1x, W2x, eps_half = v["W1x"], v["W2x"], v["eps_half"]
    edge_list, x = v["edge_list"], v["x"]
    wh, wl, scale, shift = v["wh"], v["wl"], v["scale"], v["shift"]
    HCOLS = W1COLS

    with ExitStack() as ctx:
        S = lambda name: sem("a_" + name, ctx)
        xin = [sb(ctx, f"xin{b}", [P, SUPER, D]) for b in range(2)]
        z = [sb(ctx, f"z{b}", [P, SUPER, D]) for b in range(2)]
        zT = [sb(ctx, f"zT{b}", [P, KD, SUPER * P]) for b in range(2)]
        hrow = [sb(ctx, f"hrow{b}", [P, SUPER, HCOLS]) for b in range(2)]
        stats = sb(ctx, "stats", [P, SUPER, 6])
        mv = [sb(ctx, f"mv{b}", [P, SUPER, 2]) for b in range(2)]
        vare = [sb(ctx, f"vare{b}", [P, SUPER]) for b in range(2)]
        rstd = [sb(ctx, f"rstd{b}", [P, SUPER]) for b in range(2)]
        ones_bf = sb(ctx, "ones_bf", [P, P], BF16)
        ends = sb(ctx, "ends", [EROWS, 3, ECOLS], I32)
        dstf = sb(ctx, "dstf", [EROWS, 2, ECOLS])
        pairs = sb(ctx, "pairs", [EROWS, ECOLS, 2], I32)
        pad = sb(ctx, "pad", [1, TILE, 2], I32)
        before = sb(ctx, "before", [EROWS, 4, NT], BF16)
        falls = sb(ctx, "falls", [EROWS, ECOLS])
        falls_any = sb(ctx, "falls_any", [EROWS, 1], BF16)
        sizes = sb(ctx, "sizes", [P, NT])
        over = sb(ctx, "over", [P, 2])
        KHID = HID // P
        att = sb(ctx, "att", [P, KHID, 2 * HEADS])
        att2 = sb(ctx, "att2", [P, D // P, 2])
        W1T = sb(ctx, "W1T", [P, KD, KHID, P])
        W2T = sb(ctx, "W2T", [P, KHID, D // P, P])
        stage = {n: sb(ctx, f"stage_{n}", [P, NE, KD, FH]) for n in wh}
        Wr_sb = sb(ctx, "Wr_sb", [P, KD, NE])
        bn = {n: sb(ctx, f"bn_{n}", [P, NE, KH]) for n in
              ("fb1", "g1", "be1", "m1", "v1", "fb2", "g2", "be2", "m2", "v2")}
        bnt = sb(ctx, "bnt", [P, NE, KH])
        zTp = [ps(ctx, f"zTp{b}", [P, KD, SUPER * P]) for b in range(2)]
        hp = [ps(ctx, f"hp{q}", [P, 512]) for q in range(2)]
        cnt_p = ps(ctx, "cnt_p", [P, 512])
        set_p = ps(ctx, "set_p", [P, 512])

        ends_loaded, params_loaded, wr_loaded, bn_loaded = (
            S(n) for n in ("ends_loaded", "params_loaded", "wr_loaded", "bn_loaded"))
        stage_loaded = {n: S(f"stage_{n}_loaded") for n in wh}
        const_ready, ends_ready, pairs_ready, list_stored = (S(n) for n in ("const_ready", "ends_ready", "pairs_ready", "list_stored"))
        before_ready, before_used, counted, falls_ready, starts_ready = (
            S(n) for n in ("before_ready", "before_used", "counted", "falls_ready", "starts_ready"))
        window_loaded = S("window_loaded")
        pe_set, att_ready, dve_set = S("pe_set"), S("att_ready"), S("dve_set")
        x_loaded = [S(f"x_loaded{b}") for b in range(2)]
        h_stored = [S(f"h_stored{b}") for b in range(2)]
        stats_seen, var_ready, rstd_ready, z_ready, zTp_ready, zT_ready, h_ready, hrow_ready = (
            S(n) for n in ("stats_seen", "var_ready", "rstd_ready", "z_ready", "zTp_ready", "zT_ready", "h_ready", "hrow_ready"))
        stage_split, dve_chain, pool_chain = S("stage_split"), S("dve_chain"), S("pool_chain")
        moments_passed = S("moments_passed")
        last = NSUPER - 1

        block = ctx.enter_context(nc.Block())

        @block.sync
        def _(sp):
            sp.wait_ge(const_ready, 1)
            sp.dma_start(ends[:, 0, :], v["src"].rearrange("(p c) -> p c", c=ECOLS)).then_inc(ends_loaded, 16)
            sp.dma_start(ends[:, 1, :], v["dst"].rearrange("(p c) -> p c", c=ECOLS)).then_inc(ends_loaded, 16)
            body = (EROWS - 1) * ECOLS
            sp.dma_start(ends[0:EROWS - 1, 2, :], v["dst"][1:1 + body].rearrange("(p c) -> p c", c=ECOLS)).then_inc(ends_loaded, 16)
            sp.dma_start(ends[EROWS - 1:EROWS, 2, 0:ECOLS - 1],
                         v["dst"][1 + body:E].rearrange("(p c) -> p c", p=1)).then_inc(ends_loaded, 16)
            sp.dma_start(edge_list[E:E + TILE, :].rearrange("(o e) t -> o e t", o=1), pad[:]).then_inc(list_stored, 16)

            def load(i, b, k):
                wait_count(sp, z_ready, i - 1)
                if isinstance(i, int) and i == last:
                    src = row_view(x, i, TAIL)
                    sp.dma_start(xin[b][0:TAIL // SUPER], src).then_inc(x_loaded[b], 16)
                else:
                    sp.dma_start(xin[b][:], row_view(x, i)).then_inc(x_loaded[b], 16)

            def store(i, b, k):
                if isinstance(i, int) and i == 0:
                    sp.wait_ge(pairs_ready, 1)
                    sp.dma_start(edge_list[0:E, :].rearrange("(p c) t -> p c t", c=ECOLS), pairs[:]).then_inc(list_stored, 16)
                    sp.wait_ge(list_stored, 32)
                    sp.wait_ge(starts_ready, 1)
                for j in range(NT // NSUPER):
                    t = i * (NT // NSUPER) + j
                    first = sp.value_load(starts_i[0:1, bass.ds(t, 1)], min_val=0, max_val=E)
                    sp.dma_start(windows[:, bass.ds(t, 1), :],
                                 edge_list[bass.ds(first, TILE), :].unsqueeze(1)).then_inc(window_loaded, 16)
                sp.wait_ge(hrow_ready, (i + 1) * SUPER)
                sp.dma_start(row_view(v["h1_table"], i), hrow[b][:]).then_inc(h_stored[b], 16)
                sp.dma_start(row_view(v["own1_table"], i), hrow[b][:]).then_inc(h_stored[b], 16)

            ring(sp, NSUPER, load, stores_later(store, NSUPER))
            sp.wait_ge(window_loaded, 16 * NT)
            for b in range(2):
                sp.wait_ge(h_stored[b], 32 * (NSUPER // 2))

        @block.gpsimd
        def _(pool):
            nc.gpsimd.iota(iota_row[:], pattern=[[1, TILE]], base=0, channel_multiplier=0,
                           allow_small_or_imprecise_dtypes=True)
            nc.gpsimd.iota(tile_base[:], pattern=[[TILE, NT]], base=0, channel_multiplier=0,
                           allow_small_or_imprecise_dtypes=True)
            nc.gpsimd.memset(ends[:], NOWHERE)
            nc.gpsimd.memset(pad[:, :, 0:1], 0)
            nc.gpsimd.memset(pad[:, :, 1:2], NOWHERE)
            nc.gpsimd.memset(eps_half[:], -0.5)
            nc.gpsimd.memset(ident[:], 0.0).then_inc(pool_chain, 1)
            pool.wait_ge(pool_chain, 1)
            nc.gpsimd.affine_select(out=ident[:], in_=ident[:], compare_op=ALU.not_equal, fill=1.0, base=0,
                                    pattern=[[-1, P]], channel_multiplier=1).then_inc(const_ready, 1)
            pool.wait_ge(ends_loaded, 64)
            nc.gpsimd.tensor_copy(pairs[:, :, 0], ends[:, 0, :])
            nc.gpsimd.tensor_copy(pairs[:, :, 1], ends[:, 1, :]).then_inc(pairs_ready, 1)

            pool.wait_ge(bn_loaded, 320)
            n = 1
            for l in range(2):
                b_, g_, be_, m_, v_ = (bn[q] for q in (("fb1", "g1", "be1", "m1", "v1"), ("fb2", "g2", "be2", "m2", "v2"))[l])
                half = eps_half[:].rearrange("p (e c) -> p e c", c=KH)
                for op in (lambda: nc.gpsimd.tensor_scalar(bnt[:], v_[:], BN_EPS, None, ALU.add),
                           lambda: nc.gpsimd.tensor_tensor(bnt[:], bnt[:], half, ALU.pow),
                           lambda: nc.gpsimd.tensor_tensor(scale[l][:], g_[:], bnt[:], ALU.mult),
                           lambda: nc.gpsimd.tensor_tensor(b_[:], b_[:], m_[:], ALU.subtract),
                           lambda: nc.gpsimd.tensor_tensor(b_[:], b_[:], scale[l][:], ALU.mult),
                           lambda: nc.gpsimd.tensor_tensor(shift[l][:], be_[:], b_[:], ALU.add)):
                    op().then_inc(pool_chain, 1)
                    n += 1
                    pool.wait_ge(pool_chain, n)

            for q, name in enumerate(wh):
                pool.wait_ge(stage_loaded[name], 16 * NE)
                nc.gpsimd.tensor_copy(wh[name][:], stage[name][:]).then_inc(stage_split, 1)
                pool.wait_ge(stage_split, q + 1)
                nc.gpsimd.tensor_tensor(wl[name][:], stage[name][:], wh[name][:].bitcast(F32), ALU.subtract)

            def power(i, b, k):
                pool.wait_ge(var_ready, i + 1)
                nc.gpsimd.tensor_tensor(rstd[b][:], vare[b][:], eps_half[:, 0:SUPER], ALU.pow).then_inc(rstd_ready, 1)

            ring(pool, NSUPER, power, lambda i, b, k: None)

        @block.scalar
        def _(act):
            few = ctx.enter_context(nc.allow_non_contiguous_dma(reason='vectors of parameters, once'))
            for k in range(KD):
                act.dma_start(W1x[:, k, 0:HID], v["W1"][k * P:(k + 1) * P, :]).then_inc(params_loaded, 16)
            for k in range(KHID):
                act.dma_start(W2x[:, k, 0:D], v["W2"][k * P:(k + 1) * P, :]).then_inc(params_loaded, 16)
            act.wait_ge(att_ready, 1)
            for h in range(HEADS):
                for s, a in enumerate((v["as1"], v["ad1"])):
                    c, r = h * CH // P, h * CH % P
                    act.dma_start(att[r:r + CH, c, s * HEADS + h:s * HEADS + h + 1],
                                  a[h:h + 1, :].rearrange("o c -> c o")).then_inc(params_loaded, 16)
            for s, a in enumerate((v["as2"], v["ad2"])):
                for k in range(D // P):
                    act.dma_start(att2[:, k, s:s + 1], a[0:1, k * P:(k + 1) * P].rearrange("o c -> c o")).then_inc(params_loaded, 16)
            act.dma_start(v["b1_col"][:], v["b1"].rearrange("(k c) -> c k", c=P)).then_inc(params_loaded, 16)
            act.dma_start(v["b2_row"][:], v["b2"].partition_broadcast(P)).then_inc(params_loaded, 16)
            act.dma_start(v["br_row"][:], v["br"].partition_broadcast(P)).then_inc(params_loaded, 16)
            act.dma_start(v["bo_sb"][:], v["bo"]).then_inc(params_loaded, 16)
            act.dma_start(Wr_sb[:], v["Wr"].rearrange("(k p) e -> p k e", p=P)).then_inc(wr_loaded, 16)
            for q in bn:
                for k in range(KH):
                    act.dma_start(bn[q][:, :, k], v[q][:, k * P:(k + 1) * P].rearrange("e p -> p e")).then_inc(bn_loaded, 16)

            for name in wh:
                for e in range(NE):
                    act.dma_start(stage[name][:, e], v[name][e].rearrange("(k p) n -> p k n", p=P)).then_inc(stage_loaded[name], 16)

            def evac_zT(i, b, k):
                act.wait_ge(zTp_ready, i + 1)
                wait_count(act, h_ready, (i - 1) * SUPER)
                nc.scalar.activation(zT[b][:], zTp[b][:], ACT.Copy).then_inc(zT_ready, 1)

            def evac_h(i, b, k):
                if not (isinstance(i, int) and i < 2):
                    act.wait_ge(h_stored[b], 32 * k)
                for j in range(SUPER):
                    act.wait_ge(h_ready, i * SUPER + j + 1)
                    nc.scalar.activation(hrow[b][:, j, :], hp[j % 2][:, 0:HCOLS], ACT.Copy).then_inc(hrow_ready, 1)

            ring(act, NSUPER, evac_zT, evac_h)

        @block.vector
        def _(dve):
            setup = Chain(dve, dve_set, 0)
            nc.vector.memset(att[:], 0.0).then_inc(att_ready, 1)
            nc.vector.memset(ones_bf[:], 1.0)
            dve.wait_ge(ends_loaded, 64)
            setup.link(nc.vector.tensor_copy(dstf[:], ends[:, 1:3, :]))
            setup.link(nc.vector.tensor_tensor(falls[:], dstf[:, 0, :], dstf[:, 1, :], ALU.is_gt))
            nc.vector.tensor_reduce(falls_any[:], falls[:], axis=AX.X, op=ALU.max).then_inc(falls_ready, 1)
            dve.wait_ge(const_ready, 1)
            for c in range(ECOLS):
                if c >= 4:
                    dve.wait_ge(before_used, c - 3)
                nc.vector.tensor_scalar(before[:, c % 4, :], tile_base[0:EROWS, :], dstf[:, 0, c:c + 1], None,
                                        ALU.is_gt).then_inc(before_ready, 1)
            dve.wait_ge(counted, 1)
            nc.vector.tensor_copy(starts[:, 0:NT], cnt_p[:, 0:NT])
            setup.link(nc.vector.memset(starts[:, NT:NT + 1], float(E)))
            nc.vector.tensor_copy(starts_i[:], starts[0:1, 0:NT])
            setup.link(nc.vector.tensor_tensor(sizes[:], starts[:, 1:NT + 1], starts[:, 0:NT], ALU.subtract))
            setup.link(nc.vector.tensor_reduce(over[:, 0:1], sizes[:], axis=AX.X, op=ALU.max))
            setup.link(nc.vector.tensor_scalar(over[:, 1:2], over[:, 0:1], float(TILE) + 0.5, None, ALU.is_gt))
            setup.link(nc.vector.tensor_tensor(bad[:], cnt_p[:, NT:NT + 1], over[:, 1:2], ALU.add))
            setup.link(nc.vector.tensor_scalar(bad[:], bad[:], 0.5, None, ALU.is_gt))
            nc.vector.tensor_copy(bad_i[:], bad[0:1, :]).then_inc(starts_ready, 1)
            for n, wt in enumerate((W1T, W2T)):
                dve.wait_ge(pe_set, n + 1)
                nc.vector.tensor_copy(wt[:].rearrange("p a b c -> p (a b c)"), set_p[:]).then_inc(att_ready, 1)
            dve.wait_ge(pe_set, 3)
            nc.vector.tensor_copy(W1x[:, :, HID:W1COLS], set_p[:, 0:KD * 2 * HEADS].rearrange("p (k s) -> p k s", k=KD))
            nc.vector.tensor_copy(W2x[:, :, D:W2COLS], set_p[:, 64:64 + 2 * KHID].rearrange("p (k s) -> p k s", k=KHID)).then_inc(att_ready, 1)
            dve.wait_ge(wr_loaded, 16)
            setup.link(nc.vector.tensor_copy(v["Wr_hi"][:], Wr_sb[:]))
            nc.vector.tensor_tensor(v["Wr_lo"][:], Wr_sb[:], v["Wr_hi"][:].bitcast(F32), ALU.subtract)

            chain = Chain(dve, dve_chain, 2)

            def moments(i, b, k):
                chain.round(i)
                dve.wait_ge(x_loaded[b], 16 * k + 16)
                for j in range(SUPER):
                    ins = nc.vector.bn_stats(stats[:, j, :], xin[b][:, j, :])
                chain.link(ins)
                dve.sem_inc(moments_passed, 1)
                for j in range(SUPER):
                    ins = nc.vector.bn_aggr(mv[b][:, j, :], stats[:, j, :])
                chain.link(ins)
                chain.close()
                nc.vector.tensor_scalar(vare[b][:], mv[b][:, :, 1], LN_EPS, None, ALU.add).then_inc(var_ready, 1)

            def normalise(i, b, k):
                dve.wait_ge(rstd_ready, i + 1)
                wait_count(dve, zTp_ready, i - 1)
                for j in range(SUPER):
                    ins = nc.vector.tensor_scalar(z[b][:, j, :], xin[b][:, j, :], mv[b][:, j, 0:1], rstd[b][:, j:j + 1],
                                                  ALU.subtract, ALU.mult)
                ins.then_inc(z_ready, 1)

            ring(dve, NSUPER, moments, normalise)

        @block.tensor
        def _(pe):
            for c in range(ECOLS):
                pe.wait_ge(before_ready, c + 1)
                nc.tensor.matmul(cnt_p[:, 0:NT], ones_bf[0:EROWS, :], before[:, c % 4, :], start=(c == 0),
                                 stop=(c == ECOLS - 1)).then_inc(before_used, 1)
            pe.wait_ge(falls_ready, 1)
            nc.tensor.matmul(cnt_p[:, NT:NT + 1], ones_bf[0:EROWS, :], falls_any[:], start=True, stop=True,
                             skip_group_check=True).then_inc(counted, 1)
            pe.wait_ge(params_loaded, 16 * (KD + KHID + 2 * HEADS + 2 * (D // P) + 4))
            pe.wait_ge(const_ready, 1)
            for n, (w, inner, outer) in enumerate(((W1x, KD, KHID), (W2x, KHID, D // P))):
                if n:
                    pe.wait_ge(att_ready, n + 1)
                for k in range(inner):
                    for c in range(outer):
                        q = k * outer + c
                        ins = nc.tensor.transpose(set_p[:, q * P:(q + 1) * P], w[:, k, c * P:(c + 1) * P], ident[:])
                ins.then_inc(pe_set, 1)
            pe.wait_ge(att_ready, 3)
            for k in range(KD):
                for c in range(KHID):
                    nc.tensor.matmul(set_p[:, k * 2 * HEADS:(k + 1) * 2 * HEADS], W1T[:, k, c, :], att[:, c, :],
                                     start=(c == 0), stop=(c == KHID - 1))
            for k in range(KHID):
                for c in range(D // P):
                    ins = nc.tensor.matmul(set_p[:, 64 + 2 * k:66 + 2 * k], W2T[:, k, c, :], att2[:, c, :],
                                           start=(c == 0), stop=(c == D // P - 1))
            ins.then_inc(pe_set, 1)
            pe.wait_ge(att_ready, 4)

            def transpose_z(i, b, k):
                pe.wait_ge(z_ready, i + 1)
                wait_count(pe, zT_ready, i - 1)
                for j in range(SUPER):
                    for c in range(KD):
                        ins = nc.tensor.transpose(zTp[b][:, c, j * P:(j + 1) * P], z[b][:, j, c * P:(c + 1) * P], ident[:])
                ins.then_inc(zTp_ready, 1)

            def project(i, b, k):
                pe.wait_ge(zT_ready, i + 1)
                for j in range(SUPER):
                    wait_count(pe, hrow_ready, i * SUPER + j - 1)
                    for c in range(KD):
                        ins = nc.tensor.matmul(hp[j % 2][:, 0:HCOLS], zT[b][:, c, j * P:(j + 1) * P], W1x[:, c, :],
                                               start=(c == 0), stop=(c == KD - 1))
                    ins.then_inc(h_ready, 1)

            ring(pe, NSUPER, transpose_z, project)


def phase_edge_by_edge(v, layer):
    nc, sem, sb = v["nc"], v["sem"], v["sb"]
    E, NT = v["E"], v["NT"]
    H = v["HEADS"] if layer == 1 else 1
    F = v["HID"] if layer == 1 else v["D"]
    COLS = v["W1COLS"] if layer == 1 else v["W2COLS"]
    C = F // H
    table, own_table = (v["h1_table"], v["own1_table"]) if layer == 1 else (v["h2_table"], v["own2_table"])
    state, edge_list, bad_i = v["softmax_state"], v["edge_list"], v["bad_i"]

    with ExitStack() as ctx:
        S = lambda name: sem(f"s{layer}_" + name, ctx)
        T = lambda name, shape, dt=F32: sb(ctx, f"s{layer}_" + name, shape, dt)
        edges = T("edges", [1, E, 2], I32)
        parts = T("parts", [P, 2, H])
        first = T("first", [P, 2, H])
        src_row = T("src_row", [1, COLS])
        row = T("row", [1, COLS])
        st = T("st", [1, 2, H])
        score = T("score", [1, H])
        top = T("top", [1, H])
        df = T("df", [1, 2, H])
        ex = T("ex", [1, 2, H])
        inv = T("inv", [1, H])
        w = T("w", [1, 2, H])
        add = T("add", [1, F])
        edges_loaded, parts_loaded, first_ready, state_stored = (
            S(n) for n in ("edges_loaded", "parts_loaded", "first_ready", "state_stored"))
        rows_loaded, rows_stored, df_ready, ex_ready, row_ready, dve_chain, dve_edge, passed = (
            S(n) for n in ("rows_loaded", "rows_stored", "df_ready", "ex_ready", "row_ready", "dve_chain", "dve_edge", "passed"))
        block = ctx.enter_context(nc.Block())

        @block.sync
        def _(sp):
            with sp.If(sp.value_load(bad_i[0:1, 0:1], min_val=0, max_val=1) > 0):
                sp.dma_start(edges[:], edge_list[0:E, :].unsqueeze(0)).then_inc(edges_loaded, 16)
                with sp.Fori(0, NT) as t:
                    sp.dma_start(parts[:], own_table[bass.ds(t * P, P), F:F + 2 * H].rearrange("p (s h) -> p s h", s=2)).then_inc(parts_loaded, 16)
                    sp.wait_ge(first_ready, t + 1)
                    sp.dma_start(state[bass.ds(t * P, P), 0:2 * H].rearrange("p (s h) -> p s h", s=2), first[:]).then_inc(state_stored, 16)
                    sp.wait_ge(state_stored, 16 * t + 16)
                    sp.sem_inc(passed, 1)
                sp.wait_ge(edges_loaded, 16)
                with sp.Fori(0, E) as e:
                    s = sp.value_load(edges[0:1, bass.ds(e, 1), 0], min_val=0, max_val=v["N"] - 1)
                    d = sp.value_load(edges[0:1, bass.ds(e, 1), 1], min_val=0, max_val=v["N"] - 1)
                    sp.dma_start(src_row[:], table[bass.ds(s, 1), :]).then_inc(rows_loaded, 16)
                    sp.dma_start(row[:], own_table[bass.ds(d, 1), :]).then_inc(rows_loaded, 16)
                    sp.dma_start(st[:], state[bass.ds(d, 1), 0:2 * H].rearrange("p (s h) -> p s h", s=2)).then_inc(rows_loaded, 16)
                    sp.wait_ge(row_ready, e + 1)
                    sp.dma_start(own_table[bass.ds(d, 1), :], row[:]).then_inc(rows_stored, 16)
                    sp.dma_start(state[bass.ds(d, 1), 0:2 * H].rearrange("p (s h) -> p s h", s=2), st[:]).then_inc(rows_stored, 16)
                    sp.wait_ge(rows_stored, 32 * e + 32)
                    sp.sem_inc(passed, 1)

        @block.scalar
        def _(act):
            with act.If(act.value_load(bad_i[0:1, 0:1], min_val=0, max_val=1) > 0):
                with act.Fori(0, E) as e:
                    act.wait_ge(df_ready, e + 1)
                    nc.scalar.activation(ex[:], df[:], ACT.Exp).then_inc(ex_ready, 1)

        @block.vector
        def _(dve):
            with dve.If(dve.value_load(bad_i[0:1, 0:1], min_val=0, max_val=1) > 0):
                init = Chain(dve, dve_chain, 1)
                with dve.Fori(0, NT) as t:
                    init.round(t)
                    dve.wait_ge(parts_loaded, 16 * t + 16)
                    init.link(nc.vector.tensor_tensor(first[:, 0], parts[:, 0], parts[:, 1], ALU.add))
                    nc.vector.scalar_tensor_tensor(out=first[:, 0], in0=first[:, 0], scalar=SLOPE, in1=first[:, 0],
                                                   op0=ALU.mult, op1=ALU.max)
                    nc.vector.memset(first[:, 1], 1.0).then_inc(first_ready, 1)
                chain = Chain(dve, dve_edge, 9)
                with dve.Fori(0, E) as e:
                    chain.round(e)
                    heads = lambda t: t[:, 0:F].rearrange("p (h c) -> p h c", h=H)
                    wide = lambda t: t.unsqueeze(2).broadcast_to([1, H, C])
                    dve.wait_ge(rows_loaded, 48 * e + 48)
                    chain.link(nc.vector.tensor_tensor(score[:], src_row[:, F:F + H], row[:, F + H:F + 2 * H], ALU.add))
                    chain.link(nc.vector.scalar_tensor_tensor(out=score[:], in0=score[:], scalar=SLOPE, in1=score[:],
                                                              op0=ALU.mult, op1=ALU.max))
                    chain.link(nc.vector.tensor_tensor(top[:], st[:, 0], score[:], ALU.max))
                    nc.vector.tensor_tensor(df[:, 0], st[:, 0], top[:], ALU.subtract)
                    nc.vector.tensor_tensor(df[:, 1], score[:], top[:], ALU.subtract).then_inc(df_ready, 1)
                    dve.wait_ge(ex_ready, e + 1)
                    chain.link(nc.vector.tensor_tensor(w[:, 0], st[:, 1], ex[:, 0], ALU.mult))
                    chain.link(nc.vector.tensor_tensor(st[:, 1], w[:, 0], ex[:, 1], ALU.add))
                    chain.link(nc.vector.tensor_scalar(st[:, 0], top[:], 1.0, None, ALU.mult))
                    chain.link(nc.vector.reciprocal(inv[:], st[:, 1]))
                    nc.vector.tensor_tensor(w[:, 0], w[:, 0], inv[:], ALU.mult)
                    chain.link(nc.vector.tensor_tensor(w[:, 1], ex[:, 1], inv[:], ALU.mult))
                    nc.vector.tensor_tensor(heads(add), heads(src_row), wide(w[:, 1]), ALU.mult)
                    chain.link(nc.vector.tensor_tensor(heads(row), heads(row), wide(w[:, 0]), ALU.mult))
                    nc.vector.tensor_tensor(row[:, 0:F], row[:, 0:F], add[:], ALU.add).then_inc(row_ready, 1)
                    chain.close()


def phase_aggregate(v, layer):
    nc, sem, sb, ps = v["nc"], v["sem"], v["sb"], v["ps"]
    N, D, NT, NG, NSUPER, NE, KD, FH = (v[n] for n in ("N", "D", "NT", "NG", "NSUPER", "NE", "KD", "FH"))
    H = v["HEADS"] if layer == 1 else 1
    F = v["HID"] if layer == 1 else D
    COLS = v["W1COLS"] if layer == 1 else v["W2COLS"]
    C = F // H
    W2COLS = v["W2COLS"]
    table, own_table = (v["h1_table"], v["own1_table"]) if layer == 1 else (v["h2_table"], v["own2_table"])
    ident, iota_row, windows, place = v["ident"], v["iota_row"], v["windows"], v["place"]
    KF = F // P
    R = GROUP * H
    ROWS = GROUP * TILE
    UNITS = GROUP
    UNIT = 1
    OC = W2COLS if layer == 1 else D

    with ExitStack() as ctx:
        S = lambda name: sem(f"g{layer}_" + name, ctx)
        T = lambda name, shape, dt=F32: sb(ctx, f"g{layer}_" + name, shape, dt)
        gat = [T(f"gat{b}", [P, GROUP, COLS]) for b in range(2)]
        own = [T(f"own{b}", [P, GROUP, COLS]) for b in range(2)]
        sel = [T(f"sel{b}", [P, GROUP, TILE]) for b in range(2)]
        selT = T("selT", [P, GROUP, P])
        ad = T("ad", [P, GROUP, 2, H])
        sc = T("sc", [P, 2, GROUP, H])
        rep = T("rep", [P, GROUP, H])
        rows_t = T("rows_t", [R, 2, P])
        news = T("news", [R, 2 * P])
        pen = T("pen", [R, P + 1])
        run = T("run", [R, P])
        back_t = T("back_t", [R, P])
        mx = T("mx", [P, GROUP, H])
        df = T("df", [P, 2, GROUP, H])
        msg = T("msg", [P, GROUP, COLS])
        wsum = T("wsum", [P, UNITS, 2, UNIT, H])
        res = [T(f"res{b}", [P, GROUP, OC]) for b in range(2)]
        sources = [T(f"sources{b}", [P, GROUP], I32) for b in range(2)]
        bad_far = T("bad_far", [P, 1])
        if layer == 1:
            agg = T("agg", [P, GROUP, F])
            aggT = T("aggT", [P, GROUP, KF, P])
        else:
            xin = [T(f"xin{b}", [P, GROUP, D]) for b in range(2)]
            part = T("part", [P, GROUP, D])
        selp = ps(ctx, f"g{layer}_selp", [P, GROUP, P])
        adp = ps(ctx, f"g{layer}_adp", [P, 512])
        trp = ps(ctx, f"g{layer}_trp", [P, 512])
        sump = [ps(ctx, f"g{layer}_sump{q}", [P, 512]) for q in range(2)]
        if layer == 1:
            aggp = ps(ctx, "g1_aggp", [P, 512])
            outp = ps(ctx, "g1_outp", [P, 512])

        gathered = [S(f"gathered{b}") for b in range(2)]
        own_loaded = [S(f"own_loaded{b}") for b in range(2)]
        res_stored = [S(f"res_stored{b}") for b in range(2)]
        place_ready, sel_ready, selp_ready, selT_ready, adp_ready = (
            S(n) for n in ("place_ready", "sel_ready", "selp_ready", "selT_ready", "adp_ready"))
        sc_ready, rows_ready, runs_ready, max_ready, df_ready, exp_ready, msg_ready = (
            S(n) for n in ("sc_ready", "rows_ready", "runs_ready", "max_ready", "df_ready", "exp_ready", "msg_ready"))
        sums_ready, agg_ready, aggp_ready, aggT_ready, outp_ready, out_taken, dve_chain = (
            S(n) for n in ("sums_ready", "agg_ready", "aggp_ready", "aggT_ready", "outp_ready", "out_taken", "dve_chain"))
        pool_chain, bad_ready = S("pool_chain"), S("bad_ready")
        runs_passed, sources_passed = S("runs_passed"), S("sources_passed")
        LINKS = 9 + UNITS * (4 if layer == 1 else 3)
        OWN_DMAS = 1 if layer == 1 else 2
        block = ctx.enter_context(nc.Block())

        def tile_rows(table, g, rows=ROWS):
            return table[bass.ds(g * ROWS, rows), :].rearrange("(j p) d -> p j d", p=P)

        @block.sync
        def _(sp):
            def load(g, b, k):
                wait_count(sp, agg_ready, (g - 1) * UNITS)
                sp.dma_start(own[b][:], tile_rows(own_table, g)).then_inc(own_loaded[b], 16)
                if layer == 2:
                    if isinstance(g, int) and g == NG - 1:
                        full = (N - g * ROWS) // P
                        rest = N - g * ROWS - full * P
                        sp.dma_start(xin[b][:, 0:full], tile_rows(v["x"], g, full * P)).then_inc(own_loaded[b], 16)
                        sp.dma_start(xin[b][0:rest, full], v["x"][N - rest:N, :]).then_inc(own_loaded[b], 16)
                    else:
                        sp.dma_start(xin[b][:], tile_rows(v["x"], g)).then_inc(own_loaded[b], 16)

            def store(g, b, k):
                if layer == 1:
                    sp.wait_ge(out_taken, (g + 1) * GROUP)
                    sp.dma_start(tile_rows(v["h2_table"], g), res[b][:]).then_inc(res_stored[b], 16)
                    sp.dma_start(tile_rows(v["own2_table"], g), res[b][:]).then_inc(res_stored[b], 16)
                else:
                    sp.wait_ge(agg_ready, (g + 1) * UNITS)
                    sp.dma_start(tile_rows(v["x2_table"], g), res[b][:]).then_inc(res_stored[b], 16)

            ring(sp, NG, load, store)
            for b in range(2):
                sp.wait_ge(res_stored[b], (32 if layer == 1 else 16) * (NG // 2))

        @block.gpsimd
        def _(pool):
            nc.gpsimd.memset(news[:], 1.0).then_inc(place_ready, 1)

            def gather(g, b, k):
                wait_count(pool, msg_ready, g - 1)
                nc.gpsimd.tensor_copy(sources[b][:], windows[:, bass.ds(g * GROUP, GROUP), 0]).then_inc(pool_chain, 1)
                hold(pool, pool_chain, g + 1, sources_passed)
                for j in range(GROUP):
                    pool.indirect_dma_start(gat[b][:, j, :], None, table,
                                            bass.IndirectOffsetOnAxis(ap=sources[b][:, j:j + 1], axis=0)).then_inc(gathered[b], 16)

            ring(pool, NG, gather, lambda g, b, k: None)

        @block.scalar
        def _(act):
            def evac_sel(g, b, k):
                act.wait_ge(selp_ready, g + 1)
                wait_count(act, adp_ready, g)
                for q in range(2):
                    ins = nc.scalar.activation(selT[:, q * 4:q * 4 + 4, :], selp[:, q * 4:q * 4 + 4, :], ACT.Copy)
                ins.then_inc(selT_ready, 1)

            def exponent(g, b, k):
                act.wait_ge(df_ready, g + 1)
                wait_count(act, sums_ready, g * UNITS)
                nc.scalar.activation(msg[:, :, F:F + 2 * H].rearrange("p j (s h) -> p s j h", s=2), df[:], ACT.Exp).then_inc(exp_ready, 1)
                if layer == 1:
                    for u in range(UNITS):
                        act.wait_ge(aggp_ready, g * UNITS + u + 1)
                        for c in range(KF):
                            ins = nc.scalar.activation(aggT[:, u, c, :], aggp[:, c * P:(c + 1) * P], ACT.Relu,
                                                       bias=v["b1_col"][:, c:c + 1])
                        ins.then_inc(aggT_ready, 1)
                        act.wait_ge(outp_ready, g * GROUP + u + 1)
                        if u == 0 and not (isinstance(g, int) and g < 2):
                            act.wait_ge(res_stored[b], 32 * k)
                        nc.scalar.activation(res[b][:, u, :], outp[:, 0:OC], ACT.Copy).then_inc(out_taken, 1)

            ring(act, NG, evac_sel, exponent)

        @block.vector
        def _(dve):
            nc.vector.tensor_scalar(bad_far[:], v["bad"][:], float(NOWHERE), None, ALU.mult).then_inc(bad_ready, 1)
            dve.wait_ge(bad_ready, 1)
            nc.vector.scalar_tensor_tensor(out=place[:], in0=windows[:, :, 1], scalar=bad_far[:, 0:1], in1=v["tile_base"][:],
                                           op0=ALU.add, op1=ALU.subtract).then_inc(place_ready, 1)
            dve.wait_ge(place_ready, 2)

            def select(g, b, k):
                wait_count(dve, sums_ready, (g - 1) * UNITS)
                here = place[:, bass.ds(g * GROUP, GROUP)].unsqueeze(2).broadcast_to([P, GROUP, TILE])
                nc.vector.tensor_tensor(sel[b][:], here, iota_row[:].unsqueeze(1).broadcast_to([P, GROUP, TILE]),
                                        ALU.is_equal).then_inc(sel_ready, 1)

            chain = Chain(dve, dve_chain, LINKS)

            def attend(g, b, k):
                chain.round(g)
                dve.wait_ge(adp_ready, g + 1)
                chain.link(nc.vector.tensor_copy(ad[:], adp[:, 0:GROUP * 2 * H].rearrange("p (j s h) -> p j s h", j=GROUP, s=2)))
                nc.vector.tensor_scalar(rep[:], place[:, bass.ds(g * GROUP, GROUP)].unsqueeze(2).broadcast_to([P, GROUP, H]),
                                        1.0, None, ALU.mult)
                dve.wait_ge(gathered[b], 16 * GROUP * k + 16 * GROUP)
                nc.vector.tensor_tensor(sc[:, 0], gat[b][:, :, F:F + H], ad[:, :, 1, :], ALU.add)
                chain.link(nc.vector.tensor_tensor(sc[:, 1], ad[:, :, 0, :], ad[:, :, 1, :], ALU.add))
                nc.vector.scalar_tensor_tensor(out=sc[:], in0=sc[:], scalar=SLOPE, in1=sc[:], op0=ALU.mult, op1=ALU.max).then_inc(sc_ready, 1)
                dve.wait_ge(rows_ready, g + 1)
                chain.link(nc.vector.tensor_copy(rows_t[:], trp[0:R, 0:2 * P].rearrange("r (s e) -> r s e", s=2)))
                chain.link(nc.vector.tensor_tensor(news[:, 1:P], rows_t[:, 1, 1:P], rows_t[:, 1, 0:P - 1], ALU.not_equal))
                chain.link(nc.vector.tensor_scalar(pen[:], news[:, 0:P + 1], -BIG, None, ALU.mult))
                chain.link(nc.vector.tensor_tensor_scan(run[:], pen[:, 0:P], rows_t[:, 0, :], -BIG, ALU.add, ALU.max))
                nc.vector.tensor_tensor_scan(back_t[:, ::-1], pen[:, 1:P + 1][:, ::-1], run[:, ::-1], -BIG, ALU.add, ALU.max).then_inc(runs_ready, 1)
                dve.wait_ge(max_ready, g + 1)
                chain.link(nc.vector.tensor_tensor(mx[:], trp[:, 256:256 + R].rearrange("p (j h) -> p j h", j=GROUP), sc[:, 1], ALU.max))
                chain.link(nc.vector.tensor_tensor(df[:], sc[:], mx[:].unsqueeze(1).broadcast_to([P, 2, GROUP, H]), ALU.subtract))
                nc.vector.tensor_scalar(df[:], df[:], 0.0, None, ALU.min).then_inc(df_ready, 1)
                dve.wait_ge(exp_ready, g + 1)
                chain.link(nc.vector.scalar_tensor_tensor(
                    out=msg[:, :, F + H:F + 2 * H], in0=msg[:, :, F + H:F + 2 * H], scalar=-1.0,
                    in1=trp[:, 256 + R:256 + 2 * R].rearrange("p (j h) -> p j h", j=GROUP), op0=ALU.add, op1=ALU.mult))
                nc.vector.tensor_tensor(
                    msg[:, :, 0:F].rearrange("p j (h c) -> p j h c", h=H), gat[b][:, :, 0:F].rearrange("p j (h c) -> p j h c", h=H),
                    msg[:, :, F:F + H].unsqueeze(3).broadcast_to([P, GROUP, H, C]), ALU.mult).then_inc(msg_ready, 1)
                if layer == 2:
                    nc.vector.tensor_tensor(xin[b][:], xin[b][:], v["b2_row"][:].unsqueeze(1).broadcast_to([P, GROUP, D]), ALU.add)
                    if not (isinstance(g, int) and g < 2):
                        dve.wait_ge(res_stored[b], 16 * k)
                for u in range(UNITS):
                    total = sump[u % 2][:, 0:UNIT * COLS].rearrange("p (j c) -> p j c", j=UNIT)
                    mine = own[b][:, u * UNIT:(u + 1) * UNIT, :]
                    w = wsum[:, u]
                    dve.wait_ge(sums_ready, g * UNITS + u + 1)
                    chain.link(nc.vector.tensor_scalar(w[:, 0], total[:, :, F + H:F + 2 * H], 1.0, None, ALU.add))
                    chain.link(nc.vector.tensor_tensor(w[:, 1], w[:, 0], total[:, :, F:F + H], ALU.add))
                    if layer == 1:
                        nc.vector.reciprocal(w[:, 1], w[:, 1])
                        a = agg[:, u * UNIT:(u + 1) * UNIT, :]
                        heads = lambda t: t.rearrange("p j (h c) -> p j h c", h=H)
                        chain.link(nc.vector.tensor_tensor(heads(a), heads(mine[:, :, 0:F]),
                                                           w[:, 0].unsqueeze(3).broadcast_to([P, UNIT, H, C]), ALU.mult))
                        chain.link(nc.vector.tensor_tensor(a, a, total[:, :, 0:F], ALU.add))
                        nc.vector.tensor_tensor(heads(a), heads(a), w[:, 1].unsqueeze(3).broadcast_to([P, UNIT, H, C]),
                                                ALU.mult).then_inc(agg_ready, 1)
                    else:
                        nc.vector.reciprocal(w[:, 1], w[:, 1])
                        chain.link(nc.vector.scalar_tensor_tensor(out=part[:, u, :], in0=mine[:, 0, 0:F], scalar=w[:, 0, 0, 0:1],
                                                                  in1=total[:, 0, 0:F], op0=ALU.mult, op1=ALU.add))
                        nc.vector.scalar_tensor_tensor(out=res[b][:, u, :], in0=part[:, u, :], scalar=w[:, 1, 0, 0:1],
                                                       in1=xin[b][:, u, :], op0=ALU.mult, op1=ALU.add).then_inc(agg_ready, 1)
                chain.close()

            ring(dve, NG, select, attend)

        @block.tensor
        def _(pe):
            def turn_sel(g, b, k):
                pe.wait_ge(sel_ready, g + 1)
                wait_count(pe, selT_ready, g)
                for j in range(GROUP):
                    ins = nc.tensor.transpose(selp[:, j, :], sel[b][:, j, :], ident[:])
                ins.then_inc(selp_ready, 1)
                pe.wait_ge(selT_ready, g + 1)
                more = 16 if layer == 2 and isinstance(g, int) and g == NG - 1 else 0
                pe.wait_ge(own_loaded[b], OWN_DMAS * 16 * k + OWN_DMAS * 16 + more)
                wait_count(pe, sc_ready, g)
                for j in range(GROUP):
                    ins = nc.tensor.matmul(adp[:, j * 2 * H:(j + 1) * 2 * H], selT[:, j, :], own[b][:, j, F:F + 2 * H],
                                           start=True, stop=True)
                ins.then_inc(adp_ready, 1)

            def aggregate(g, b, k):
                pe.wait_ge(sc_ready, g + 1)
                nc.tensor.transpose(trp[0:R, 0:P], sc[:, 0].rearrange("p j h -> p (j h)"), ident[:])
                nc.tensor.transpose(trp[0:R, P:2 * P], rep[:].rearrange("p j h -> p (j h)"), ident[:]).then_inc(rows_ready, 1)
                hold(pe, runs_ready, g + 1, runs_passed)
                nc.tensor.transpose(trp[:, 256:256 + R], back_t[:], ident[0:R, 0:R])
                nc.tensor.transpose(trp[:, 256 + R:256 + 2 * R], news[:, 0:P], ident[0:R, 0:R]).then_inc(max_ready, 1)
                pe.wait_ge(msg_ready, g + 1)
                for u in range(UNITS):
                    wait_count(pe, agg_ready, g * UNITS + u - 1)
                    for j in range(UNIT):
                        t = u * UNIT + j
                        ins = nc.tensor.matmul(sump[u % 2][:, j * COLS:(j + 1) * COLS], sel[b][:, t, :], msg[:, t, :],
                                               start=True, stop=True)
                    ins.then_inc(sums_ready, 1)
                if layer == 1:
                    for u in range(UNITS):
                        pe.wait_ge(agg_ready, g * UNITS + u + 1)
                        wait_count(pe, aggT_ready, g * UNITS + u)
                        for c in range(KF):
                            ins = nc.tensor.transpose(aggp[:, c * P:(c + 1) * P], agg[:, u, c * P:(c + 1) * P], ident[:])
                        ins.then_inc(aggp_ready, 1)
                        pe.wait_ge(aggT_ready, g * UNITS + u + 1)
                        wait_count(pe, out_taken, g * UNITS + u)
                        for c in range(KF):
                            ins = nc.tensor.matmul(outp[:, 0:OC], aggT[:, u, c, :], v["W2x"][:, c, :],
                                                   start=(c == 0), stop=(c == KF - 1))
                        ins.then_inc(outp_ready, 1)

            ring(pe, NG, turn_sel, aggregate)


def phase_experts(v):
    nc, sem, sb, ps = v["nc"], v["sem"], v["sb"], v["ps"]
    D, NE, FH, KD, KH, NSUPER, TAIL = (v[n] for n in ("D", "NE", "FH", "KD", "KH", "NSUPER", "TAIL"))
    ident, wh, wl, scale, shift = v["ident"], v["wh"], v["wl"], v["scale"], v["shift"]
    last = NSUPER - 1
    with ExitStack() as ctx:
        S = lambda name: sem("e_" + name, ctx)
        T = lambda name, shape, dt=F32: sb(ctx, "e_" + name, shape, dt)
        xin = [T(f"xin{b}", [P, SUPER, D]) for b in range(2)]
        z = T("z", [P, SUPER, D])
        z_hi = [T(f"z_hi{b}", [P, KD, SUPER * P], F32R) for b in range(2)]
        z_lo = [T(f"z_lo{b}", [P, KD, SUPER * P], F32R) for b in range(2)]
        stats = T("stats", [P, SUPER, 6])
        mv = T("mv", [P, SUPER, 2])
        vare = T("vare", [P, SUPER])
        rstd = T("rstd", [P, SUPER])
        logit = T("logit", [P, SUPER, NE])
        top1 = T("top1", [P, SUPER])
        tot = T("tot", [P, SUPER])
        share = [T(f"share{b}", [P, SUPER, NE]) for b in range(2)]
        shareT = T("shareT", [NE, SUPER * P])
        acc = [T(f"acc{b}", [P, SUPER, D]) for b in range(2)]
        h = [T(f"h{l}", [P, KH, SUPER * P]) for l in (1, 2)]
        h_hi = [T(f"h{l}_hi", [P, KH, SUPER * P], F32R) for l in (1, 2)]
        h_lo = [T(f"h{l}_lo", [P, KH, SUPER * P], F32R) for l in (1, 2)]
        up = [ps(ctx, f"e_u{l}", [P, KH, 512]) for l in (1, 2)]
        yp = ps(ctx, "e_y", [P, SUPER, D])
        misc = ps(ctx, "e_misc", [P, 2, 512])
        x_loaded = [S(f"x_loaded{b}") for b in range(2)]
        out_stored = [S(f"out_stored{b}") for b in range(2)]
        (var_ready, rstd_ready, z_ready, zT_ready, z_hi_ready, z_lo_ready, logit_ready, exp_in, exp_ready, share_ready,
         shareT_p, shareT_ready, bias_ready, acc_ready, dve_chain) = (
            S(n) for n in ("var_ready", "rstd_ready", "z_ready", "zT_ready", "z_hi_ready", "z_lo_ready", "logit_ready", "exp_in",
                           "exp_ready", "share_ready", "shareT_p", "shareT_ready", "bias_ready", "acc_ready", "dve_chain"))
        u_ready = [S(f"u{l}_ready") for l in (1, 2)]
        hi_ready = [S(f"h{l}_hi_ready") for l in (1, 2)]
        lo_ready = [S(f"h{l}_lo_ready") for l in (1, 2)]
        y_ready, y_taken, tot_ready = S("y_ready"), S("y_taken"), S("tot_ready")
        moments_passed = S("moments_passed")
        width = lambda i: 1 if isinstance(i, int) and i == last else SUPER
        HALVES = 2
        halves = lambda i: 1 if isinstance(i, int) and i == last else HALVES

        def half_count(i, e, q):
            if isinstance(i, int) and i == last:
                return last * NE * HALVES + e + 1
            return (i * NE + e) * HALVES + q + 1


        def experts(eng, ahead, step):
            def body(i, b, k):
                for e in range(NE):
                    step(i, b, k, e)
                    if not (isinstance(i, int) and i == last):
                        ahead(i + 1, 1 - b, k + b, e)
            for e in range(NE):
                ahead(0, 0, 0, e)
            step(0, 0, 0, -1)
            body(0, 0, 0)
            body(1, 1, 0)
            turns = (NSUPER - 1) // 2
            with eng.Fori(1, turns) as k:
                body(2 * k, 0, k)
                body(2 * k + 1, 1, k)
            for i in range(2 * turns, NSUPER):
                body(i, i % 2, i // 2)

        block = ctx.enter_context(nc.Block())

        @block.sync
        def _(sp):
            def load(i, b, k):
                wait_count(sp, acc_ready, i - 1)
                if isinstance(i, int) and i == last:
                    sp.dma_start(xin[b][:, 0:1, :], row_view(v["x2_table"], i, P, 1)).then_inc(x_loaded[b], 16)
                else:
                    sp.dma_start(xin[b][:], row_view(v["x2_table"], i)).then_inc(x_loaded[b], 16)

            def store(i, b, k):
                sp.wait_ge(y_taken, half_count(i, NE - 1, halves(i) - 1))
                if isinstance(i, int) and i == last:
                    sp.dma_start(row_view(v["out"], i, TAIL, 1), acc[b][0:TAIL, 0:1, :]).then_inc(out_stored[b], 16)
                else:
                    sp.dma_start(row_view(v["out"], i), acc[b][:]).then_inc(out_stored[b], 16)

            ring(sp, NSUPER, load, stores_later(store, NSUPER))
            for b in range(2):
                sp.wait_ge(out_stored[b], 16 * (NSUPER // 2))


        @block.gpsimd
        def _(pool):
            def power(i, b, k):
                pool.wait_ge(var_ready, i + 1)
                nc.gpsimd.tensor_tensor(rstd[:], vare[:], v["eps_half"][:, 0:SUPER], ALU.pow).then_inc(rstd_ready, 1)
            ring(pool, NSUPER, power, lambda i, b, k: None)

        @block.scalar
        def _(act):
            def ahead(i, b, k, n):
                w = width(i) * P
                if n == 3:
                    act.wait_ge(zT_ready, i + 1)
                    for c in range(KD):
                        ins = nc.scalar.activation(z_hi[b][:, c, 0:w], misc[:, c, 0:w], ACT.Copy)
                    ins.then_inc(z_hi_ready, 1)
                if n == 5:
                    act.wait_ge(exp_in, i + 1)
                    nc.scalar.activation(share[b][:], logit[:], ACT.Exp).then_inc(exp_ready, 1)

            def relu(l, i, e, last_w):
                for c in range(KH):
                    act.wait_ge(u_ready[l], (i * NE + e) * KH + c + 1)
                    for o in (h[l], h_hi[l]):
                        ins = nc.scalar.activation(o[:, c, 0:last_w], up[l][:, c, 0:last_w], ACT.Relu,
                                                   bias=shift[l][:, e, c:c + 1], scale=scale[l][:, e, c:c + 1])
                    ins.then_inc(hi_ready[l], 1)

            def step(i, b, k, e):
                if e >= 0:
                    relu(1, i, e, width(i) * P)
                if e + 1 < NE:
                    relu(0, i, e + 1, width(i) * P)
                elif not (isinstance(i, int) and i == last):
                    relu(0, i + 1, 0, width(i + 1) * P)

            experts(act, ahead, step)

        @block.vector
        def _(dve):
            chain = Chain(dve, dve_chain, 5)

            def ahead(i, b, k, n):
                w = width(i)
                if n == 0:
                    chain.round(i)
                    dve.wait_ge(x_loaded[b], 16 * k + 16)
                    for j in range(w):
                        ins = nc.vector.bn_stats(stats[:, j, :], xin[b][:, j, :])
                    chain.link(ins)
                    dve.sem_inc(moments_passed, 1)
                    for j in range(w):
                        ins = nc.vector.bn_aggr(mv[:, j, :], stats[:, j, :])
                    chain.link(ins)
                    nc.vector.tensor_scalar(vare[:], mv[:, :, 1], LN_EPS, None, ALU.add).then_inc(var_ready, 1)
                if n == 1:
                    dve.wait_ge(rstd_ready, i + 1)
                    for j in range(w):
                        ins = nc.vector.tensor_scalar(z[:, j, :], xin[b][:, j, :], mv[:, j, 0:1], rstd[:, j:j + 1],
                                                      ALU.subtract, ALU.mult)
                    ins.then_inc(z_ready, 1)
                if n == 3:
                    dve.wait_ge(z_hi_ready, i + 1)
                    for c in range(KD):
                        ins = nc.vector.tensor_tensor(z_lo[b][:, c, 0:w * P], misc[:, c, 0:w * P],
                                                      z_hi[b][:, c, 0:w * P].bitcast(F32), ALU.subtract)
                    ins.then_inc(z_lo_ready, 1)
                if n == 4:
                    dve.wait_ge(logit_ready, i + 1)
                    lg = misc[:, 0, 0:w * NE].rearrange("p (j e) -> p j e", j=w)
                    chain.link(nc.vector.tensor_tensor(logit[:, 0:w], lg, v["br_row"][:].unsqueeze(1).broadcast_to([P, w, NE]), ALU.add))
                    chain.link(nc.vector.tensor_reduce(top1[:, 0:w], logit[:, 0:w], axis=AX.X, op=ALU.max))
                    nc.vector.tensor_tensor(logit[:, 0:w], logit[:, 0:w], top1[:, 0:w].unsqueeze(2).broadcast_to([P, w, NE]),
                                            ALU.subtract).then_inc(exp_in, 1)
                if n == 5:
                    dve.wait_ge(exp_ready, i + 1)
                    chain.link(nc.vector.tensor_reduce(tot[:, 0:w], share[b][:, 0:w], axis=AX.X, op=ALU.add))
                    nc.vector.reciprocal(tot[:, 0:w], tot[:, 0:w]).then_inc(tot_ready, 1)
                    dve.wait_ge(tot_ready, i + 1)
                    nc.vector.tensor_tensor(share[b][:, 0:w], share[b][:, 0:w], tot[:, 0:w].unsqueeze(2).broadcast_to([P, w, NE]),
                                            ALU.mult).then_inc(share_ready, 1)
                    chain.close()
                if n == 6:
                    dve.wait_ge(shareT_p, i + 1)
                    nc.vector.tensor_copy(shareT[:, 0:w * P], misc[0:NE, 1, 0:w * P]).then_inc(shareT_ready, 1)
                if n == 7:
                    dve.wait_ge(bias_ready, i + 1)
                    if not (isinstance(i, int) and i < 2):
                        dve.wait_ge(out_stored[b], 16 * k)
                    both = misc[:].rearrange("p q (j d) -> p (q j) d", d=D)
                    nc.vector.tensor_tensor(acc[b][:, 0:w], both[:, 0:w], xin[b][:, 0:w], ALU.add).then_inc(acc_ready, 1)

            def low(l, i, e, w):
                for c in range(KH):
                    dve.wait_ge(hi_ready[l], (i * NE + e) * KH + c + 1)
                    nc.vector.tensor_tensor(h_lo[l][:, c, 0:w], h[l][:, c, 0:w], h_hi[l][:, c, 0:w].bitcast(F32),
                                            ALU.subtract).then_inc(lo_ready[l], 1)

            def step(i, b, k, e):
                w = width(i)
                if e >= 0:
                    low(1, i, e, w * P)
                if e + 1 < NE:
                    low(0, i, e + 1, w * P)
                elif not (isinstance(i, int) and i == last):
                    low(0, i + 1, 0, width(i + 1) * P)
                if e < 0:
                    return
                dve.wait_ge(acc_ready, i + 1)
                for q in range(halves(i)):
                    dve.wait_ge(y_ready, half_count(i, e, q))
                    if e:
                        dve.wait_ge(y_taken, half_count(i, e - 1, q))
                    for j in range(q * 2, min(q * 2 + 2, w)):
                        ins = nc.vector.scalar_tensor_tensor(out=acc[b][:, j, :], in0=yp[:, j, :], scalar=share[b][:, j, e:e + 1],
                                                             in1=acc[b][:, j, :], op0=ALU.mult, op1=ALU.add)
                    ins.then_inc(y_taken, 1)

            experts(dve, ahead, step)

        @block.tensor
        def _(pe):
            def ahead(i, b, k, n):
                w = width(i)
                if n == 3:
                    pe.wait_ge(z_ready, i + 1)
                    wait_count(pe, acc_ready, i)
                    for j in range(w):
                        for c in range(KD):
                            ins = nc.tensor.transpose(misc[:, c, j * P:(j + 1) * P], z[:, j, c * P:(c + 1) * P], ident[:])
                    ins.then_inc(zT_ready, 1)
                if n == 4:
                    pe.wait_ge(z_lo_ready, i + 1)
                    for j in range(w):
                        terms = [(zz, ww, c) for c in range(KD) for zz, ww in
                                 ((z_hi[b], v["Wr_hi"]), (z_hi[b], v["Wr_lo"]), (z_lo[b], v["Wr_hi"]))]
                        for n_, (zz, ww, c) in enumerate(terms):
                            ins = nc.tensor.matmul(misc[:, 0, j * NE:(j + 1) * NE], zz[:, c, j * P:(j + 1) * P], ww[:, c, :],
                                                   start=(n_ == 0), stop=(n_ == len(terms) - 1))
                    ins.then_inc(logit_ready, 1)
                if n == 6:
                    pe.wait_ge(share_ready, i + 1)
                    for j in range(w):
                        ins = nc.tensor.transpose(misc[0:NE, 1, j * P:(j + 1) * P], share[b][:, j, :], ident[:])
                    ins.then_inc(shareT_p, 1)
                if n == 7:
                    pe.wait_ge(shareT_ready, i + 1)
                    both = misc[:].rearrange("p q (j d) -> p (q j) d", d=D)
                    for j in range(w):
                        ins = nc.tensor.matmul(both[:, j, :], shareT[:, j * P:(j + 1) * P], v["bo_sb"][:], start=True, stop=True)
                    ins.then_inc(bias_ready, 1)

            def dense(l, i, e, rhs_hi, rhs_lo, name, w, chunks):
                for c in range(chunks):
                    terms = [(ww, rr, k) for k in range(KD) for ww, rr in
                             ((wh[name], rhs_hi), (wl[name], rhs_hi), (wh[name], rhs_lo))]
                    for n, (ww, rr, k) in enumerate(terms):
                        ins = nc.tensor.matmul(up[l][:, c, 0:w], ww[:, e, k, c * P:(c + 1) * P], rr[:, k, 0:w],
                                               start=(n == 0), stop=(n == len(terms) - 1))
                    ins.then_inc(u_ready[l], 1)

            def step(i, b, k, e):
                w = width(i)
                if e >= 0:
                    pe.wait_ge(lo_ready[0], (i * NE + e + 1) * KH)
                    dense(1, i, e, h_hi[0], h_lo[0], "fW2", w * P, KH)
                if e + 1 < NE:
                    if e < 0:
                        pe.wait_ge(z_lo_ready, i + 1)
                    dense(0, i, e + 1, z_hi[b], z_lo[b], "fW1", w * P, KH)
                elif not (isinstance(i, int) and i == last):
                    dense(0, i + 1, 0, z_hi[1 - b], z_lo[1 - b], "fW1", width(i + 1) * P, KH)
                if e < 0:
                    return
                pe.wait_ge(lo_ready[1], (i * NE + e + 1) * KH)
                for q in range(halves(i)):
                    if e:
                        pe.wait_ge(y_taken, half_count(i, e - 1, q))
                    elif not (isinstance(i, int) and i == 0):
                        pe.wait_ge(y_taken, (i * NE - 1) * HALVES + q + 1)
                    for j in range(q * 2, min(q * 2 + 2, w)):
                        terms = [(hh, ww, k) for k in range(KH) for hh, ww in
                                 ((h_hi[1], wh["Wo"]), (h_hi[1], wl["Wo"]), (h_lo[1], wh["Wo"]))]
                        for n, (hh, ww, c) in enumerate(terms):
                            ins = nc.tensor.matmul(yp[:, j, :], hh[:, c, j * P:(j + 1) * P], ww[:, e, c, :],
                                                   start=(n == 0), stop=(n == len(terms) - 1))
                    ins.then_inc(y_ready, 1)

            experts(pe, ahead, step)


_INS = ["x", "src", "dst", "L0_gnn_W1", "L0_gnn_att_src1", "L0_gnn_att_dst1", "L0_gnn_b1", "L0_gnn_W2", "L0_gnn_att_src2",
        "L0_gnn_att_dst2", "L0_gnn_b2", "L0_ffn_Wr", "L0_ffn_br", "L0_ffn_W1", "L0_ffn_b1", "L0_ffn_g1", "L0_ffn_be1",
        "L0_ffn_m1", "L0_ffn_v1", "L0_ffn_W2", "L0_ffn_b2", "L0_ffn_g2", "L0_ffn_be2", "L0_ffn_m2", "L0_ffn_v2",
        "L0_ffn_Wo", "L0_ffn_bo"]


def kernel(**inputs):
    import numpy as _np
    import concourse.bacc as _bacc
    from concourse import mybir as _mybir
    from concourse.bass_utils import run_bass_kernel_spmd as _run

    nc = _bacc.Bacc("TRN2", target_bir_lowering=False, num_devices=1)
    arrays, args = {}, []
    for name in _INS:
        a = _np.ascontiguousarray(inputs[name])
        arrays[f"in_{name}"] = a
        args.append(nc.dram_tensor(f"in_{name}", a.shape, _mybir.dt.from_np(a.dtype), kind="ExternalInput").ap())
    shape = inputs["x"].shape
    args.append(nc.dram_tensor("out_0", shape, _mybir.dt.float32, kind="ExternalOutput").ap())
    gnn_ffn(nc, *args)
    r = _run(nc, [arrays], core_ids=[0])
    return r.results[0]["out_0"]
```

```python
import numpy as np
import concourse.bass as bass
from concourse import mybir
from contextlib import ExitStack

F32 = mybir.dt.float32
F32R = mybir.dt.float32r
BF16 = mybir.dt.bfloat16
I32 = mybir.dt.int32
ALU = mybir.AluOpType
ACT = mybir.ActivationFunctionType
AX = mybir.AxisListType

P = 128
LN_EPS = 1e-5
BN_EPS = 1e-3
SLOPE = 0.2
BIG = 3e38
NOWHERE = 1 << 20
TILE = 128
GROUP = 8
SUPER = 4


def ring(eng, count, front, back, slots=2):
    front(0, 0, 0)
    for i in range(slots):
        front(i + 1, (i + 1) % slots, (i + 1) // slots)
        back(i, i, 0)
    turns = (count - 1) // slots
    with eng.Fori(1, turns) as k:
        for q in range(slots):
            front(slots * k + q + 1, (q + 1) % slots, k + (q + 1) // slots)
            back(slots * k + q, q, k)
    for i in range(slots * turns, count):
        if i + 1 < count:
            front(i + 1, (i + 1) % slots, (i + 1) // slots)
        back(i, i % slots, i // slots)


def wait_count(eng, sem, count):
    if isinstance(count, int) and count <= 0:
        return
    eng.wait_ge(sem, count)


def hold(eng, sem, count, passed):
    eng.wait_ge(sem, count)
    eng.sem_inc(passed, 1)


def stores_later(store, count, slots=2):
    def back(i, b, k):
        if isinstance(i, int) and i == 0:
            return
        store(i - 1, (b - 1) % slots, k - 1 if b == 0 else k)
        if isinstance(i, int) and i == count - 1:
            store(i, b, k)
    return back


class Chain:

    def __init__(self, eng, sem, per_round):
        self.eng, self.sem, self.per_round, self.n, self.base = eng, sem, per_round, 0, 0

    def round(self, i):
        self.base, self.n = i * self.per_round, 0

    def link(self, ins):
        self.n += 1
        ins.then_inc(self.sem, 1)
        self.eng.wait_ge(self.sem, self.base + self.n)

    def close(self):
        assert self.n == self.per_round, (self.n, self.per_round)


def gnn_ffn(nc, x, src, dst, W1, as1, ad1, b1, W2, as2, ad2, b2, Wr, br,
            fW1, fb1, g1, be1, m1, v1, fW2, fb2, g2, be2, m2, v2, Wo, bo, out):
    N, D = x.shape
    E = src.shape[0]
    HEADS, CH = as1.shape
    HID = HEADS * CH
    NE, _, FH = fW1.shape
    KD = D // P
    KH = FH // P
    SROWS = P * SUPER
    NSUPER = -(-N // SROWS)
    TAIL = N - (NSUPER - 1) * SROWS
    NT = NSUPER * SROWS // TILE
    NG = NT // GROUP
    NPAD = NT * TILE
    EROWS = 125
    ECOLS = E // EROWS
    assert EROWS * ECOLS == E and NT % GROUP == 0 and TAIL % SUPER == 0 and TAIL <= P
    W1COLS = HID + 2 * HEADS
    W2COLS = D + 2
    top = ExitStack()

    def dram(name, shape, dt=F32):
        return nc.dram_tensor(name, shape, dt, kind="Internal").ap()

    edge_list = dram("edge_list", [E + TILE, 2], I32)
    h1_table = dram("h1_table", [NPAD, W1COLS])
    h2_table = dram("h2_table", [NPAD, W2COLS])
    saved_rows = dram("saved_rows", [NPAD, W1COLS])
    x2_table = dram("x2_table", [NPAD, D])
    softmax_state = dram("softmax_state", [NPAD, 2 * HEADS])

    def sem(name, ctx=top):
        return ctx.enter_context(nc.semaphore(name))

    def sb(ctx, name, shape, dt=F32):
        return ctx.enter_context(nc.sbuf_tensor(name, shape, dt))

    def ps(ctx, name, shape, dt=F32):
        return ctx.enter_context(nc.psum_tensor(name, shape, dt))

    with top:
        ident = sb(top, "ident", [P, P])
        iota_row = sb(top, "iota_row", [P, TILE])
        tile_base = sb(top, "tile_base", [P, NT])
        eps_half = sb(top, "eps_half", [P, 16])
        windows = sb(top, "windows", [P, NT, 2], I32)
        place = sb(top, "place", [P, NT])
        starts = sb(top, "starts", [P, NT + 1])
        starts_i = sb(top, "starts_i", [1, NT], I32)
        bad = sb(top, "bad", [P, 1])
        bad_i = sb(top, "bad_i", [1, 1], I32)
        W1x = sb(top, "W1x", [P, KD, W1COLS])
        W2x = sb(top, "W2x", [P, HID // P, W2COLS])
        b1_col = sb(top, "b1_col", [P, HID // P])
        b2_row = sb(top, "b2_row", [P, D])
        wh = {n: sb(top, f"{n}_hi", [P, NE, KD, FH], F32R) for n in ("fW1", "fW2", "Wo")}
        wl = {n: sb(top, f"{n}_lo", [P, NE, KD, FH], F32R) for n in ("fW1", "fW2", "Wo")}
        scale = [sb(top, f"bn_scale{n}", [P, NE, KH]) for n in (1, 2)]
        shift = [sb(top, f"bn_shift{n}", [P, NE, KH]) for n in (1, 2)]
        Wr_hi = sb(top, "Wr_hi", [P, KD, NE], F32R)
        Wr_lo = sb(top, "Wr_lo", [P, KD, NE], F32R)
        br_row = sb(top, "br_row", [P, NE])
        bo_sb = sb(top, "bo_sb", [NE, D])

        phase_edges_and_layer1(locals())
        phase_edge_by_edge(locals(), 1)
        phase_aggregate(locals(), 1)
        phase_edge_by_edge(locals(), 2)
        phase_aggregate(locals(), 2)
        phase_experts(locals())


def row_view(table, i, rows=P * SUPER, per=SUPER):
    return table[bass.ds(i * P * SUPER, rows), :].rearrange("(p j) d -> p j d", j=per)


def phase_edges_and_layer1(v):
    nc, sem, sb, ps = v["nc"], v["sem"], v["sb"], v["ps"]
    N, D, E, HEADS, CH, HID, NE, FH = (v[n] for n in ("N", "D", "E", "HEADS", "CH", "HID", "NE", "FH"))
    KD, KH, NSUPER, TAIL, NT, EROWS, ECOLS, NPAD = (v[n] for n in ("KD", "KH", "NSUPER", "TAIL", "NT", "EROWS", "ECOLS", "NPAD"))
    W1COLS, W2COLS = v["W1COLS"], v["W2COLS"]
    ident, iota_row, tile_base, windows = v["ident"], v["iota_row"], v["tile_base"], v["windows"]
    starts, starts_i, bad, bad_i = v["starts"], v["starts_i"], v["bad"], v["bad_i"]
    W1x, W2x, eps_half = v["W1x"], v["W2x"], v["eps_half"]
    edge_list, x = v["edge_list"], v["x"]
    wh, wl, scale, shift = v["wh"], v["wl"], v["scale"], v["shift"]
    HCOLS = W1COLS

    with ExitStack() as ctx:
        S = lambda name: sem("a_" + name, ctx)
        xin = [sb(ctx, f"xin{b}", [P, SUPER, D]) for b in range(4)]
        z = [sb(ctx, f"z{b}", [P, SUPER, D]) for b in range(2)]
        zT = [sb(ctx, f"zT{b}", [P, KD, SUPER * P]) for b in range(2)]
        hrow = [sb(ctx, f"hrow{b}", [P, SUPER, HCOLS]) for b in range(2)]
        stats = sb(ctx, "stats", [P, SUPER, 6])
        mv = [sb(ctx, f"mv{b}", [P, SUPER, 2]) for b in range(2)]
        vare = [sb(ctx, f"vare{b}", [P, SUPER]) for b in range(2)]
        rstd = [sb(ctx, f"rstd{b}", [P, SUPER]) for b in range(2)]
        ones_bf = sb(ctx, "ones_bf", [P, P], BF16)
        ends = sb(ctx, "ends", [EROWS, 3, ECOLS], I32)
        dstf = sb(ctx, "dstf", [EROWS, 2, ECOLS])
        pairs = sb(ctx, "pairs", [EROWS, ECOLS, 2], I32)
        pad = sb(ctx, "pad", [1, TILE, 2], I32)
        before = sb(ctx, "before", [EROWS, 4, NT], BF16)
        falls = sb(ctx, "falls", [EROWS, ECOLS])
        falls_any = sb(ctx, "falls_any", [EROWS, 1], BF16)
        sizes = sb(ctx, "sizes", [P, NT])
        over = sb(ctx, "over", [P, 2])
        KHID = HID // P
        att = sb(ctx, "att", [P, KHID, 2 * HEADS])
        att2 = sb(ctx, "att2", [P, D // P, 2])
        W1T = sb(ctx, "W1T", [P, KD, KHID, P])
        W2T = sb(ctx, "W2T", [P, KHID, D // P, P])
        stage = {n: sb(ctx, f"stage_{n}", [P, NE, KD, FH]) for n in wh}
        Wr_sb = sb(ctx, "Wr_sb", [P, KD, NE])
        bn = {n: sb(ctx, f"bn_{n}", [P, NE, KH]) for n in
              ("fb1", "g1", "be1", "m1", "v1", "fb2", "g2", "be2", "m2", "v2")}
        bnt = sb(ctx, "bnt", [P, NE, KH])
        zTp = [ps(ctx, f"zTp{b}", [P, KD, SUPER * P]) for b in range(2)]
        hp = [ps(ctx, f"hp{q}", [P, 512]) for q in range(2)]
        cnt_p = ps(ctx, "cnt_p", [P, 512])
        set_p = ps(ctx, "set_p", [P, 512])

        ends_loaded, params_loaded, wr_loaded, bn_loaded = (
            S(n) for n in ("ends_loaded", "params_loaded", "wr_loaded", "bn_loaded"))
        stage_loaded = {n: S(f"stage_{n}_loaded") for n in wh}
        const_ready, ends_ready, pairs_ready, list_stored = (S(n) for n in ("const_ready", "ends_ready", "pairs_ready", "list_stored"))
        before_ready, before_used, counted, falls_ready, starts_ready = (
            S(n) for n in ("before_ready", "before_used", "counted", "falls_ready", "starts_ready"))
        window_loaded = S("window_loaded")
        pe_set, att_ready, dve_set = S("pe_set"), S("att_ready"), S("dve_set")
        x_loaded = [S(f"x_loaded{b}") for b in range(4)]
        h_stored = [S(f"h_stored{b}") for b in range(4)]
        stats_seen, var_ready, rstd_ready, z_ready, zTp_ready, zT_ready, h_ready, hrow_ready = (
            S(n) for n in ("stats_seen", "var_ready", "rstd_ready", "z_ready", "zTp_ready", "zT_ready", "h_ready", "hrow_ready"))
        stage_split, dve_chain, pool_chain = S("stage_split"), S("dve_chain"), S("pool_chain")
        moments_passed, store_passed = S("moments_passed"), S("store_passed")
        last = NSUPER - 1

        block = ctx.enter_context(nc.Block())

        @block.sync
        def _(sp):
            sp.wait_ge(const_ready, 1)
            sp.dma_start(ends[:, 0, :], v["src"].rearrange("(p c) -> p c", c=ECOLS)).then_inc(ends_loaded, 16)
            sp.dma_start(ends[:, 1, :], v["dst"].rearrange("(p c) -> p c", c=ECOLS)).then_inc(ends_loaded, 16)
            body = (EROWS - 1) * ECOLS
            sp.dma_start(ends[0:EROWS - 1, 2, :], v["dst"][1:1 + body].rearrange("(p c) -> p c", c=ECOLS)).then_inc(ends_loaded, 16)
            sp.dma_start(ends[EROWS - 1:EROWS, 2, 0:ECOLS - 1],
                         v["dst"][1 + body:E].rearrange("(p c) -> p c", p=1)).then_inc(ends_loaded, 16)
            sp.dma_start(edge_list[E:E + TILE, :].rearrange("(o e) t -> o e t", o=1), pad[:]).then_inc(list_stored, 16)

            def load(i, b, k):
                wait_count(sp, z_ready, i - 3)
                if isinstance(i, int) and i == last:
                    src = row_view(x, i, TAIL)
                    sp.dma_start(xin[b][0:TAIL // SUPER], src).then_inc(x_loaded[b], 16)
                else:
                    sp.dma_start(xin[b][:], row_view(x, i)).then_inc(x_loaded[b], 16)

            def fill_windows(i, b, k):
                if isinstance(i, int) and i == 0:
                    sp.wait_ge(pairs_ready, 1)
                    sp.dma_start(edge_list[0:E, :].rearrange("(p c) t -> p c t", c=ECOLS), pairs[:]).then_inc(list_stored, 16)
                    sp.wait_ge(list_stored, 32)
                    sp.wait_ge(starts_ready, 1)
                for j in range(NT // NSUPER):
                    t = i * (NT // NSUPER) + j
                    first = sp.value_load(starts_i[0:1, bass.ds(t, 1)], min_val=0, max_val=E)
                    sp.dma_start(windows[:, bass.ds(t, 1), :],
                                 edge_list[bass.ds(first, TILE), :].unsqueeze(1)).then_inc(window_loaded, 16)
            ring(sp, NSUPER, load, fill_windows, 4)
            sp.wait_ge(window_loaded, 16 * NT)
            for b in range(4):
                sp.wait_ge(h_stored[b], 16 * (NSUPER // 4))

        @block.gpsimd
        def _(pool):
            nc.gpsimd.iota(iota_row[:], pattern=[[1, TILE]], base=0, channel_multiplier=0,
                           allow_small_or_imprecise_dtypes=True)
            nc.gpsimd.iota(tile_base[:], pattern=[[TILE, NT]], base=0, channel_multiplier=0,
                           allow_small_or_imprecise_dtypes=True)
            nc.gpsimd.memset(ends[:], NOWHERE)
            nc.gpsimd.memset(pad[:, :, 0:1], 0)
            nc.gpsimd.memset(pad[:, :, 1:2], NOWHERE)
            nc.gpsimd.memset(eps_half[:], -0.5)
            nc.gpsimd.memset(ident[:], 0.0).then_inc(pool_chain, 1)
            pool.wait_ge(pool_chain, 1)
            nc.gpsimd.affine_select(out=ident[:], in_=ident[:], compare_op=ALU.not_equal, fill=1.0, base=0,
                                    pattern=[[-1, P]], channel_multiplier=1).then_inc(const_ready, 1)
            pool.wait_ge(ends_loaded, 64)
            nc.gpsimd.tensor_copy(pairs[:, :, 0], ends[:, 0, :])
            nc.gpsimd.tensor_copy(pairs[:, :, 1], ends[:, 1, :]).then_inc(pairs_ready, 1)

            pool.wait_ge(bn_loaded, 320)
            n = 1
            for l in range(2):
                b_, g_, be_, m_, v_ = (bn[q] for q in (("fb1", "g1", "be1", "m1", "v1"), ("fb2", "g2", "be2", "m2", "v2"))[l])
                half = eps_half[:].rearrange("p (e c) -> p e c", c=KH)
                for op in (lambda: nc.gpsimd.tensor_scalar(bnt[:], v_[:], BN_EPS, None, ALU.add),
                           lambda: nc.gpsimd.tensor_tensor(bnt[:], bnt[:], half, ALU.pow),
                           lambda: nc.gpsimd.tensor_tensor(scale[l][:], g_[:], bnt[:], ALU.mult),
                           lambda: nc.gpsimd.tensor_tensor(b_[:], b_[:], m_[:], ALU.subtract),
                           lambda: nc.gpsimd.tensor_tensor(b_[:], b_[:], scale[l][:], ALU.mult),
                           lambda: nc.gpsimd.tensor_tensor(shift[l][:], be_[:], b_[:], ALU.add)):
                    op().then_inc(pool_chain, 1)
                    n += 1
                    pool.wait_ge(pool_chain, n)

            for q, name in enumerate(wh):
                pool.wait_ge(stage_loaded[name], 16 * NE)
                nc.gpsimd.tensor_copy(wh[name][:], stage[name][:]).then_inc(stage_split, 1)
                pool.wait_ge(stage_split, q + 1)
                nc.gpsimd.tensor_tensor(wl[name][:], stage[name][:], wh[name][:].bitcast(F32), ALU.subtract)

            def power(i, b, k):
                pool.wait_ge(var_ready, i + 1)
                nc.gpsimd.tensor_tensor(rstd[b % 2][:], vare[b % 2][:], eps_half[:, 0:SUPER], ALU.pow).then_inc(rstd_ready, 1)

            def store(i, b, k):
                pool.wait_ge(hrow_ready, (i + 1) * SUPER)
                pool.sem_inc(store_passed, 1)
                pool.dma_start(row_view(v["h1_table"], i), hrow[b % 2][:]).then_inc(h_stored[b], 16)

            ring(pool, NSUPER, power, stores_later(store, NSUPER, 4), 4)

        @block.scalar
        def _(act):
            few = ctx.enter_context(nc.allow_non_contiguous_dma(reason='vectors of parameters, once'))
            for k in range(KD):
                act.dma_start(W1x[:, k, 0:HID], v["W1"][k * P:(k + 1) * P, :]).then_inc(params_loaded, 16)
            for k in range(KHID):
                act.dma_start(W2x[:, k, 0:D], v["W2"][k * P:(k + 1) * P, :]).then_inc(params_loaded, 16)
            act.wait_ge(att_ready, 1)
            for h in range(HEADS):
                for s, a in enumerate((v["as1"], v["ad1"])):
                    c, r = h * CH // P, h * CH % P
                    act.dma_start(att[r:r + CH, c, s * HEADS + h:s * HEADS + h + 1],
                                  a[h:h + 1, :].rearrange("o c -> c o")).then_inc(params_loaded, 16)
            for s, a in enumerate((v["as2"], v["ad2"])):
                for k in range(D // P):
                    act.dma_start(att2[:, k, s:s + 1], a[0:1, k * P:(k + 1) * P].rearrange("o c -> c o")).then_inc(params_loaded, 16)
            act.dma_start(v["b1_col"][:], v["b1"].rearrange("(k c) -> c k", c=P)).then_inc(params_loaded, 16)
            act.dma_start(v["b2_row"][:], v["b2"].partition_broadcast(P)).then_inc(params_loaded, 16)
            act.dma_start(v["br_row"][:], v["br"].partition_broadcast(P)).then_inc(params_loaded, 16)
            act.dma_start(v["bo_sb"][:], v["bo"]).then_inc(params_loaded, 16)
            act.dma_start(Wr_sb[:], v["Wr"].rearrange("(k p) e -> p k e", p=P)).then_inc(wr_loaded, 16)
            for q in bn:
                for k in range(KH):
                    act.dma_start(bn[q][:, :, k], v[q][:, k * P:(k + 1) * P].rearrange("e p -> p e")).then_inc(bn_loaded, 16)

            for name in wh:
                for e in range(NE):
                    act.dma_start(stage[name][:, e], v[name][e].rearrange("(k p) n -> p k n", p=P)).then_inc(stage_loaded[name], 16)

            def evac_zT(i, b, k):
                act.wait_ge(zTp_ready, i + 1)
                wait_count(act, h_ready, (i - 1) * SUPER)
                nc.scalar.activation(zT[b % 2][:], zTp[b % 2][:], ACT.Copy).then_inc(zT_ready, 1)

            def evac_h(i, b, k):
                if not (isinstance(i, int) and i < 2):
                    act.wait_ge(h_stored[(b - 2) % 4], 16 * (k if b < 2 else k + 1))
                for j in range(SUPER):
                    act.wait_ge(h_ready, i * SUPER + j + 1)
                    nc.scalar.activation(hrow[b % 2][:, j, :], hp[j % 2][:, 0:HCOLS], ACT.Copy).then_inc(hrow_ready, 1)

            ring(act, NSUPER, evac_zT, evac_h, 4)

        @block.vector
        def _(dve):
            setup = Chain(dve, dve_set, 0)
            nc.vector.memset(att[:], 0.0).then_inc(att_ready, 1)
            nc.vector.memset(ones_bf[:], 1.0)
            dve.wait_ge(ends_loaded, 64)
            setup.link(nc.vector.tensor_copy(dstf[:], ends[:, 1:3, :]))
            setup.link(nc.vector.tensor_tensor(falls[:], dstf[:, 0, :], dstf[:, 1, :], ALU.is_gt))
            nc.vector.tensor_reduce(falls_any[:], falls[:], axis=AX.X, op=ALU.max).then_inc(falls_ready, 1)
            dve.wait_ge(const_ready, 1)
            for c in range(ECOLS):
                if c >= 4:
                    dve.wait_ge(before_used, c - 3)
                nc.vector.tensor_scalar(before[:, c % 4, :], tile_base[0:EROWS, :], dstf[:, 0, c:c + 1], None,
                                        ALU.is_gt).then_inc(before_ready, 1)
            dve.wait_ge(counted, 1)
            nc.vector.tensor_copy(starts[:, 0:NT], cnt_p[:, 0:NT])
            setup.link(nc.vector.memset(starts[:, NT:NT + 1], float(E)))
            nc.vector.tensor_copy(starts_i[:], starts[0:1, 0:NT])
            setup.link(nc.vector.tensor_tensor(sizes[:], starts[:, 1:NT + 1], starts[:, 0:NT], ALU.subtract))
            setup.link(nc.vector.tensor_reduce(over[:, 0:1], sizes[:], axis=AX.X, op=ALU.max))
            setup.link(nc.vector.tensor_scalar(over[:, 1:2], over[:, 0:1], float(TILE) + 0.5, None, ALU.is_gt))
            setup.link(nc.vector.tensor_tensor(bad[:], cnt_p[:, NT:NT + 1], over[:, 1:2], ALU.add))
            setup.link(nc.vector.tensor_scalar(bad[:], bad[:], 0.5, None, ALU.is_gt))
            nc.vector.tensor_copy(bad_i[:], bad[0:1, :]).then_inc(starts_ready, 1)
            for n, wt in enumerate((W1T, W2T)):
                dve.wait_ge(pe_set, n + 1)
                nc.vector.tensor_copy(wt[:].rearrange("p a b c -> p (a b c)"), set_p[:]).then_inc(att_ready, 1)
            dve.wait_ge(pe_set, 3)
            nc.vector.tensor_copy(W1x[:, :, HID:W1COLS], set_p[:, 0:KD * 2 * HEADS].rearrange("p (k s) -> p k s", k=KD))
            nc.vector.tensor_copy(W2x[:, :, D:W2COLS], set_p[:, 64:64 + 2 * KHID].rearrange("p (k s) -> p k s", k=KHID)).then_inc(att_ready, 1)
            dve.wait_ge(wr_loaded, 16)
            setup.link(nc.vector.tensor_copy(v["Wr_hi"][:], Wr_sb[:]))
            nc.vector.tensor_tensor(v["Wr_lo"][:], Wr_sb[:], v["Wr_hi"][:].bitcast(F32), ALU.subtract)

            chain = Chain(dve, dve_chain, 2)

            def moments(i, b, k):
                chain.round(i)
                dve.wait_ge(x_loaded[b], 16 * k + 16)
                for j in range(SUPER):
                    ins = nc.vector.bn_stats(stats[:, j, :], xin[b][:, j, :])
                chain.link(ins)
                dve.sem_inc(moments_passed, 1)
                for j in range(SUPER):
                    ins = nc.vector.bn_aggr(mv[b % 2][:, j, :], stats[:, j, :])
                chain.link(ins)
                chain.close()
                nc.vector.tensor_scalar(vare[b % 2][:], mv[b % 2][:, :, 1], LN_EPS, None, ALU.add).then_inc(var_ready, 1)

            def normalise(i, b, k):
                dve.wait_ge(rstd_ready, i + 1)
                wait_count(dve, zTp_ready, i - 1)
                for j in range(SUPER):
                    ins = nc.vector.tensor_scalar(z[b % 2][:, j, :], xin[b][:, j, :], mv[b % 2][:, j, 0:1], rstd[b % 2][:, j:j + 1],
                                                  ALU.subtract, ALU.mult)
                ins.then_inc(z_ready, 1)

            ring(dve, NSUPER, moments, normalise, 4)

        @block.tensor
        def _(pe):
            for c in range(ECOLS):
                pe.wait_ge(before_ready, c + 1)
                nc.tensor.matmul(cnt_p[:, 0:NT], ones_bf[0:EROWS, :], before[:, c % 4, :], start=(c == 0),
                                 stop=(c == ECOLS - 1)).then_inc(before_used, 1)
            pe.wait_ge(falls_ready, 1)
            nc.tensor.matmul(cnt_p[:, NT:NT + 1], ones_bf[0:EROWS, :], falls_any[:], start=True, stop=True,
                             skip_group_check=True).then_inc(counted, 1)
            pe.wait_ge(params_loaded, 16 * (KD + KHID + 2 * HEADS + 2 * (D // P) + 4))
            pe.wait_ge(const_ready, 1)
            for n, (w, inner, outer) in enumerate(((W1x, KD, KHID), (W2x, KHID, D // P))):
                if n:
                    pe.wait_ge(att_ready, n + 1)
                for k in range(inner):
                    for c in range(outer):
                        q = k * outer + c
                        ins = nc.tensor.transpose(set_p[:, q * P:(q + 1) * P], w[:, k, c * P:(c + 1) * P], ident[:])
                ins.then_inc(pe_set, 1)
            pe.wait_ge(att_ready, 3)
            for k in range(KD):
                for c in range(KHID):
                    nc.tensor.matmul(set_p[:, k * 2 * HEADS:(k + 1) * 2 * HEADS], W1T[:, k, c, :], att[:, c, :],
                                     start=(c == 0), stop=(c == KHID - 1))
            for k in range(KHID):
                for c in range(D // P):
                    ins = nc.tensor.matmul(set_p[:, 64 + 2 * k:66 + 2 * k], W2T[:, k, c, :], att2[:, c, :],
                                           start=(c == 0), stop=(c == D // P - 1))
            ins.then_inc(pe_set, 1)
            pe.wait_ge(att_ready, 4)

            def transpose_z(i, b, k):
                pe.wait_ge(z_ready, i + 1)
                wait_count(pe, zT_ready, i - 1)
                for j in range(SUPER):
                    for c in range(KD):
                        ins = nc.tensor.transpose(zTp[b % 2][:, c, j * P:(j + 1) * P], z[b % 2][:, j, c * P:(c + 1) * P], ident[:])
                ins.then_inc(zTp_ready, 1)

            def project(i, b, k):
                pe.wait_ge(zT_ready, i + 1)
                for j in range(SUPER):
                    wait_count(pe, hrow_ready, i * SUPER + j - 1)
                    for c in range(KD):
                        ins = nc.tensor.matmul(hp[j % 2][:, 0:HCOLS], zT[b % 2][:, c, j * P:(j + 1) * P], W1x[:, c, :],
                                               start=(c == 0), stop=(c == KD - 1))
                    ins.then_inc(h_ready, 1)

            ring(pe, NSUPER, transpose_z, project, 4)


def phase_edge_by_edge(v, layer):
    nc, sem, sb = v["nc"], v["sem"], v["sb"]
    E, NT = v["E"], v["NT"]
    H = v["HEADS"] if layer == 1 else 1
    F = v["HID"] if layer == 1 else v["D"]
    COLS = v["W1COLS"] if layer == 1 else v["W2COLS"]
    C = F // H
    table = v["h1_table"] if layer == 1 else v["h2_table"]
    state, edge_list, bad_i = v["softmax_state"], v["edge_list"], v["bad_i"]
    saved = v["saved_rows"]

    with ExitStack() as ctx:
        S = lambda name: sem(f"s{layer}_" + name, ctx)
        T = lambda name, shape, dt=F32: sb(ctx, f"s{layer}_" + name, shape, dt)
        edges = T("edges", [1, E, 2], I32)
        parts = T("parts", [P, 2, H])
        first = T("first", [P, 2, H])
        src_row = T("src_row", [1, COLS])
        row = T("row", [1, COLS])
        st = T("st", [1, 2, H])
        score = T("score", [1, H])
        top = T("top", [1, H])
        df = T("df", [1, 2, H])
        ex = T("ex", [1, 2, H])
        inv = T("inv", [1, H])
        w = T("w", [1, 2, H])
        add = T("add", [1, F])
        edges_loaded, parts_loaded, first_ready, state_stored = (
            S(n) for n in ("edges_loaded", "parts_loaded", "first_ready", "state_stored"))
        rows_loaded, rows_stored, df_ready, ex_ready, row_ready, dve_chain, dve_edge, passed = (
            S(n) for n in ("rows_loaded", "rows_stored", "df_ready", "ex_ready", "row_ready", "dve_chain", "dve_edge", "passed"))
        block = ctx.enter_context(nc.Block())

        @block.sync
        def _(sp):
            with sp.If(sp.value_load(bad_i[0:1, 0:1], min_val=0, max_val=1) > 0):
                sp.dma_start(edges[:], edge_list[0:E, :].unsqueeze(0)).then_inc(edges_loaded, 16)
                with sp.Fori(0, NT) as t:
                    sp.dma_start(parts[:], table[bass.ds(t * P, P), F:F + 2 * H].rearrange("p (s h) -> p s h", s=2)).then_inc(parts_loaded, 16)
                    sp.dma_start(saved[bass.ds(t * P, P), 0:COLS], table[bass.ds(t * P, P), :]).then_inc(state_stored, 16)
                    sp.wait_ge(first_ready, t + 1)
                    sp.dma_start(state[bass.ds(t * P, P), 0:2 * H].rearrange("p (s h) -> p s h", s=2), first[:]).then_inc(state_stored, 16)
                    sp.wait_ge(state_stored, 32 * t + 32)
                    sp.sem_inc(passed, 1)
                sp.wait_ge(edges_loaded, 16)
                with sp.Fori(0, E) as e:
                    s = sp.value_load(edges[0:1, bass.ds(e, 1), 0], min_val=0, max_val=v["N"] - 1)
                    d = sp.value_load(edges[0:1, bass.ds(e, 1), 1], min_val=0, max_val=v["N"] - 1)
                    sp.dma_start(src_row[:], saved[bass.ds(s, 1), 0:COLS]).then_inc(rows_loaded, 16)
                    sp.dma_start(row[:], table[bass.ds(d, 1), :]).then_inc(rows_loaded, 16)
                    sp.dma_start(st[:], state[bass.ds(d, 1), 0:2 * H].rearrange("p (s h) -> p s h", s=2)).then_inc(rows_loaded, 16)
                    sp.wait_ge(row_ready, e + 1)
                    sp.dma_start(table[bass.ds(d, 1), :], row[:]).then_inc(rows_stored, 16)
                    sp.dma_start(state[bass.ds(d, 1), 0:2 * H].rearrange("p (s h) -> p s h", s=2), st[:]).then_inc(rows_stored, 16)
                    sp.wait_ge(rows_stored, 32 * e + 32)
                    sp.sem_inc(passed, 1)

        @block.scalar
        def _(act):
            with act.If(act.value_load(bad_i[0:1, 0:1], min_val=0, max_val=1) > 0):
                with act.Fori(0, E) as e:
                    act.wait_ge(df_ready, e + 1)
                    nc.scalar.activation(ex[:], df[:], ACT.Exp).then_inc(ex_ready, 1)

        @block.vector
        def _(dve):
            with dve.If(dve.value_load(bad_i[0:1, 0:1], min_val=0, max_val=1) > 0):
                init = Chain(dve, dve_chain, 1)
                with dve.Fori(0, NT) as t:
                    init.round(t)
                    dve.wait_ge(parts_loaded, 16 * t + 16)
                    init.link(nc.vector.tensor_tensor(first[:, 0], parts[:, 0], parts[:, 1], ALU.add))
                    nc.vector.scalar_tensor_tensor(out=first[:, 0], in0=first[:, 0], scalar=SLOPE, in1=first[:, 0],
                                                   op0=ALU.mult, op1=ALU.max)
                    nc.vector.memset(first[:, 1], 1.0).then_inc(first_ready, 1)
                chain = Chain(dve, dve_edge, 9)
                with dve.Fori(0, E) as e:
                    chain.round(e)
                    heads = lambda t: t[:, 0:F].rearrange("p (h c) -> p h c", h=H)
                    wide = lambda t: t.unsqueeze(2).broadcast_to([1, H, C])
                    dve.wait_ge(rows_loaded, 48 * e + 48)
                    chain.link(nc.vector.tensor_tensor(score[:], src_row[:, F:F + H], row[:, F + H:F + 2 * H], ALU.add))
                    chain.link(nc.vector.scalar_tensor_tensor(out=score[:], in0=score[:], scalar=SLOPE, in1=score[:],
                                                              op0=ALU.mult, op1=ALU.max))
                    chain.link(nc.vector.tensor_tensor(top[:], st[:, 0], score[:], ALU.max))
                    nc.vector.tensor_tensor(df[:, 0], st[:, 0], top[:], ALU.subtract)
                    nc.vector.tensor_tensor(df[:, 1], score[:], top[:], ALU.subtract).then_inc(df_ready, 1)
                    dve.wait_ge(ex_ready, e + 1)
                    chain.link(nc.vector.tensor_tensor(w[:, 0], st[:, 1], ex[:, 0], ALU.mult))
                    chain.link(nc.vector.tensor_tensor(st[:, 1], w[:, 0], ex[:, 1], ALU.add))
                    chain.link(nc.vector.tensor_scalar(st[:, 0], top[:], 1.0, None, ALU.mult))
                    chain.link(nc.vector.reciprocal(inv[:], st[:, 1]))
                    nc.vector.tensor_tensor(w[:, 0], w[:, 0], inv[:], ALU.mult)
                    chain.link(nc.vector.tensor_tensor(w[:, 1], ex[:, 1], inv[:], ALU.mult))
                    nc.vector.tensor_tensor(heads(add), heads(src_row), wide(w[:, 1]), ALU.mult)
                    chain.link(nc.vector.tensor_tensor(heads(row), heads(row), wide(w[:, 0]), ALU.mult))
                    nc.vector.tensor_tensor(row[:, 0:F], row[:, 0:F], add[:], ALU.add).then_inc(row_ready, 1)
                    chain.close()


def phase_aggregate(v, layer):
    nc, sem, sb, ps = v["nc"], v["sem"], v["sb"], v["ps"]
    N, D, NG = (v[n] for n in ("N", "D", "NG"))
    H = v["HEADS"] if layer == 1 else 1
    F = v["HID"] if layer == 1 else D
    COLS = v["W1COLS"] if layer == 1 else v["W2COLS"]
    C = F // H
    table = v["h1_table"] if layer == 1 else v["h2_table"]
    ident, iota_row, windows, place = v["ident"], v["iota_row"], v["windows"], v["place"]
    KF = F // P
    R = GROUP * H
    ROWS = GROUP * TILE
    OC = v["W2COLS"] if layer == 1 else D
    AD, ROW, MAX, NEW, SUM = 0, 2 * R, 2 * R + 2 * P, 3 * R + 2 * P, 4 * R + 2 * P
    assert SUM + 2 * R <= 512

    with ExitStack() as ctx:
        S = lambda name: sem(f"g{layer}_" + name, ctx)
        T = lambda name, shape, dt=F32: sb(ctx, f"g{layer}_" + name, shape, dt)
        sources = [T(f"sources{b}", [P, GROUP], I32) for b in range(2)]
        gat = [T(f"gat{b}", [P, GROUP, COLS]) for b in range(2)]
        own = [T(f"own{b}", [P, GROUP, COLS]) for b in range(2)]
        sel = [T(f"sel{b}", [P, GROUP, TILE]) for b in range(2)]
        selT = T("selT", [P, GROUP, P])
        ad = T("ad", [P, GROUP, 2, H])
        sc = T("sc", [P, 2, GROUP, H])
        rep = T("rep", [P, GROUP, H])
        rows_t = T("rows_t", [R, 2, P])
        news = T("news", [R, 2 * P])
        pen = T("pen", [R, P + 1])
        run = T("run", [R, P])
        back_t = T("back_t", [R, P])
        mx = T("mx", [P, GROUP, H])
        df = T("df", [P, 2, GROUP, H])
        ex = [T(f"ex{b}", [P, GROUP, 2, H]) for b in range(2)]
        msg = [T(f"msg{b}", [P, GROUP, F]) for b in range(2)]
        w = [T(f"w{b}", [P, 2, GROUP, H]) for b in range(2)]
        res = [T(f"res{b}", [P, GROUP, OC]) for b in range(2)]
        bad_far = T("bad_far", [P, 1])
        part = [T(f"part{q}", [P, F]) for q in range(2)]
        if layer == 1:
            scaled = T("scaled", [P, F])
            agg = [T(f"agg{q}", [P, F]) for q in range(2)]
            aggT = [T(f"aggT{q}", [P, KF, P]) for q in range(2)]
        else:
            xin = [T(f"xin{b}", [P, GROUP, D]) for b in range(2)]
        selp = ps(ctx, f"g{layer}_selp", [P, GROUP, P])
        small = ps(ctx, f"g{layer}_small", [P, 512])
        sump = [ps(ctx, f"g{layer}_sump{q}", [P, 512]) for q in range(2)]
        if layer == 1:
            aggp = [ps(ctx, f"g1_aggp{q}", [P, 512]) for q in range(2)]
            outp = ps(ctx, "g1_outp", [P, 512])

        gathered = [S(f"gathered{b}") for b in range(2)]
        own_loaded = [S(f"own_loaded{b}") for b in range(2)]
        res_stored = [S(f"res_stored{b}") for b in range(2)]
        place_ready, sel_ready, selp_ready, selT_ready, ad_ready = (
            S(n) for n in ("place_ready", "sel_ready", "selp_ready", "selT_ready", "ad_ready"))
        sc_ready, rows_ready, runs_ready, max_ready, df_ready, exp_ready, msg_ready = (
            S(n) for n in ("sc_ready", "rows_ready", "runs_ready", "max_ready", "df_ready", "exp_ready", "msg_ready"))
        wsum_ready, w_ready = S("wsum_ready"), S("w_ready")
        sums_ready, agg_ready, dve_chain, tile_chain = (S(n) for n in ("sums_ready", "agg_ready", "dve_chain", "tile_chain"))
        if layer == 1:
            aggp_ready, aggT_ready, outp_ready, out_taken = (S(n) for n in ("aggp_ready", "aggT_ready", "outp_ready", "out_taken"))
        else:
            xb_ready = S("xb_ready")
        pool_chain, bad_ready = S("pool_chain"), S("bad_ready")
        runs_passed, sources_passed = S("runs_passed"), S("sources_passed")
        block = ctx.enter_context(nc.Block())

        def tile_rows(table, g, rows=ROWS):
            return table[bass.ds(g * ROWS, rows), :].rearrange("(j p) d -> p j d", p=P)

        def groups(eng, piece, tile, after=0):
            def body(g, b, k):
                for u in range(GROUP + after):
                    tile(g, b, k, u)
                    if u < GROUP and not (isinstance(g, int) and g == NG - 1):
                        piece(g + 1, 1 - b, k + b, u)
            for u in range(GROUP):
                piece(0, 0, 0, u)
            body(0, 0, 0)
            body(1, 1, 0)
            turns = (NG - 1) // 2
            with eng.Fori(1, turns) as k:
                body(2 * k, 0, k)
                body(2 * k + 1, 1, k)
            for g in range(2 * turns, NG):
                body(g, g % 2, g // 2)

        @block.sync
        def _(sp):
            def load(g, b, k):
                wait_count(sp, agg_ready, (g - 1) * GROUP)
                sp.dma_start(own[b][:], tile_rows(table, g)).then_inc(own_loaded[b], 16)
                if layer == 2:
                    if isinstance(g, int) and g == NG - 1:
                        full = (N - g * ROWS) // P
                        rest = N - g * ROWS - full * P
                        sp.dma_start(xin[b][:, 0:full], tile_rows(v["x"], g, full * P)).then_inc(own_loaded[b], 16)
                        sp.dma_start(xin[b][0:rest, full], v["x"][N - rest:N, :]).then_inc(own_loaded[b], 16)
                    else:
                        sp.dma_start(xin[b][:], tile_rows(v["x"], g)).then_inc(own_loaded[b], 16)

            def store(g, b, k):
                if layer == 1:
                    sp.wait_ge(out_taken, (g + 1) * GROUP)
                    sp.dma_start(tile_rows(v["h2_table"], g), res[b][:]).then_inc(res_stored[b], 16)
                else:
                    sp.wait_ge(agg_ready, (g + 1) * GROUP)
                    sp.dma_start(tile_rows(v["x2_table"], g), res[b][:]).then_inc(res_stored[b], 16)

            ring(sp, NG, load, stores_later(store, NG))
            for b in range(2):
                sp.wait_ge(res_stored[b], 16 * (NG // 2))

        own_dmas = 1 if layer == 1 else 2

        def own_count(g, k):
            more = 1 if layer == 2 and isinstance(g, int) and g == NG - 1 else 0
            return 16 * own_dmas * k + 16 * (own_dmas + more)

        @block.gpsimd
        def _(pool):
            nc.gpsimd.memset(news[:], 1.0).then_inc(place_ready, 1)

            def gather(g, b, k):
                wait_count(pool, msg_ready, g - 1)
                nc.gpsimd.tensor_copy(sources[b][:], windows[:, bass.ds(g * GROUP, GROUP), 0]).then_inc(pool_chain, 1)
                hold(pool, pool_chain, g + 1, sources_passed)
                for j in range(GROUP):
                    pool.indirect_dma_start(gat[b][:, j, :], None, table,
                                            bass.IndirectOffsetOnAxis(ap=sources[b][:, j:j + 1], axis=0)).then_inc(gathered[b], 16)

            def residual(g, b, k):
                if layer == 2:
                    pool.wait_ge(own_loaded[b], own_count(g, k))
                    nc.gpsimd.tensor_tensor(xin[b][:], xin[b][:], v["b2_row"][:].unsqueeze(1).broadcast_to([P, GROUP, D]),
                                            ALU.add).then_inc(xb_ready, 1)

            ring(pool, NG, gather, residual)

        @block.scalar
        def _(act):
            def piece(g, b, k, u):
                if u == 1:
                    act.wait_ge(selp_ready, g + 1)
                    wait_count(act, ad_ready, g)
                    for q in range(2):
                        ins = nc.scalar.activation(selT[:, q * 4:q * 4 + 4, :], selp[:, q * 4:q * 4 + 4, :], ACT.Copy)
                    ins.then_inc(selT_ready, 1)
                if u == 5:
                    act.wait_ge(df_ready, g + 1)
                    nc.scalar.activation(ex[b][:].rearrange("p j s h -> p s j h"), df[:], ACT.Exp).then_inc(exp_ready, 1)

            def tile(g, b, k, u):
                if layer == 2:
                    return
                n = g * GROUP + u
                if 1 <= u <= GROUP:
                    act.wait_ge(aggp_ready, n)
                    for c in range(KF):
                        ins = nc.scalar.activation(aggT[(u - 1) % 2][:, c, :], aggp[(u - 1) % 2][:, c * P:(c + 1) * P], ACT.Relu,
                                                   bias=v["b1_col"][:, c:c + 1])
                    ins.then_inc(aggT_ready, 1)
                if u >= 2:
                    act.wait_ge(outp_ready, n - 1)
                    if u == 2 and not (isinstance(g, int) and g < 2):
                        act.wait_ge(res_stored[b], 16 * k)
                    nc.scalar.activation(res[b][:, u - 2, :], outp[:, 0:OC], ACT.Copy).then_inc(out_taken, 1)

            groups(act, piece, tile, 2)

        @block.vector
        def _(dve):
            nc.vector.tensor_scalar(bad_far[:], v["bad"][:], float(NOWHERE), None, ALU.mult).then_inc(bad_ready, 1)
            dve.wait_ge(bad_ready, 1)
            nc.vector.scalar_tensor_tensor(out=place[:], in0=windows[:, :, 1], scalar=bad_far[:, 0:1], in1=v["tile_base"][:],
                                           op0=ALU.add, op1=ALU.subtract).then_inc(place_ready, 1)
            dve.wait_ge(place_ready, 2)
            chain = Chain(dve, dve_chain, 10)
            chain_t = Chain(dve, tile_chain, 2 if layer == 1 else 1)
            heads = lambda t: t.rearrange("p (h c) -> p h c", h=H)

            def piece(g, b, k, u):
                if u == 0:
                    wait_count(dve, sums_ready, (g - 1) * GROUP)
                    for j in range(GROUP):
                        ins = nc.vector.tensor_scalar(sel[b][:, j, :], iota_row[:], place[:, bass.ds(g * GROUP + j, 1)], None,
                                                      ALU.is_equal)
                    ins.then_inc(sel_ready, 1)
                if u == 2:
                    chain.round(g)
                    dve.wait_ge(ad_ready, g + 1)
                    chain.link(nc.vector.tensor_copy(ad[:], small[:, AD:AD + 2 * R].rearrange("p (j s h) -> p j s h", j=GROUP, s=2)))
                    nc.vector.tensor_scalar(rep[:], place[:, bass.ds(g * GROUP, GROUP)].unsqueeze(2).broadcast_to([P, GROUP, H]),
                                            1.0, None, ALU.mult)
                    dve.wait_ge(gathered[b], 16 * GROUP * k + 16 * GROUP)
                    nc.vector.tensor_tensor(sc[:, 0], gat[b][:, :, F:F + H], ad[:, :, 1, :], ALU.add)
                    chain.link(nc.vector.tensor_tensor(sc[:, 1], ad[:, :, 0, :], ad[:, :, 1, :], ALU.add))
                    nc.vector.scalar_tensor_tensor(out=sc[:], in0=sc[:], scalar=SLOPE, in1=sc[:], op0=ALU.mult,
                                                   op1=ALU.max).then_inc(sc_ready, 1)
                if u == 3:
                    dve.wait_ge(rows_ready, g + 1)
                    chain.link(nc.vector.tensor_copy(rows_t[:], small[0:R, ROW:ROW + 2 * P].rearrange("r (s e) -> r s e", s=2)))
                    chain.link(nc.vector.tensor_tensor(news[:, 1:P], rows_t[:, 1, 1:P], rows_t[:, 1, 0:P - 1], ALU.not_equal))
                    chain.link(nc.vector.tensor_scalar(pen[:], news[:, 0:P + 1], -BIG, None, ALU.mult))
                    chain.link(nc.vector.tensor_tensor_scan(run[:], pen[:, 0:P], rows_t[:, 0, :], -BIG, ALU.add, ALU.max))
                    nc.vector.tensor_tensor_scan(back_t[:, ::-1], pen[:, 1:P + 1][:, ::-1], run[:, ::-1], -BIG, ALU.add,
                                                 ALU.max).then_inc(runs_ready, 1)
                if u == 5:
                    dve.wait_ge(max_ready, g + 1)
                    chain.link(nc.vector.tensor_tensor(mx[:], small[:, MAX:MAX + R].rearrange("p (j h) -> p j h", j=GROUP), sc[:, 1], ALU.max))
                    chain.link(nc.vector.tensor_tensor(df[:], sc[:], mx[:].unsqueeze(1).broadcast_to([P, 2, GROUP, H]), ALU.subtract))
                    nc.vector.tensor_scalar(df[:], df[:], 0.0, None, ALU.min).then_inc(df_ready, 1)
                if u == 6:
                    dve.wait_ge(exp_ready, g + 1)
                    nc.vector.scalar_tensor_tensor(
                        out=ex[b][:, :, 1, :], in0=ex[b][:, :, 1, :], scalar=-1.0,
                        in1=small[:, NEW:NEW + R].rearrange("p (j h) -> p j h", j=GROUP), op0=ALU.add, op1=ALU.mult)
                    nc.vector.tensor_tensor(
                        msg[b][:].rearrange("p j (h c) -> p j h c", h=H), gat[b][:, :, 0:F].rearrange("p j (h c) -> p j h c", h=H),
                        ex[b][:, :, 0, :].unsqueeze(3).broadcast_to([P, GROUP, H, C]), ALU.mult).then_inc(msg_ready, 1)
                if u == 7:
                    sums = small[:, SUM:SUM + 2 * R].rearrange("p (j s h) -> p s j h", j=GROUP, s=2)
                    dve.wait_ge(wsum_ready, g + 1)
                    chain.link(nc.vector.tensor_scalar(w[b][:, 0], sums[:, 1], 1.0, None, ALU.add))
                    chain.link(nc.vector.tensor_tensor(w[b][:, 1], w[b][:, 0], sums[:, 0], ALU.add))
                    nc.vector.reciprocal(w[b][:, 1], w[b][:, 1]).then_inc(w_ready, 1)
                    chain.close()

            def tile(g, b, k, u):
                chain_t.round(g * GROUP + u)
                mine, q = own[b][:, u, 0:F], u % 2
                if u == 0:
                    dve.wait_ge(w_ready, g + 1)
                    if layer == 2:
                        dve.wait_ge(xb_ready, g + 1)
                        if not (isinstance(g, int) and g < 2):
                            dve.wait_ge(res_stored[b], 16 * k)
                if layer == 1:
                    chain_t.link(nc.vector.tensor_tensor(heads(part[q][:]), heads(mine),
                                                         w[b][:, 0, u, :].unsqueeze(2).broadcast_to([P, H, C]), ALU.mult))
                dve.wait_ge(sums_ready, g * GROUP + u + 1)
                if layer == 1:
                    chain_t.link(nc.vector.tensor_tensor(scaled[:], sump[q][:, 0:F], part[q][:], ALU.add))
                    nc.vector.tensor_tensor(heads(agg[q][:]), heads(scaled[:]), w[b][:, 1, u, :].unsqueeze(2).broadcast_to([P, H, C]),
                                            ALU.mult).then_inc(agg_ready, 1)
                else:
                    chain_t.link(nc.vector.scalar_tensor_tensor(out=part[q][:], in0=mine, scalar=w[b][:, 0, u, 0:1],
                                                                in1=sump[q][:, 0:F], op0=ALU.mult, op1=ALU.add))
                    nc.vector.scalar_tensor_tensor(out=res[b][:, u, :], in0=part[q][:], scalar=w[b][:, 1, u, 0:1],
                                                   in1=xin[b][:, u, :], op0=ALU.mult, op1=ALU.add).then_inc(agg_ready, 1)
                chain_t.close()

            groups(dve, piece, tile)

        @block.tensor
        def _(pe):
            def piece(g, b, k, u):
                if u == 1:
                    pe.wait_ge(sel_ready, g + 1)
                    wait_count(pe, selT_ready, g)
                    for j in range(GROUP):
                        ins = nc.tensor.transpose(selp[:, j, :], sel[b][:, j, :], ident[:])
                    ins.then_inc(selp_ready, 1)
                if u == 2:
                    pe.wait_ge(selT_ready, g + 1)
                    pe.wait_ge(own_loaded[b], own_count(g, k))
                    wait_count(pe, w_ready, g)
                    for j in range(GROUP):
                        ins = nc.tensor.matmul(small[:, AD + j * 2 * H:AD + (j + 1) * 2 * H], selT[:, j, :], own[b][:, j, F:F + 2 * H],
                                               start=True, stop=True)
                    ins.then_inc(ad_ready, 1)
                if u == 3:
                    pe.wait_ge(sc_ready, g + 1)
                    nc.tensor.transpose(small[0:R, ROW:ROW + P], sc[:, 0].rearrange("p j h -> p (j h)"), ident[:])
                    nc.tensor.transpose(small[0:R, ROW + P:ROW + 2 * P], rep[:].rearrange("p j h -> p (j h)"), ident[:]).then_inc(rows_ready, 1)
                if u == 5:
                    hold(pe, runs_ready, g + 1, runs_passed)
                    nc.tensor.transpose(small[:, MAX:MAX + R], back_t[:], ident[0:R, 0:R])
                    nc.tensor.transpose(small[:, NEW:NEW + R], news[:, 0:P], ident[0:R, 0:R]).then_inc(max_ready, 1)
                if u == 7:
                    pe.wait_ge(msg_ready, g + 1)
                    for j in range(GROUP):
                        ins = nc.tensor.matmul(small[:, SUM + j * 2 * H:SUM + (j + 1) * 2 * H], sel[b][:, j, :],
                                               ex[b][:, j].rearrange("p s h -> p (s h)"), start=True, stop=True)
                    ins.then_inc(wsum_ready, 1)

            def tile(g, b, k, u):
                n = g * GROUP + u
                if u < GROUP:
                    wait_count(pe, agg_ready, n - 1)
                    nc.tensor.matmul(sump[u % 2][:, 0:F], sel[b][:, u, :], msg[b][:, u, :], start=True, stop=True).then_inc(sums_ready, 1)
                if layer == 2:
                    return
                if 1 <= u <= GROUP:
                    q = (u - 1) % 2
                    pe.wait_ge(agg_ready, n)
                    wait_count(pe, aggT_ready, n - 2)
                    for c in range(KF):
                        ins = nc.tensor.transpose(aggp[q][:, c * P:(c + 1) * P], agg[q][:, c * P:(c + 1) * P], ident[:])
                    ins.then_inc(aggp_ready, 1)
                if u >= 2:
                    q = u % 2
                    pe.wait_ge(aggT_ready, n - 1)
                    wait_count(pe, out_taken, n - 2)
                    for c in range(KF):
                        ins = nc.tensor.matmul(outp[:, 0:OC], aggT[q][:, c, :], v["W2x"][:, c, :],
                                               start=(c == 0), stop=(c == KF - 1))
                    ins.then_inc(outp_ready, 1)

            groups(pe, piece, tile, 0 if layer == 2 else 2)


def phase_experts(v):
    nc, sem, sb, ps = v["nc"], v["sem"], v["sb"], v["ps"]
    D, NE, FH, KD, KH, NSUPER, TAIL = (v[n] for n in ("D", "NE", "FH", "KD", "KH", "NSUPER", "TAIL"))
    ident, wh, wl, scale, shift = v["ident"], v["wh"], v["wl"], v["scale"], v["shift"]
    last = NSUPER - 1
    with ExitStack() as ctx:
        S = lambda name: sem("e_" + name, ctx)
        T = lambda name, shape, dt=F32: sb(ctx, "e_" + name, shape, dt)
        xin = [T(f"xin{b}", [P, SUPER, D]) for b in range(2)]
        z = T("z", [P, SUPER, D])
        z_hi = [T(f"z_hi{b}", [P, KD, SUPER * P], F32R) for b in range(2)]
        z_lo = [T(f"z_lo{b}", [P, KD, SUPER * P], F32R) for b in range(2)]
        stats = T("stats", [P, SUPER, 6])
        mv = T("mv", [P, SUPER, 2])
        vare = T("vare", [P, SUPER])
        rstd = T("rstd", [P, SUPER])
        logit = T("logit", [P, SUPER, NE])
        top1 = T("top1", [P, SUPER])
        tot = T("tot", [P, SUPER])
        share = [T(f"share{b}", [P, SUPER, NE]) for b in range(2)]
        shareT = T("shareT", [NE, SUPER * P])
        acc = [T(f"acc{b}", [P, SUPER, D]) for b in range(2)]
        h = [T(f"h{l}", [P, KH, SUPER * P]) for l in (1, 2)]
        h_hi = [T(f"h{l}_hi", [P, KH, SUPER * P], F32R) for l in (1, 2)]
        h_lo = [T(f"h{l}_lo", [P, KH, SUPER * P], F32R) for l in (1, 2)]
        up = [ps(ctx, f"e_u{l}", [P, KH, 512]) for l in (1, 2)]
        yp = ps(ctx, "e_y", [P, SUPER, D])
        misc = ps(ctx, "e_misc", [P, 2, 512])
        x_loaded = [S(f"x_loaded{b}") for b in range(2)]
        out_stored = [S(f"out_stored{b}") for b in range(2)]
        (var_ready, rstd_ready, z_ready, zT_ready, z_hi_ready, z_lo_ready, logit_ready, exp_in, exp_ready, share_ready,
         shareT_p, shareT_ready, bias_ready, acc_ready, dve_chain) = (
            S(n) for n in ("var_ready", "rstd_ready", "z_ready", "zT_ready", "z_hi_ready", "z_lo_ready", "logit_ready", "exp_in",
                           "exp_ready", "share_ready", "shareT_p", "shareT_ready", "bias_ready", "acc_ready", "dve_chain"))
        u_ready = [S(f"u{l}_ready") for l in (1, 2)]
        hi_ready = [S(f"h{l}_hi_ready") for l in (1, 2)]
        lo_ready = [S(f"h{l}_lo_ready") for l in (1, 2)]
        y_ready, y_taken, tot_ready = S("y_ready"), S("y_taken"), S("tot_ready")
        moments_passed = S("moments_passed")
        width = lambda i: 1 if isinstance(i, int) and i == last else SUPER
        HALVES = 2
        halves = lambda i: 1 if isinstance(i, int) and i == last else HALVES

        def half_count(i, e, q):
            if isinstance(i, int) and i == last:
                return last * NE * HALVES + e + 1
            return (i * NE + e) * HALVES + q + 1


        def experts(eng, ahead, step):
            def body(i, b, k):
                for e in range(NE):
                    step(i, b, k, e)
                    if not (isinstance(i, int) and i == last):
                        ahead(i + 1, 1 - b, k + b, e)
            for e in range(NE):
                ahead(0, 0, 0, e)
            step(0, 0, 0, -1)
            body(0, 0, 0)
            body(1, 1, 0)
            turns = (NSUPER - 1) // 2
            with eng.Fori(1, turns) as k:
                body(2 * k, 0, k)
                body(2 * k + 1, 1, k)
            for i in range(2 * turns, NSUPER):
                body(i, i % 2, i // 2)

        block = ctx.enter_context(nc.Block())

        @block.sync
        def _(sp):
            def load(i, b, k):
                wait_count(sp, acc_ready, i - 1)
                if isinstance(i, int) and i == last:
                    sp.dma_start(xin[b][:, 0:1, :], row_view(v["x2_table"], i, P, 1)).then_inc(x_loaded[b], 16)
                else:
                    sp.dma_start(xin[b][:], row_view(v["x2_table"], i)).then_inc(x_loaded[b], 16)

            def store(i, b, k):
                sp.wait_ge(y_taken, half_count(i, NE - 1, halves(i) - 1))
                if isinstance(i, int) and i == last:
                    sp.dma_start(row_view(v["out"], i, TAIL, 1), acc[b][0:TAIL, 0:1, :]).then_inc(out_stored[b], 16)
                else:
                    sp.dma_start(row_view(v["out"], i), acc[b][:]).then_inc(out_stored[b], 16)

            ring(sp, NSUPER, load, stores_later(store, NSUPER))
            for b in range(2):
                sp.wait_ge(out_stored[b], 16 * (NSUPER // 2))


        @block.gpsimd
        def _(pool):
            def power(i, b, k):
                pool.wait_ge(var_ready, i + 1)
                nc.gpsimd.tensor_tensor(rstd[:], vare[:], v["eps_half"][:, 0:SUPER], ALU.pow).then_inc(rstd_ready, 1)
            ring(pool, NSUPER, power, lambda i, b, k: None)

        @block.scalar
        def _(act):
            def ahead(i, b, k, n):
                w = width(i) * P
                if n == 3:
                    act.wait_ge(zT_ready, i + 1)
                    for c in range(KD):
                        ins = nc.scalar.activation(z_hi[b][:, c, 0:w], misc[:, c, 0:w], ACT.Copy)
                    ins.then_inc(z_hi_ready, 1)
                if n == 5:
                    act.wait_ge(exp_in, i + 1)
                    nc.scalar.activation(share[b][:], logit[:], ACT.Exp).then_inc(exp_ready, 1)

            def relu(l, i, e, last_w):
                for c in range(KH):
                    act.wait_ge(u_ready[l], (i * NE + e) * KH + c + 1)
                    for o in (h[l], h_hi[l]):
                        ins = nc.scalar.activation(o[:, c, 0:last_w], up[l][:, c, 0:last_w], ACT.Relu,
                                                   bias=shift[l][:, e, c:c + 1], scale=scale[l][:, e, c:c + 1])
                    ins.then_inc(hi_ready[l], 1)

            def step(i, b, k, e):
                if e >= 0:
                    relu(1, i, e, width(i) * P)
                if e + 1 < NE:
                    relu(0, i, e + 1, width(i) * P)
                elif not (isinstance(i, int) and i == last):
                    relu(0, i + 1, 0, width(i + 1) * P)

            experts(act, ahead, step)

        @block.vector
        def _(dve):
            chain = Chain(dve, dve_chain, 5)

            def ahead(i, b, k, n):
                w = width(i)
                if n == 0:
                    chain.round(i)
                    dve.wait_ge(x_loaded[b], 16 * k + 16)
                    for j in range(w):
                        ins = nc.vector.bn_stats(stats[:, j, :], xin[b][:, j, :])
                    chain.link(ins)
                    dve.sem_inc(moments_passed, 1)
                    for j in range(w):
                        ins = nc.vector.bn_aggr(mv[:, j, :], stats[:, j, :])
                    chain.link(ins)
                    nc.vector.tensor_scalar(vare[:], mv[:, :, 1], LN_EPS, None, ALU.add).then_inc(var_ready, 1)
                if n == 1:
                    dve.wait_ge(rstd_ready, i + 1)
                    for j in range(w):
                        ins = nc.vector.tensor_scalar(z[:, j, :], xin[b][:, j, :], mv[:, j, 0:1], rstd[:, j:j + 1],
                                                      ALU.subtract, ALU.mult)
                    ins.then_inc(z_ready, 1)
                if n == 3:
                    dve.wait_ge(z_hi_ready, i + 1)
                    for c in range(KD):
                        ins = nc.vector.tensor_tensor(z_lo[b][:, c, 0:w * P], misc[:, c, 0:w * P],
                                                      z_hi[b][:, c, 0:w * P].bitcast(F32), ALU.subtract)
                    ins.then_inc(z_lo_ready, 1)
                if n == 4:
                    dve.wait_ge(logit_ready, i + 1)
                    lg = misc[:, 0, 0:w * NE].rearrange("p (j e) -> p j e", j=w)
                    chain.link(nc.vector.tensor_tensor(logit[:, 0:w], lg, v["br_row"][:].unsqueeze(1).broadcast_to([P, w, NE]), ALU.add))
                    chain.link(nc.vector.tensor_reduce(top1[:, 0:w], logit[:, 0:w], axis=AX.X, op=ALU.max))
                    nc.vector.tensor_tensor(logit[:, 0:w], logit[:, 0:w], top1[:, 0:w].unsqueeze(2).broadcast_to([P, w, NE]),
                                            ALU.subtract).then_inc(exp_in, 1)
                if n == 5:
                    dve.wait_ge(exp_ready, i + 1)
                    chain.link(nc.vector.tensor_reduce(tot[:, 0:w], share[b][:, 0:w], axis=AX.X, op=ALU.add))
                    nc.vector.reciprocal(tot[:, 0:w], tot[:, 0:w]).then_inc(tot_ready, 1)
                    dve.wait_ge(tot_ready, i + 1)
                    nc.vector.tensor_tensor(share[b][:, 0:w], share[b][:, 0:w], tot[:, 0:w].unsqueeze(2).broadcast_to([P, w, NE]),
                                            ALU.mult).then_inc(share_ready, 1)
                    chain.close()
                if n == 6:
                    dve.wait_ge(shareT_p, i + 1)
                    nc.vector.tensor_copy(shareT[:, 0:w * P], misc[0:NE, 1, 0:w * P]).then_inc(shareT_ready, 1)
                if n == 7:
                    dve.wait_ge(bias_ready, i + 1)
                    if not (isinstance(i, int) and i < 2):
                        dve.wait_ge(out_stored[b], 16 * k)
                    both = misc[:].rearrange("p q (j d) -> p (q j) d", d=D)
                    nc.vector.tensor_tensor(acc[b][:, 0:w], both[:, 0:w], xin[b][:, 0:w], ALU.add).then_inc(acc_ready, 1)

            def low(l, i, e, w):
                for c in range(KH):
                    dve.wait_ge(hi_ready[l], (i * NE + e) * KH + c + 1)
                    nc.vector.tensor_tensor(h_lo[l][:, c, 0:w], h[l][:, c, 0:w], h_hi[l][:, c, 0:w].bitcast(F32),
                                            ALU.subtract).then_inc(lo_ready[l], 1)

            def step(i, b, k, e):
                w = width(i)
                if e >= 0:
                    low(1, i, e, w * P)
                if e + 1 < NE:
                    low(0, i, e + 1, w * P)
                elif not (isinstance(i, int) and i == last):
                    low(0, i + 1, 0, width(i + 1) * P)
                if e < 0:
                    return
                dve.wait_ge(acc_ready, i + 1)
                for q in range(halves(i)):
                    dve.wait_ge(y_ready, half_count(i, e, q))
                    if e:
                        dve.wait_ge(y_taken, half_count(i, e - 1, q))
                    for j in range(q * 2, min(q * 2 + 2, w)):
                        ins = nc.vector.scalar_tensor_tensor(out=acc[b][:, j, :], in0=yp[:, j, :], scalar=share[b][:, j, e:e + 1],
                                                             in1=acc[b][:, j, :], op0=ALU.mult, op1=ALU.add)
                    ins.then_inc(y_taken, 1)

            experts(dve, ahead, step)

        @block.tensor
        def _(pe):
            def ahead(i, b, k, n):
                w = width(i)
                if n == 3:
                    pe.wait_ge(z_ready, i + 1)
                    wait_count(pe, acc_ready, i)
                    for j in range(w):
                        for c in range(KD):
                            ins = nc.tensor.transpose(misc[:, c, j * P:(j + 1) * P], z[:, j, c * P:(c + 1) * P], ident[:])
                    ins.then_inc(zT_ready, 1)
                if n == 4:
                    pe.wait_ge(z_lo_ready, i + 1)
                    for j in range(w):
                        terms = [(zz, ww, c) for c in range(KD) for zz, ww in
                                 ((z_hi[b], v["Wr_hi"]), (z_hi[b], v["Wr_lo"]), (z_lo[b], v["Wr_hi"]))]
                        for n_, (zz, ww, c) in enumerate(terms):
                            ins = nc.tensor.matmul(misc[:, 0, j * NE:(j + 1) * NE], zz[:, c, j * P:(j + 1) * P], ww[:, c, :],
                                                   start=(n_ == 0), stop=(n_ == len(terms) - 1))
                    ins.then_inc(logit_ready, 1)
                if n == 6:
                    pe.wait_ge(share_ready, i + 1)
                    for j in range(w):
                        ins = nc.tensor.transpose(misc[0:NE, 1, j * P:(j + 1) * P], share[b][:, j, :], ident[:])
                    ins.then_inc(shareT_p, 1)
                if n == 7:
                    pe.wait_ge(shareT_ready, i + 1)
                    both = misc[:].rearrange("p q (j d) -> p (q j) d", d=D)
                    for j in range(w):
                        ins = nc.tensor.matmul(both[:, j, :], shareT[:, j * P:(j + 1) * P], v["bo_sb"][:], start=True, stop=True)
                    ins.then_inc(bias_ready, 1)

            def dense(l, i, e, rhs_hi, rhs_lo, name, w, chunks):
                for c in range(chunks):
                    terms = [(ww, rr, k) for k in range(KD) for ww, rr in
                             ((wh[name], rhs_hi), (wl[name], rhs_hi), (wh[name], rhs_lo))]
                    for n, (ww, rr, k) in enumerate(terms):
                        ins = nc.tensor.matmul(up[l][:, c, 0:w], ww[:, e, k, c * P:(c + 1) * P], rr[:, k, 0:w],
                                               start=(n == 0), stop=(n == len(terms) - 1))
                    ins.then_inc(u_ready[l], 1)

            def step(i, b, k, e):
                w = width(i)
                if e >= 0:
                    pe.wait_ge(lo_ready[0], (i * NE + e + 1) * KH)
                    dense(1, i, e, h_hi[0], h_lo[0], "fW2", w * P, KH)
                if e + 1 < NE:
                    if e < 0:
                        pe.wait_ge(z_lo_ready, i + 1)
                    dense(0, i, e + 1, z_hi[b], z_lo[b], "fW1", w * P, KH)
                elif not (isinstance(i, int) and i == last):
                    dense(0, i + 1, 0, z_hi[1 - b], z_lo[1 - b], "fW1", width(i + 1) * P, KH)
                if e < 0:
                    return
                pe.wait_ge(lo_ready[1], (i * NE + e + 1) * KH)
                for q in range(halves(i)):
                    if e:
                        pe.wait_ge(y_taken, half_count(i, e - 1, q))
                    elif not (isinstance(i, int) and i == 0):
                        pe.wait_ge(y_taken, (i * NE - 1) * HALVES + q + 1)
                    for j in range(q * 2, min(q * 2 + 2, w)):
                        terms = [(hh, ww, k) for k in range(KH) for hh, ww in
                                 ((h_hi[1], wh["Wo"]), (h_hi[1], wl["Wo"]), (h_lo[1], wh["Wo"]))]
                        for n, (hh, ww, c) in enumerate(terms):
                            ins = nc.tensor.matmul(yp[:, j, :], hh[:, c, j * P:(j + 1) * P], ww[:, e, c, :],
                                                   start=(n == 0), stop=(n == len(terms) - 1))
                    ins.then_inc(y_ready, 1)

            experts(pe, ahead, step)


_INS = ["x", "src", "dst", "L0_gnn_W1", "L0_gnn_att_src1", "L0_gnn_att_dst1", "L0_gnn_b1", "L0_gnn_W2", "L0_gnn_att_src2",
        "L0_gnn_att_dst2", "L0_gnn_b2", "L0_ffn_Wr", "L0_ffn_br", "L0_ffn_W1", "L0_ffn_b1", "L0_ffn_g1", "L0_ffn_be1",
        "L0_ffn_m1", "L0_ffn_v1", "L0_ffn_W2", "L0_ffn_b2", "L0_ffn_g2", "L0_ffn_be2", "L0_ffn_m2", "L0_ffn_v2",
        "L0_ffn_Wo", "L0_ffn_bo"]


def kernel(**inputs):
    import numpy as _np
    import concourse.bacc as _bacc
    from concourse import mybir as _mybir
    from concourse.bass_utils import run_bass_kernel_spmd as _run

    nc = _bacc.Bacc("TRN2", target_bir_lowering=False, num_devices=1)
    arrays, args = {}, []
    for name in _INS:
        a = _np.ascontiguousarray(inputs[name])
        arrays[f"in_{name}"] = a
        args.append(nc.dram_tensor(f"in_{name}", a.shape, _mybir.dt.from_np(a.dtype), kind="ExternalInput").ap())
    shape = inputs["x"].shape
    args.append(nc.dram_tensor("out_0", shape, _mybir.dt.float32, kind="ExternalOutput").ap())
    gnn_ffn(nc, *args)
    r = _run(nc, [arrays], core_ids=[0])
    return r.results[0]["out_0"]
```

```python
import numpy as np
import concourse.bass as bass
from concourse import mybir
from contextlib import ExitStack

F32 = mybir.dt.float32
F32R = mybir.dt.float32r
BF16 = mybir.dt.bfloat16
I32 = mybir.dt.int32
ALU = mybir.AluOpType
ACT = mybir.ActivationFunctionType
AX = mybir.AxisListType

P = 128
LN_EPS = 1e-5
BN_EPS = 1e-3
SLOPE = 0.2
BIG = 3e38
NOWHERE = 1 << 20
TILE = 128
GROUP = 8
QUAD = 32
SUPER = 4


def ring(eng, count, front, back, slots=2):
    front(0, 0, 0)
    for i in range(slots):
        front(i + 1, (i + 1) % slots, (i + 1) // slots)
        back(i, i, 0)
    turns = (count - 1) // slots
    if turns > 1:
        with eng.Fori(1, turns) as k:
            for q in range(slots):
                front(slots * k + q + 1, (q + 1) % slots, k + (q + 1) // slots)
                back(slots * k + q, q, k)
    for i in range(slots * turns, count):
        if i + 1 < count:
            front(i + 1, (i + 1) % slots, (i + 1) // slots)
        back(i, i % slots, i // slots)


def wait_count(eng, sem, count):
    if isinstance(count, int) and count <= 0:
        return
    eng.wait_ge(sem, count)


def hold(eng, sem, count, passed):
    eng.wait_ge(sem, count)
    eng.sem_inc(passed, 1)


def stores_later(store, count, slots=2):
    def back(i, b, k):
        if isinstance(i, int) and i == 0:
            return
        store(i - 1, (b - 1) % slots, k - 1 if b == 0 else k)
        if isinstance(i, int) and i == count - 1:
            store(i, b, k)
    return back


class Chain:

    def __init__(self, eng, sem, per_round):
        self.eng, self.sem, self.per_round, self.n, self.base = eng, sem, per_round, 0, 0

    def round(self, i):
        self.base, self.n = i * self.per_round, 0

    def link(self, ins):
        self.n += 1
        ins.then_inc(self.sem, 1)
        self.eng.wait_ge(self.sem, self.base + self.n)

    def close(self):
        assert self.n == self.per_round, (self.n, self.per_round)


def gnn_ffn(nc, x, src, dst, W1, as1, ad1, b1, W2, as2, ad2, b2, Wr, br,
            fW1, fb1, g1, be1, m1, v1, fW2, fb2, g2, be2, m2, v2, Wo, bo, out):
    N, D = x.shape
    E = src.shape[0]
    HEADS, CH = as1.shape
    HID = HEADS * CH
    NE, _, FH = fW1.shape
    KD = D // P
    KH = FH // P
    SROWS = P * SUPER
    NSUPER = -(-N // SROWS)
    TAIL = N - (NSUPER - 1) * SROWS
    NT = NSUPER * SROWS // TILE
    NG = NT // GROUP
    NPAD = NT * TILE
    EROWS = 125
    ECOLS = E // EROWS
    assert EROWS * ECOLS == E and NT % GROUP == 0 and TAIL % SUPER == 0 and TAIL <= P
    W1COLS = HID + 2 * HEADS
    W2COLS = D + 2
    top = ExitStack()

    def dram(name, shape, dt=F32):
        return nc.dram_tensor(name, shape, dt, kind="Internal").ap()

    edge_list = dram("edge_list", [E + TILE, 2], I32)
    h1_table = dram("h1_table", [NPAD, W1COLS])
    h2_table = dram("h2_table", [NPAD, W2COLS])
    saved_rows = dram("saved_rows", [NPAD, W1COLS])
    x2_table = dram("x2_table", [NPAD, D])
    softmax_state = dram("softmax_state", [NPAD, 2 * HEADS])

    def sem(name, ctx=top):
        return ctx.enter_context(nc.semaphore(name))

    def sb(ctx, name, shape, dt=F32):
        return ctx.enter_context(nc.sbuf_tensor(name, shape, dt))

    def ps(ctx, name, shape, dt=F32):
        return ctx.enter_context(nc.psum_tensor(name, shape, dt))

    with top:
        waits_passed = sem("waits_passed")
        ident = sb(top, "ident", [P, P])
        iota_row = sb(top, "iota_row", [P, TILE])
        tile_base = sb(top, "tile_base", [P, NT])
        eps_half = sb(top, "eps_half", [P, 16])
        windows = sb(top, "windows", [P, NT, 2], I32)
        place = sb(top, "place", [P, NT])
        starts_i = sb(top, "starts_i", [1, NT], I32)
        bad = sb(top, "bad", [P, 1])
        bad_i = sb(top, "bad_i", [1, 1], I32)
        W1x = sb(top, "W1x", [P, KD, W1COLS])
        W2x = sb(top, "W2x", [P, HID // P, W2COLS])
        b1_col = sb(top, "b1_col", [P, HID // P])
        b2_row = sb(top, "b2_row", [P, D])
        wh = {n: sb(top, f"{n}_hi", [P, NE, KD, FH], F32R) for n in ("fW1", "fW2", "Wo")}
        wl = {n: sb(top, f"{n}_lo", [P, NE, KD, FH], F32R) for n in ("fW1", "fW2", "Wo")}
        scale = [sb(top, f"bn_scale{n}", [P, NE, KH]) for n in (1, 2)]
        shift = [sb(top, f"bn_shift{n}", [P, NE, KH]) for n in (1, 2)]
        Wr_a = sb(top, "Wr_a", [P, KD, 2 * NE], F32R)
        Wr_b = sb(top, "Wr_b", [P, KD, 2 * NE], F32R)
        fold = sb(top, "fold", [2 * NE, NE])
        br_row = sb(top, "br_row", [P, NE])
        bo3 = sb(top, "bo3", [2 * QUAD + NE, D], F32R)

        phase_edges_and_layer1(locals())
        phase_edge_by_edge(locals(), 1)
        phase_aggregate(locals(), 1)
        phase_edge_by_edge(locals(), 2)
        phase_aggregate(locals(), 2)
        phase_experts(locals())


def row_view(table, i, rows=P * SUPER, per=SUPER):
    return table[bass.ds(i * P * SUPER, rows), :].rearrange("(p j) d -> p j d", j=per)


def phase_edges_and_layer1(v):
    nc, sem, sb, ps = v["nc"], v["sem"], v["sb"], v["ps"]
    N, D, E, HEADS, CH, HID, NE, FH = (v[n] for n in ("N", "D", "E", "HEADS", "CH", "HID", "NE", "FH"))
    KD, KH, NSUPER, TAIL, NT, EROWS, ECOLS, NPAD = (v[n] for n in ("KD", "KH", "NSUPER", "TAIL", "NT", "EROWS", "ECOLS", "NPAD"))
    W1COLS, W2COLS = v["W1COLS"], v["W2COLS"]
    ident, iota_row, tile_base, windows = v["ident"], v["iota_row"], v["tile_base"], v["windows"]
    starts_i, bad, bad_i = v["starts_i"], v["bad"], v["bad_i"]
    W1x, W2x, eps_half = v["W1x"], v["W2x"], v["eps_half"]
    edge_list, x = v["edge_list"], v["x"]
    wh, wl, scale, shift = v["wh"], v["wl"], v["scale"], v["shift"]
    HCOLS = W1COLS

    with ExitStack() as ctx:
        S = lambda name: sem("a_" + name, ctx)
        starts = sb(ctx, "starts", [P, NT + 1])
        xin = [sb(ctx, f"xin{b}", [P, SUPER, D]) for b in range(4)]
        z = [sb(ctx, f"z{b}", [P, SUPER, D]) for b in range(2)]
        zT = [sb(ctx, f"zT{b}", [P, KD, SUPER * P]) for b in range(2)]
        hrow = [sb(ctx, f"hrow{b}", [P, SUPER, HCOLS]) for b in range(2)]
        stats = sb(ctx, "stats", [P, SUPER, 6])
        mv = [sb(ctx, f"mv{b}", [P, SUPER, 2]) for b in range(2)]
        vare = [sb(ctx, f"vare{b}", [P, SUPER]) for b in range(2)]
        rstd = [sb(ctx, f"rstd{b}", [P, SUPER]) for b in range(2)]
        ones_bf = sb(ctx, "ones_bf", [P, P], BF16)
        ends = sb(ctx, "ends", [EROWS, 3, ECOLS], I32)
        dstf = sb(ctx, "dstf", [EROWS, 2, ECOLS])
        pairs = sb(ctx, "pairs", [EROWS, ECOLS, 2], I32)
        pad = sb(ctx, "pad", [1, TILE, 2], I32)
        before = sb(ctx, "before", [EROWS, 4, NT], BF16)
        falls = sb(ctx, "falls", [EROWS, ECOLS])
        falls_any = sb(ctx, "falls_any", [EROWS, 1], BF16)
        sizes = sb(ctx, "sizes", [P, NT])
        over = sb(ctx, "over", [P, 2])
        KHID = HID // P
        att = sb(ctx, "att", [P, KHID, 2 * HEADS])
        att2 = sb(ctx, "att2", [P, D // P, 2])
        W1T = sb(ctx, "W1T", [P, KD, KHID, P])
        W2T = sb(ctx, "W2T", [P, KHID, D // P, P])
        stage = {n: sb(ctx, f"stage_{n}", [P, NE, KD, FH]) for n in wh}
        Wr_sb = sb(ctx, "Wr_sb", [P, KD, NE])
        bo_all = sb(ctx, "bo_all", [2 * QUAD + NE, D])
        bn = {n: sb(ctx, f"bn_{n}", [P, NE, KH]) for n in
              ("fb1", "g1", "be1", "m1", "v1", "fb2", "g2", "be2", "m2", "v2")}
        bnt = sb(ctx, "bnt", [P, NE, KH])
        zTp = [ps(ctx, f"zTp{b}", [P, KD, SUPER * P]) for b in range(2)]
        hp = [ps(ctx, f"hp{q}", [P, 512]) for q in range(2)]
        cnt_p = ps(ctx, "cnt_p", [P, 512])
        set_p = ps(ctx, "set_p", [P, 512])

        ends_loaded, params_loaded, bn_loaded = (
            S(n) for n in ("ends_loaded", "params_loaded", "bn_loaded"))
        stage_loaded = {n: S(f"stage_{n}_loaded") for n in wh}
        const_ready, pairs_ready, list_stored = (S(n) for n in ("const_ready", "pairs_ready", "list_stored"))
        before_ready, before_used, counted, falls_ready, starts_ready = (
            S(n) for n in ("before_ready", "before_used", "counted", "falls_ready", "starts_ready"))
        window_loaded = S("window_loaded")
        pe_set, att_ready, dve_set = S("pe_set"), S("att_ready"), S("dve_set")
        x_loaded = [S(f"x_loaded{b}") for b in range(4)]
        h_stored = [S(f"h_stored{b}") for b in range(4)]
        var_ready, rstd_ready, z_ready, zTp_ready, zT_ready, h_ready, hrow_ready = (
            S(n) for n in ("var_ready", "rstd_ready", "z_ready", "zTp_ready", "zT_ready", "h_ready", "hrow_ready"))
        stage_split, dve_chain, pool_chain = S("stage_split"), S("dve_chain"), S("pool_chain")
        last = NSUPER - 1
        names = list(wh)
        split_in_loop = min(NE, (NSUPER - 1) // 4 - 1)
        assert split_in_loop == (NSUPER - 1) // 4 - 1
        in_loop = lambda k: not isinstance(k, int) or 1 <= k <= split_in_loop
        expert = lambda t, e: t[:, bass.ds(e, 1)].rearrange("p o k n -> p (o k n)")
        PARAMS = 16 * (KD + KHID + 2 * HEADS + 2 * (D // P) + 7)

        block = ctx.enter_context(nc.Block())

        @block.sync
        def _(sp):
            sp.wait_ge(const_ready, 1)
            sp.dma_start(ends[:, 0, :], v["src"].rearrange("(p c) -> p c", c=ECOLS)).then_inc(ends_loaded, 16)
            sp.dma_start(ends[:, 1, :], v["dst"].rearrange("(p c) -> p c", c=ECOLS)).then_inc(ends_loaded, 16)
            body = (EROWS - 1) * ECOLS
            sp.dma_start(ends[0:EROWS - 1, 2, :], v["dst"][1:1 + body].rearrange("(p c) -> p c", c=ECOLS)).then_inc(ends_loaded, 16)
            sp.dma_start(ends[EROWS - 1:EROWS, 2, 0:ECOLS - 1],
                         v["dst"][1 + body:E].rearrange("(p c) -> p c", p=1)).then_inc(ends_loaded, 16)
            sp.dma_start(edge_list[E:E + TILE, :].rearrange("(o e) t -> o e t", o=1), pad[:]).then_inc(list_stored, 16)

            def load(i, b, k):
                wait_count(sp, z_ready, i - 3)
                if isinstance(i, int) and i == last:
                    src = row_view(x, i, TAIL)
                    sp.dma_start(xin[b][0:TAIL // SUPER], src).then_inc(x_loaded[b], 16)
                else:
                    sp.dma_start(xin[b][:], row_view(x, i)).then_inc(x_loaded[b], 16)

            def fill_windows(i, b, k):
                if isinstance(i, int) and i == 0:
                    sp.wait_ge(pairs_ready, 1)
                    sp.dma_start(edge_list[0:E, :].rearrange("(p c) t -> p c t", c=ECOLS), pairs[:]).then_inc(list_stored, 16)
                    sp.wait_ge(list_stored, 32)
                    sp.wait_ge(starts_ready, 1)
                for j in range(NT // NSUPER):
                    t = i * (NT // NSUPER) + j
                    first = sp.value_load(starts_i[0:1, bass.ds(t, 1)], min_val=0, max_val=E)
                    sp.dma_start(windows[:, bass.ds(t, 1), :],
                                 edge_list[bass.ds(first, TILE), :].unsqueeze(1)).then_inc(window_loaded, 16)
            ring(sp, NSUPER, load, fill_windows, 4)
            sp.wait_ge(window_loaded, 16 * NT)
            for b in range(4):
                sp.wait_ge(h_stored[b], 16 * (NSUPER // 4))

        @block.gpsimd
        def _(pool):
            nc.gpsimd.iota(iota_row[:], pattern=[[1, TILE]], base=0, channel_multiplier=0,
                           allow_small_or_imprecise_dtypes=True)
            nc.gpsimd.iota(tile_base[:], pattern=[[TILE, NT]], base=0, channel_multiplier=0,
                           allow_small_or_imprecise_dtypes=True)
            nc.gpsimd.memset(ends[:], NOWHERE)
            nc.gpsimd.memset(pad[:, :, 0:1], 0)
            nc.gpsimd.memset(pad[:, :, 1:2], NOWHERE)
            nc.gpsimd.memset(eps_half[:], -0.5)
            nc.gpsimd.memset(ident[:], 0.0).then_inc(pool_chain, 1)
            pool.wait_ge(pool_chain, 1)
            nc.gpsimd.affine_select(out=ident[:], in_=ident[:], compare_op=ALU.not_equal, fill=1.0, base=0,
                                    pattern=[[-1, P]], channel_multiplier=1).then_inc(const_ready, 1)
            pool.wait_ge(ends_loaded, 64)
            nc.gpsimd.tensor_copy(pairs[:, :, 0], ends[:, 0, :])
            nc.gpsimd.tensor_copy(pairs[:, :, 1], ends[:, 1, :]).then_inc(pairs_ready, 1)

            pool.wait_ge(bn_loaded, 320)
            n = 1
            for l in range(2):
                b_, g_, be_, m_, v_ = (bn[q] for q in (("fb1", "g1", "be1", "m1", "v1"), ("fb2", "g2", "be2", "m2", "v2"))[l])
                half = eps_half[:].rearrange("p (e c) -> p e c", c=KH)
                for op in (lambda: nc.gpsimd.tensor_scalar(bnt[:], v_[:], BN_EPS, None, ALU.add),
                           lambda: nc.gpsimd.tensor_tensor(bnt[:], bnt[:], half, ALU.pow),
                           lambda: nc.gpsimd.tensor_tensor(scale[l][:], g_[:], bnt[:], ALU.mult),
                           lambda: nc.gpsimd.tensor_tensor(b_[:], b_[:], m_[:], ALU.subtract),
                           lambda: nc.gpsimd.tensor_tensor(b_[:], b_[:], scale[l][:], ALU.mult),
                           lambda: nc.gpsimd.tensor_tensor(shift[l][:], be_[:], b_[:], ALU.add)):
                    op().then_inc(pool_chain, 1)
                    n += 1
                    pool.wait_ge(pool_chain, n)

            def low_part(e, q):
                name = names[q]
                pool.wait_ge(stage_split, e * len(names) + q + 1)
                nc.gpsimd.tensor_tensor(expert(wl[name], e), expert(stage[name], e), expert(wh[name], e).bitcast(F32), ALU.subtract)

            def power(i, b, k):
                pool.wait_ge(var_ready, i + 1)
                nc.gpsimd.tensor_tensor(rstd[b % 2][:], vare[b % 2][:], eps_half[:, 0:SUPER], ALU.pow).then_inc(rstd_ready, 1)

            def store(i, b, k):
                pool.wait_ge(hrow_ready, (i + 1) * SUPER)
                pool.sem_inc(v["waits_passed"], 1)
                pool.dma_start(row_view(v["h1_table"], i), hrow[b % 2][:]).then_inc(h_stored[b], 16)

            store_before = stores_later(store, NSUPER, 4)

            def back(i, b, k):
                store_before(i, b, k)
                if in_loop(k) and b > 0:
                    low_part(k - 1, b - 1)

            ring(pool, NSUPER, power, back, 4)
            for e in range(split_in_loop, NE):
                for q in range(len(names)):
                    low_part(e, q)

        @block.scalar
        def _(act):
            few = ctx.enter_context(nc.allow_non_contiguous_dma(reason='vectors of parameters, once'))
            for k in range(KD):
                act.dma_start(W1x[:, k, 0:HID], v["W1"][k * P:(k + 1) * P, :]).then_inc(params_loaded, 16)
            for k in range(KHID):
                act.dma_start(W2x[:, k, 0:D], v["W2"][k * P:(k + 1) * P, :]).then_inc(params_loaded, 16)
            act.wait_ge(att_ready, 1)
            for h in range(HEADS):
                for s, a in enumerate((v["as1"], v["ad1"])):
                    c, r = h * CH // P, h * CH % P
                    act.dma_start(att[r:r + CH, c, s * HEADS + h:s * HEADS + h + 1],
                                  a[h:h + 1, :].rearrange("o c -> c o")).then_inc(params_loaded, 16)
            for s, a in enumerate((v["as2"], v["ad2"])):
                for k in range(D // P):
                    act.dma_start(att2[:, k, s:s + 1], a[0:1, k * P:(k + 1) * P].rearrange("o c -> c o")).then_inc(params_loaded, 16)
            act.dma_start(v["b1_col"][:], v["b1"].rearrange("(k c) -> c k", c=P)).then_inc(params_loaded, 16)
            act.dma_start(v["b2_row"][:], v["b2"].partition_broadcast(P)).then_inc(params_loaded, 16)
            act.dma_start(v["br_row"][:], v["br"].partition_broadcast(P)).then_inc(params_loaded, 16)
            for n in range(3):
                act.dma_start(bo_all[n * QUAD:n * QUAD + NE, :], v["bo"]).then_inc(params_loaded, 16)
            act.dma_start(Wr_sb[:], v["Wr"].rearrange("(k p) e -> p k e", p=P)).then_inc(params_loaded, 16)
            for q in bn:
                for k in range(KH):
                    act.dma_start(bn[q][:, :, k], v[q][:, k * P:(k + 1) * P].rearrange("e p -> p e")).then_inc(bn_loaded, 16)

            for name in wh:
                for e in range(NE):
                    act.dma_start(stage[name][:, e], v[name][e].rearrange("(k p) n -> p k n", p=P)).then_inc(stage_loaded[name], 16)

            def high_part(e, q):
                name = names[q]
                act.wait_ge(stage_loaded[name], 16 * NE)
                nc.scalar.activation(expert(wh[name], e), expert(stage[name], e), ACT.Copy).then_inc(stage_split, 1)

            def evac_zT(i, b, k):
                act.wait_ge(zTp_ready, i + 1)
                wait_count(act, h_ready, (i - 1) * SUPER)
                nc.scalar.activation(zT[b % 2][:], zTp[b % 2][:], ACT.Copy).then_inc(zT_ready, 1)

            def evac_h(i, b, k):
                if not (isinstance(i, int) and i < 2):
                    act.wait_ge(h_stored[(b - 2) % 4], 16 * (k if b < 2 else k + 1))
                for j in range(SUPER):
                    act.wait_ge(h_ready, i * SUPER + j + 1)
                    nc.scalar.activation(hrow[b % 2][:, j, :], hp[j % 2][:, 0:HCOLS], ACT.Copy).then_inc(hrow_ready, 1)
                if in_loop(k) and b < len(names):
                    high_part(k - 1, b)

            ring(act, NSUPER, evac_zT, evac_h, 4)
            for e in range(split_in_loop, NE):
                for q in range(len(names)):
                    high_part(e, q)

        @block.vector
        def _(dve):
            setup = Chain(dve, dve_set, 0)
            nc.vector.memset(bo_all[:], 0.0)
            nc.vector.memset(att[:], 0.0).then_inc(att_ready, 1)
            nc.vector.memset(ones_bf[:], 1.0)
            dve.wait_ge(ends_loaded, 64)
            setup.link(nc.vector.tensor_copy(dstf[:], ends[:, 1:3, :]))
            setup.link(nc.vector.tensor_tensor(falls[:], dstf[:, 0, :], dstf[:, 1, :], ALU.is_gt))
            nc.vector.tensor_reduce(falls_any[:], falls[:], axis=AX.X, op=ALU.max).then_inc(falls_ready, 1)
            dve.wait_ge(const_ready, 1)
            for c in range(ECOLS):
                if c >= 4:
                    dve.wait_ge(before_used, c - 3)
                nc.vector.tensor_scalar(before[:, c % 4, :], tile_base[0:EROWS, :], dstf[:, 0, c:c + 1], None,
                                        ALU.is_gt).then_inc(before_ready, 1)
            dve.wait_ge(counted, 1)
            nc.vector.tensor_copy(starts[:, 0:NT], cnt_p[:, 0:NT])
            setup.link(nc.vector.memset(starts[:, NT:NT + 1], float(E)))
            nc.vector.tensor_copy(starts_i[:], starts[0:1, 0:NT])
            setup.link(nc.vector.tensor_tensor(sizes[:], starts[:, 1:NT + 1], starts[:, 0:NT], ALU.subtract))
            setup.link(nc.vector.tensor_reduce(over[:, 0:1], sizes[:], axis=AX.X, op=ALU.max))
            setup.link(nc.vector.tensor_scalar(over[:, 1:2], over[:, 0:1], float(TILE) + 0.5, None, ALU.is_gt))
            setup.link(nc.vector.tensor_tensor(bad[:], cnt_p[:, NT:NT + 1], over[:, 1:2], ALU.add))
            setup.link(nc.vector.tensor_scalar(bad[:], bad[:], 0.5, None, ALU.is_gt))
            nc.vector.tensor_copy(bad_i[:], bad[0:1, :]).then_inc(starts_ready, 1)
            for n, wt in enumerate((W1T, W2T)):
                dve.wait_ge(pe_set, n + 1)
                nc.vector.tensor_copy(wt[:].rearrange("p a b c -> p (a b c)"), set_p[:]).then_inc(att_ready, 1)
            dve.wait_ge(pe_set, 3)
            nc.vector.tensor_copy(W1x[:, :, HID:W1COLS], set_p[:, 0:KD * 2 * HEADS].rearrange("p (k s) -> p k s", k=KD))
            nc.vector.tensor_copy(W2x[:, :, D:W2COLS], set_p[:, 64:64 + 2 * KHID].rearrange("p (k s) -> p k s", k=KHID)).then_inc(att_ready, 1)
            dve.wait_ge(params_loaded, PARAMS)
            hi = v["Wr_a"][:, :, 0:NE]
            nc.vector.memset(v["Wr_b"][:].bitcast(F32), 0.0)
            setup.link(nc.vector.tensor_copy(hi, Wr_sb[:]))
            nc.vector.tensor_copy(v["Wr_b"][:, :, 0:NE], Wr_sb[:])
            nc.vector.tensor_tensor(v["Wr_a"][:, :, NE:2 * NE], Wr_sb[:], hi.bitcast(F32), ALU.subtract)
            nc.vector.tensor_tensor(v["fold"][:], ident[0:2 * NE, 0:NE], ident[0:2 * NE, NE:2 * NE], ALU.add)
            setup.link(nc.vector.tensor_copy(v["bo3"][:], bo_all[:]))
            low_rows = slice(2 * QUAD, 2 * QUAD + NE)
            nc.vector.tensor_tensor(v["bo3"][low_rows, :], bo_all[low_rows, :], v["bo3"][low_rows, :].bitcast(F32), ALU.subtract)

            chain = Chain(dve, dve_chain, 2)

            def moments(i, b, k):
                chain.round(i)
                dve.wait_ge(x_loaded[b], 16 * k + 16)
                for j in range(SUPER):
                    ins = nc.vector.bn_stats(stats[:, j, :], xin[b][:, j, :])
                chain.link(ins)
                dve.sem_inc(v["waits_passed"], 1)
                for j in range(SUPER):
                    ins = nc.vector.bn_aggr(mv[b % 2][:, j, :], stats[:, j, :])
                chain.link(ins)
                chain.close()
                nc.vector.tensor_scalar(vare[b % 2][:], mv[b % 2][:, :, 1], LN_EPS, None, ALU.add).then_inc(var_ready, 1)

            def normalise(i, b, k):
                dve.wait_ge(rstd_ready, i + 1)
                wait_count(dve, zTp_ready, i - 1)
                for j in range(SUPER):
                    ins = nc.vector.tensor_scalar(z[b % 2][:, j, :], xin[b][:, j, :], mv[b % 2][:, j, 0:1], rstd[b % 2][:, j:j + 1],
                                                  ALU.subtract, ALU.mult)
                ins.then_inc(z_ready, 1)

            ring(dve, NSUPER, moments, normalise, 4)

        @block.tensor
        def _(pe):
            for c in range(ECOLS):
                pe.wait_ge(before_ready, c + 1)
                nc.tensor.matmul(cnt_p[:, 0:NT], ones_bf[0:EROWS, :], before[:, c % 4, :], start=(c == 0),
                                 stop=(c == ECOLS - 1)).then_inc(before_used, 1)
            pe.wait_ge(falls_ready, 1)
            nc.tensor.matmul(cnt_p[:, NT:NT + 1], ones_bf[0:EROWS, :], falls_any[:], start=True, stop=True,
                             skip_group_check=True).then_inc(counted, 1)
            pe.wait_ge(params_loaded, PARAMS)
            pe.wait_ge(const_ready, 1)
            for n, (w, inner, outer) in enumerate(((W1x, KD, KHID), (W2x, KHID, D // P))):
                if n:
                    pe.wait_ge(att_ready, n + 1)
                for k in range(inner):
                    for c in range(outer):
                        q = k * outer + c
                        ins = nc.tensor.transpose(set_p[:, q * P:(q + 1) * P], w[:, k, c * P:(c + 1) * P], ident[:])
                ins.then_inc(pe_set, 1)
            pe.wait_ge(att_ready, 3)
            for k in range(KD):
                for c in range(KHID):
                    nc.tensor.matmul(set_p[:, k * 2 * HEADS:(k + 1) * 2 * HEADS], W1T[:, k, c, :], att[:, c, :],
                                     start=(c == 0), stop=(c == KHID - 1))
            for k in range(KHID):
                for c in range(D // P):
                    ins = nc.tensor.matmul(set_p[:, 64 + 2 * k:66 + 2 * k], W2T[:, k, c, :], att2[:, c, :],
                                           start=(c == 0), stop=(c == D // P - 1))
            ins.then_inc(pe_set, 1)
            pe.wait_ge(att_ready, 4)

            def transpose_z(i, b, k):
                pe.wait_ge(z_ready, i + 1)
                wait_count(pe, zT_ready, i - 1)
                for j in range(SUPER):
                    for c in range(KD):
                        ins = nc.tensor.transpose(zTp[b % 2][:, c, j * P:(j + 1) * P], z[b % 2][:, j, c * P:(c + 1) * P], ident[:])
                ins.then_inc(zTp_ready, 1)

            def project(i, b, k):
                pe.wait_ge(zT_ready, i + 1)
                for j in range(SUPER):
                    wait_count(pe, hrow_ready, i * SUPER + j - 1)
                    for c in range(KD):
                        ins = nc.tensor.matmul(hp[j % 2][:, 0:HCOLS], zT[b % 2][:, c, j * P:(j + 1) * P], W1x[:, c, :],
                                               start=(c == 0), stop=(c == KD - 1))
                    ins.then_inc(h_ready, 1)

            ring(pe, NSUPER, transpose_z, project, 4)


def phase_edge_by_edge(v, layer):
    nc, sem, sb = v["nc"], v["sem"], v["sb"]
    E, NT = v["E"], v["NT"]
    H = v["HEADS"] if layer == 1 else 1
    F = v["HID"] if layer == 1 else v["D"]
    COLS = v["W1COLS"] if layer == 1 else v["W2COLS"]
    C = F // H
    table = v["h1_table"] if layer == 1 else v["h2_table"]
    state, edge_list, bad_i = v["softmax_state"], v["edge_list"], v["bad_i"]
    saved = v["saved_rows"]

    with ExitStack() as ctx:
        S = lambda name: sem(f"s{layer}_" + name, ctx)
        T = lambda name, shape, dt=F32: sb(ctx, f"s{layer}_" + name, shape, dt)
        edges = T("edges", [1, E, 2], I32)
        parts = T("parts", [P, 2, H])
        first = T("first", [P, 2, H])
        src_row = T("src_row", [1, COLS])
        row = T("row", [1, COLS])
        st = T("st", [1, 2, H])
        score = T("score", [1, H])
        top = T("top", [1, H])
        df = T("df", [1, 2, H])
        ex = T("ex", [1, 2, H])
        inv = T("inv", [1, H])
        w = T("w", [1, 2, H])
        add = T("add", [1, F])
        edges_loaded, parts_loaded, first_ready, state_stored = (
            S(n) for n in ("edges_loaded", "parts_loaded", "first_ready", "state_stored"))
        rows_loaded, rows_stored, df_ready, ex_ready, row_ready, dve_chain, dve_edge, passed = (
            S(n) for n in ("rows_loaded", "rows_stored", "df_ready", "ex_ready", "row_ready", "dve_chain", "dve_edge", "passed"))
        block = ctx.enter_context(nc.Block())

        @block.sync
        def _(sp):
            with sp.If(sp.value_load(bad_i[0:1, 0:1], min_val=0, max_val=1) > 0):
                sp.dma_start(edges[:], edge_list[0:E, :].unsqueeze(0)).then_inc(edges_loaded, 16)
                with sp.Fori(0, NT) as t:
                    sp.dma_start(parts[:], table[bass.ds(t * P, P), F:F + 2 * H].rearrange("p (s h) -> p s h", s=2)).then_inc(parts_loaded, 16)
                    sp.dma_start(saved[bass.ds(t * P, P), 0:COLS], table[bass.ds(t * P, P), :]).then_inc(state_stored, 16)
                    sp.wait_ge(first_ready, t + 1)
                    sp.dma_start(state[bass.ds(t * P, P), 0:2 * H].rearrange("p (s h) -> p s h", s=2), first[:]).then_inc(state_stored, 16)
                    sp.wait_ge(state_stored, 32 * t + 32)
                    sp.sem_inc(passed, 1)
                sp.wait_ge(edges_loaded, 16)
                with sp.Fori(0, E) as e:
                    s = sp.value_load(edges[0:1, bass.ds(e, 1), 0], min_val=0, max_val=v["N"] - 1)
                    d = sp.value_load(edges[0:1, bass.ds(e, 1), 1], min_val=0, max_val=v["N"] - 1)
                    sp.dma_start(src_row[:], saved[bass.ds(s, 1), 0:COLS]).then_inc(rows_loaded, 16)
                    sp.dma_start(row[:], table[bass.ds(d, 1), :]).then_inc(rows_loaded, 16)
                    sp.dma_start(st[:], state[bass.ds(d, 1), 0:2 * H].rearrange("p (s h) -> p s h", s=2)).then_inc(rows_loaded, 16)
                    sp.wait_ge(row_ready, e + 1)
                    sp.dma_start(table[bass.ds(d, 1), :], row[:]).then_inc(rows_stored, 16)
                    sp.dma_start(state[bass.ds(d, 1), 0:2 * H].rearrange("p (s h) -> p s h", s=2), st[:]).then_inc(rows_stored, 16)
                    sp.wait_ge(rows_stored, 32 * e + 32)
                    sp.sem_inc(passed, 1)

        @block.scalar
        def _(act):
            with act.If(act.value_load(bad_i[0:1, 0:1], min_val=0, max_val=1) > 0):
                with act.Fori(0, E) as e:
                    act.wait_ge(df_ready, e + 1)
                    nc.scalar.activation(ex[:], df[:], ACT.Exp).then_inc(ex_ready, 1)

        @block.vector
        def _(dve):
            with dve.If(dve.value_load(bad_i[0:1, 0:1], min_val=0, max_val=1) > 0):
                init = Chain(dve, dve_chain, 1)
                with dve.Fori(0, NT) as t:
                    init.round(t)
                    dve.wait_ge(parts_loaded, 16 * t + 16)
                    init.link(nc.vector.tensor_tensor(first[:, 0], parts[:, 0], parts[:, 1], ALU.add))
                    nc.vector.scalar_tensor_tensor(out=first[:, 0], in0=first[:, 0], scalar=SLOPE, in1=first[:, 0],
                                                   op0=ALU.mult, op1=ALU.max)
                    nc.vector.memset(first[:, 1], 1.0).then_inc(first_ready, 1)
                chain = Chain(dve, dve_edge, 9)
                with dve.Fori(0, E) as e:
                    chain.round(e)
                    heads = lambda t: t[:, 0:F].rearrange("p (h c) -> p h c", h=H)
                    wide = lambda t: t.unsqueeze(2).broadcast_to([1, H, C])
                    dve.wait_ge(rows_loaded, 48 * e + 48)
                    chain.link(nc.vector.tensor_tensor(score[:], src_row[:, F:F + H], row[:, F + H:F + 2 * H], ALU.add))
                    chain.link(nc.vector.scalar_tensor_tensor(out=score[:], in0=score[:], scalar=SLOPE, in1=score[:],
                                                              op0=ALU.mult, op1=ALU.max))
                    chain.link(nc.vector.tensor_tensor(top[:], st[:, 0], score[:], ALU.max))
                    nc.vector.tensor_tensor(df[:, 0], st[:, 0], top[:], ALU.subtract)
                    nc.vector.tensor_tensor(df[:, 1], score[:], top[:], ALU.subtract).then_inc(df_ready, 1)
                    dve.wait_ge(ex_ready, e + 1)
                    chain.link(nc.vector.tensor_tensor(w[:, 0], st[:, 1], ex[:, 0], ALU.mult))
                    chain.link(nc.vector.tensor_tensor(st[:, 1], w[:, 0], ex[:, 1], ALU.add))
                    chain.link(nc.vector.tensor_scalar(st[:, 0], top[:], 1.0, None, ALU.mult))
                    chain.link(nc.vector.reciprocal(inv[:], st[:, 1]))
                    nc.vector.tensor_tensor(w[:, 0], w[:, 0], inv[:], ALU.mult)
                    chain.link(nc.vector.tensor_tensor(w[:, 1], ex[:, 1], inv[:], ALU.mult))
                    nc.vector.tensor_tensor(heads(add), heads(src_row), wide(w[:, 1]), ALU.mult)
                    chain.link(nc.vector.tensor_tensor(heads(row), heads(row), wide(w[:, 0]), ALU.mult))
                    nc.vector.tensor_tensor(row[:, 0:F], row[:, 0:F], add[:], ALU.add).then_inc(row_ready, 1)
                    chain.close()


def phase_aggregate(v, layer):
    nc, sem, sb, ps = v["nc"], v["sem"], v["sb"], v["ps"]
    N, D, NG = (v[n] for n in ("N", "D", "NG"))
    H = v["HEADS"] if layer == 1 else 1
    F = v["HID"] if layer == 1 else D
    COLS = v["W1COLS"] if layer == 1 else v["W2COLS"]
    C = F // H
    table = v["h1_table"] if layer == 1 else v["h2_table"]
    ident, iota_row, windows, place = v["ident"], v["iota_row"], v["windows"], v["place"]
    KF = F // P
    R = GROUP * H
    ROWS = GROUP * TILE
    SLOTS = 3
    OC = v["W2COLS"] if layer == 1 else D
    AD, ROW, MAX, NEW, SUM = 0, 2 * R, 2 * R + 2 * P, 3 * R + 2 * P, 4 * R + 2 * P
    assert SUM + 2 * R <= 512

    with ExitStack() as ctx:
        S = lambda name: sem(f"g{layer}_" + name, ctx)
        T = lambda name, shape, dt=F32: sb(ctx, f"g{layer}_" + name, shape, dt)
        sources = [T(f"sources{b}", [P, GROUP], I32) for b in range(SLOTS)]
        gat = [T(f"gat{b}", [P, GROUP, COLS]) for b in range(SLOTS)]
        own = [T(f"own{b}", [P, GROUP, COLS]) for b in range(SLOTS)]
        sel = [T(f"sel{b}", [P, GROUP, TILE]) for b in range(SLOTS)]
        selT = T("selT", [P, GROUP, P])
        ad = T("ad", [P, GROUP, 2, H])
        sc = T("sc", [P, 2, GROUP, H])
        rep = T("rep", [P, GROUP, H])
        rows_t = T("rows_t", [R, 2, P])
        news = T("news", [R, P + 1])
        pen = T("pen", [R, P + 1])
        run = T("run", [R, P])
        back_t = T("back_t", [R, P])
        mx = T("mx", [P, GROUP, H])
        df = T("df", [P, 2, GROUP, H])
        ex = [T(f"ex{b}", [P, GROUP, 2, H]) for b in range(SLOTS)]
        w = [T(f"w{b}", [P, 2, GROUP, H]) for b in range(SLOTS)]
        res = [T(f"res{b}", [P, GROUP, OC]) for b in range(SLOTS)]
        bad_far = T("bad_far", [P, 1])
        if layer == 2:
            part = [T(f"part{q}", [P, F]) for q in range(2)]
        else:
            agg = [T(f"agg{q}", [P, F]) for q in range(2)]
            aggT = [T(f"aggT{q}", [P, KF, P]) for q in range(2)]
        selp = ps(ctx, f"g{layer}_selp", [P, GROUP, P])
        small = ps(ctx, f"g{layer}_small", [P, 512])
        SUMS = 2 if layer == 1 else GROUP
        if layer == 1:
            sump = [ps(ctx, f"g1_sump{q}", [P, 512]) for q in range(SUMS)]
            aggp = [ps(ctx, f"g1_aggp{q}", [P, 512]) for q in range(2)]
            outp = ps(ctx, "g1_outp", [P, 512])
            sum_of = lambda u: sump[u % SUMS][:, 0:F]
        else:
            sump = ps(ctx, "g2_sump", [P, SUMS, F])
            sum_of = lambda u: sump[:, u, :]

        gathered = [S(f"gathered{b}") for b in range(SLOTS)]
        own_loaded = [S(f"own_loaded{b}") for b in range(SLOTS)]
        res_stored = [S(f"res_stored{b}") for b in range(SLOTS)]
        place_ready, sel_ready, selp_ready, selT_ready, ad_ready = (
            S(n) for n in ("place_ready", "sel_ready", "selp_ready", "selT_ready", "ad_ready"))
        sc_ready, rows_ready, runs_ready, max_ready, df_ready, exp_ready, ex_ready, msg_ready = (
            S(n) for n in ("sc_ready", "rows_ready", "runs_ready", "max_ready", "df_ready", "exp_ready", "ex_ready", "msg_ready"))
        wsum_ready, w_ready = S("wsum_ready"), S("w_ready")
        sums_ready, agg_ready, dve_chain, tile_chain = (S(n) for n in ("sums_ready", "agg_ready", "dve_chain", "tile_chain"))
        if layer == 1:
            aggp_ready, aggT_ready, outp_ready, out_taken = (S(n) for n in ("aggp_ready", "aggT_ready", "outp_ready", "out_taken"))
        else:
            xb_ready = S("xb_ready")
        pool_chain, bad_ready = S("pool_chain"), S("bad_ready")
        block = ctx.enter_context(nc.Block())

        def tile_rows(table, g, rows=ROWS):
            return table[bass.ds(g * ROWS, rows), :].rearrange("(j p) d -> p j d", p=P)

        def groups(eng, select, weigh, tile, after=0):
            def body(g, b, k):
                for u in range(GROUP + after):
                    tile(g, b, k, u)
                    if u < GROUP and not (isinstance(g, int) and g + 1 >= NG):
                        weigh(g + 1, (b + 1) % SLOTS, k + (b + 1) // SLOTS, u)
                    if u < GROUP and not (isinstance(g, int) and g + 2 >= NG):
                        select(g + 2, (b + 2) % SLOTS, u)
            for u in range(GROUP):
                select(0, 0, u)
            for u in range(GROUP):
                weigh(0, 0, 0, u)
                select(1, 1, u)
            turns = (NG - 2) // SLOTS
            for g in range(SLOTS):
                body(g, g, 0)
            if turns > 1:
                with eng.Fori(1, turns) as k:
                    for b in range(SLOTS):
                        body(SLOTS * k + b, b, k)
            for g in range(SLOTS * turns, NG):
                body(g, g % SLOTS, g // SLOTS)

        @block.sync
        def _(sp):
            def load(g, b, k):
                wait_count(sp, agg_ready, (g - 2) * GROUP)
                sp.dma_start(own[b][:], tile_rows(table, g)).then_inc(own_loaded[b], 16)
                if layer == 2:
                    if not (isinstance(g, int) and g < SLOTS):
                        sp.wait_ge(res_stored[b], 16 * k)
                    if isinstance(g, int) and g == NG - 1:
                        full = (N - g * ROWS) // P
                        rest = N - g * ROWS - full * P
                        sp.dma_start(res[b][:, 0:full], tile_rows(v["x"], g, full * P)).then_inc(own_loaded[b], 16)
                        sp.dma_start(res[b][0:rest, full], v["x"][N - rest:N, :]).then_inc(own_loaded[b], 16)
                    else:
                        sp.dma_start(res[b][:], tile_rows(v["x"], g)).then_inc(own_loaded[b], 16)

            def store(g, b, k):
                if layer == 1:
                    sp.wait_ge(out_taken, (g + 1) * GROUP)
                    sp.dma_start(tile_rows(v["h2_table"], g), res[b][:]).then_inc(res_stored[b], 16)
                else:
                    sp.wait_ge(agg_ready, (g + 1) * GROUP)
                    sp.dma_start(tile_rows(v["x2_table"], g), res[b][:]).then_inc(res_stored[b], 16)

            ring(sp, NG, load, stores_later(store, NG, SLOTS), SLOTS)
            for b in range(SLOTS):
                sp.wait_ge(res_stored[b], 16 * ((NG - b + SLOTS - 1) // SLOTS))

        own_dmas = 1 if layer == 1 else 2

        def own_count(g, k):
            more = 1 if layer == 2 and isinstance(g, int) and g == NG - 1 else 0
            return 16 * own_dmas * k + 16 * (own_dmas + more)

        @block.gpsimd
        def _(pool):
            nc.gpsimd.memset(news[:], 1.0).then_inc(place_ready, 1)

            def gather(g, b, k):
                wait_count(pool, sums_ready, (g - 2) * GROUP)
                nc.gpsimd.tensor_copy(sources[b][:], windows[:, bass.ds(g * GROUP, GROUP), 0]).then_inc(pool_chain, 1)
                hold(pool, pool_chain, g + 1, v["waits_passed"])
                for j in range(GROUP):
                    pool.indirect_dma_start(gat[b][:, j, :], None, table,
                                            bass.IndirectOffsetOnAxis(ap=sources[b][:, j:j + 1], axis=0)).then_inc(gathered[b], 16)

            def residual(g, b, k):
                if layer == 2:
                    pool.wait_ge(own_loaded[b], own_count(g, k))
                    nc.gpsimd.tensor_tensor(res[b][:], res[b][:], v["b2_row"][:].unsqueeze(1).broadcast_to([P, GROUP, D]),
                                            ALU.add).then_inc(xb_ready, 1)

            ring(pool, NG, gather, residual, SLOTS)

        @block.scalar
        def _(act):
            def select(g, b, u):
                if u == 6:
                    act.wait_ge(selp_ready, g + 1)
                    wait_count(act, ad_ready, g)
                    for q in range(2):
                        ins = nc.scalar.activation(selT[:, q * 4:q * 4 + 4, :], selp[:, q * 4:q * 4 + 4, :], ACT.Copy)
                    ins.then_inc(selT_ready, 1)

            def weigh(g, b, k, u):
                if u == 3:
                    act.wait_ge(df_ready, g + 1)
                    nc.scalar.activation(ex[b][:].rearrange("p j s h -> p s j h"), df[:], ACT.Exp).then_inc(exp_ready, 1)

            def tile(g, b, k, u):
                if layer == 2:
                    return
                n = g * GROUP + u
                if 1 <= u <= GROUP:
                    act.wait_ge(aggp_ready, n)
                    for c in range(KF):
                        ins = nc.scalar.activation(aggT[(u - 1) % 2][:, c, :], aggp[(u - 1) % 2][:, c * P:(c + 1) * P], ACT.Relu,
                                                   bias=v["b1_col"][:, c:c + 1])
                    ins.then_inc(aggT_ready, 1)
                if u >= 2:
                    act.wait_ge(outp_ready, n - 1)
                    if u == 2 and not (isinstance(g, int) and g < SLOTS):
                        act.wait_ge(res_stored[b], 16 * k)
                    nc.scalar.activation(res[b][:, u - 2, :], outp[:, 0:OC], ACT.Copy).then_inc(out_taken, 1)

            groups(act, select, weigh, tile, 2)

        @block.vector
        def _(dve):
            nc.vector.tensor_scalar(bad_far[:], v["bad"][:], float(NOWHERE), None, ALU.mult).then_inc(bad_ready, 1)
            dve.wait_ge(bad_ready, 1)
            nc.vector.scalar_tensor_tensor(out=place[:], in0=windows[:, :, 1], scalar=bad_far[:, 0:1], in1=v["tile_base"][:],
                                           op0=ALU.add, op1=ALU.subtract).then_inc(place_ready, 1)
            dve.wait_ge(place_ready, 2)
            chain = Chain(dve, dve_chain, 10)
            chain_t = Chain(dve, tile_chain, 2 if layer == 1 else 1)
            heads = lambda t: t.rearrange("p (h c) -> p h c", h=H)

            def select(g, b, u):
                if u == 5:
                    wait_count(dve, sums_ready, (g - 2) * GROUP)
                    for j in range(GROUP):
                        ins = nc.vector.tensor_scalar(sel[b][:, j, :], iota_row[:], place[:, bass.ds(g * GROUP + j, 1)], None,
                                                      ALU.is_equal)
                    ins.then_inc(sel_ready, 1)

            def weigh(g, b, k, u):
                if u == 1:
                    chain.round(g)
                    dve.wait_ge(ad_ready, g + 1)
                    chain.link(nc.vector.tensor_copy(ad[:], small[:, AD:AD + 2 * R].rearrange("p (j s h) -> p j s h", j=GROUP, s=2)))
                    nc.vector.tensor_scalar(rep[:], place[:, bass.ds(g * GROUP, GROUP)].unsqueeze(2).broadcast_to([P, GROUP, H]),
                                            1.0, None, ALU.mult)
                    dve.wait_ge(gathered[b], 16 * GROUP * k + 16 * GROUP)
                    nc.vector.tensor_tensor(sc[:, 0], gat[b][:, :, F:F + H], ad[:, :, 1, :], ALU.add)
                    chain.link(nc.vector.tensor_tensor(sc[:, 1], ad[:, :, 0, :], ad[:, :, 1, :], ALU.add))
                    nc.vector.scalar_tensor_tensor(out=sc[:], in0=sc[:], scalar=SLOPE, in1=sc[:], op0=ALU.mult,
                                                   op1=ALU.max).then_inc(sc_ready, 1)
                if u == 2:
                    dve.wait_ge(rows_ready, g + 1)
                    chain.link(nc.vector.tensor_copy(rows_t[:], small[0:R, ROW:ROW + 2 * P].rearrange("r (s e) -> r s e", s=2)))
                    chain.link(nc.vector.tensor_tensor(news[:, 1:P], rows_t[:, 1, 1:P], rows_t[:, 1, 0:P - 1], ALU.not_equal))
                    chain.link(nc.vector.tensor_scalar(pen[:], news[:, 0:P + 1], -BIG, None, ALU.mult))
                    chain.link(nc.vector.tensor_tensor_scan(run[:], pen[:, 0:P], rows_t[:, 0, :], -BIG, ALU.add, ALU.max))
                    nc.vector.tensor_tensor_scan(back_t[:, ::-1], pen[:, 1:P + 1][:, ::-1], run[:, ::-1], -BIG, ALU.add,
                                                 ALU.max).then_inc(runs_ready, 1)
                if u == 3:
                    dve.wait_ge(max_ready, g + 1)
                    chain.link(nc.vector.tensor_tensor(mx[:], small[:, MAX:MAX + R].rearrange("p (j h) -> p j h", j=GROUP), sc[:, 1], ALU.max))
                    chain.link(nc.vector.tensor_tensor(df[:], sc[:], mx[:].unsqueeze(1).broadcast_to([P, 2, GROUP, H]), ALU.subtract))
                    nc.vector.tensor_scalar(df[:], df[:], 0.0, None, ALU.min).then_inc(df_ready, 1)
                if u == 4:
                    dve.wait_ge(exp_ready, g + 1)
                    nc.vector.scalar_tensor_tensor(
                        out=ex[b][:, :, 1, :], in0=ex[b][:, :, 1, :], scalar=-1.0,
                        in1=small[:, NEW:NEW + R].rearrange("p (j h) -> p j h", j=GROUP), op0=ALU.add, op1=ALU.mult).then_inc(ex_ready, 1)
                    nc.vector.tensor_tensor(
                        gat[b][:, :, 0:F].rearrange("p j (h c) -> p j h c", h=H), gat[b][:, :, 0:F].rearrange("p j (h c) -> p j h c", h=H),
                        ex[b][:, :, 0, :].unsqueeze(3).broadcast_to([P, GROUP, H, C]), ALU.mult).then_inc(msg_ready, 1)
                if u == 6:
                    sums = small[:, SUM:SUM + 2 * R].rearrange("p (j s h) -> p s j h", j=GROUP, s=2)
                    dve.wait_ge(wsum_ready, g + 1)
                    chain.link(nc.vector.tensor_scalar(w[b][:, 0], sums[:, 1], 1.0, None, ALU.add))
                    chain.link(nc.vector.tensor_tensor(w[b][:, 1], w[b][:, 0], sums[:, 0], ALU.add))
                    nc.vector.reciprocal(w[b][:, 1], w[b][:, 1]).then_inc(w_ready, 1)
                    chain.close()

            def tile(g, b, k, u):
                chain_t.round(g * GROUP + u)
                mine, q = own[b][:, u, 0:F], u % 2
                if u == 0:
                    dve.wait_ge(w_ready, g + 1)
                    if layer == 2:
                        dve.wait_ge(xb_ready, g + 1)
                if layer == 1:
                    wait_count(dve, aggp_ready, g * GROUP + u - 1)
                    chain_t.link(nc.vector.tensor_tensor(heads(agg[q][:]), heads(mine),
                                                         w[b][:, 0, u, :].unsqueeze(2).broadcast_to([P, H, C]), ALU.mult))
                dve.wait_ge(sums_ready, g * GROUP + (u if layer == 1 else u | 1) + 1)
                if layer == 1:
                    chain_t.link(nc.vector.tensor_tensor(agg[q][:], sum_of(u), agg[q][:], ALU.add))
                    nc.vector.tensor_tensor(heads(agg[q][:]), heads(agg[q][:]), w[b][:, 1, u, :].unsqueeze(2).broadcast_to([P, H, C]),
                                            ALU.mult).then_inc(agg_ready, 1)
                else:
                    chain_t.link(nc.vector.scalar_tensor_tensor(out=part[q][:], in0=mine, scalar=w[b][:, 0, u, 0:1],
                                                                in1=sum_of(u), op0=ALU.mult, op1=ALU.add))
                    nc.vector.scalar_tensor_tensor(out=res[b][:, u, :], in0=part[q][:], scalar=w[b][:, 1, u, 0:1],
                                                   in1=res[b][:, u, :], op0=ALU.mult, op1=ALU.add).then_inc(agg_ready, 1)
                chain_t.close()

            groups(dve, select, weigh, tile)

        @block.tensor
        def _(pe):
            def select(g, b, u):
                if u == 6:
                    pe.wait_ge(sel_ready, g + 1)
                    wait_count(pe, selT_ready, g)
                    for j in range(GROUP):
                        ins = nc.tensor.transpose(selp[:, j, :], sel[b][:, j, :], ident[:])
                    ins.then_inc(selp_ready, 1)

            def weigh(g, b, k, u):
                if u == 0:
                    pe.wait_ge(selT_ready, g + 1)
                    pe.wait_ge(own_loaded[b], own_count(g, k))
                    wait_count(pe, w_ready, g)
                    for j in range(GROUP):
                        ins = nc.tensor.matmul(small[:, AD + j * 2 * H:AD + (j + 1) * 2 * H], selT[:, j, :], own[b][:, j, F:F + 2 * H],
                                               start=True, stop=True)
                    ins.then_inc(ad_ready, 1)
                if u == 2:
                    pe.wait_ge(sc_ready, g + 1)
                    nc.tensor.transpose(small[0:R, ROW:ROW + P], sc[:, 0].rearrange("p j h -> p (j h)"), ident[:])
                    nc.tensor.transpose(small[0:R, ROW + P:ROW + 2 * P], rep[:].rearrange("p j h -> p (j h)"), ident[:]).then_inc(rows_ready, 1)
                if u == 3:
                    hold(pe, runs_ready, g + 1, v["waits_passed"])
                    nc.tensor.transpose(small[:, MAX:MAX + R], back_t[:], ident[0:R, 0:R])
                    nc.tensor.transpose(small[:, NEW:NEW + R], news[:, 0:P], ident[0:R, 0:R]).then_inc(max_ready, 1)
                if u == 5:
                    pe.wait_ge(ex_ready, g + 1)
                    for j in range(GROUP):
                        ins = nc.tensor.matmul(small[:, SUM + j * 2 * H:SUM + (j + 1) * 2 * H], sel[b][:, j, :],
                                               ex[b][:, j].rearrange("p s h -> p (s h)"), start=True, stop=True)
                    ins.then_inc(wsum_ready, 1)

            def sums(g, b, t):
                if t == 0:
                    pe.wait_ge(msg_ready, g + 1)
                wait_count(pe, agg_ready, g * GROUP + t - 1 if layer == 1 else (g - 1) * GROUP + (t | 1) + 1)
                nc.tensor.matmul(sum_of(t), sel[b][:, t, :], gat[b][:, t, 0:F], start=True, stop=True).then_inc(sums_ready, 1)

            def tile(g, b, k, u):
                if layer == 2:
                    for t in {0: (0, 1), 1: (2, 3), 3: (4, 5), 4: (6, 7)}.get(u, ()):
                        sums(g, b, t)
                    return
                n = g * GROUP + u
                if 1 <= u <= GROUP:
                    q = (u - 1) % 2
                    pe.wait_ge(agg_ready, n)
                    wait_count(pe, aggT_ready, n - 2)
                    for c in range(KF):
                        ins = nc.tensor.transpose(aggp[q][:, c * P:(c + 1) * P], agg[q][:, c * P:(c + 1) * P], ident[:])
                    ins.then_inc(aggp_ready, 1)
                if isinstance(g, int) and g == 0 and u == 0:
                    sums(0, 0, 0)
                    sums(0, 0, 1)
                if 1 <= u < GROUP - 1:
                    sums(g, b, u + 1)
                if u in (GROUP - 1, GROUP) and not (isinstance(g, int) and g + 1 >= NG):
                    sums(g + 1, (b + 1) % SLOTS, u - GROUP + 1)
                if u >= 2:
                    q = u % 2
                    pe.wait_ge(aggT_ready, n - 1)
                    wait_count(pe, out_taken, n - 2)
                    for c in range(KF):
                        ins = nc.tensor.matmul(outp[:, 0:OC], aggT[q][:, c, :], v["W2x"][:, c, :],
                                               start=(c == 0), stop=(c == KF - 1))
                    ins.then_inc(outp_ready, 1)

            groups(pe, select, weigh, tile, 0 if layer == 2 else 2)


def phase_experts(v):
    nc, sem, sb, ps = v["nc"], v["sem"], v["sb"], v["ps"]
    D, NE, FH, KD, KH, NSUPER, TAIL = (v[n] for n in ("D", "NE", "FH", "KD", "KH", "NSUPER", "TAIL"))
    ident, wh, wl, scale, shift = v["ident"], v["wh"], v["wl"], v["scale"], v["shift"]
    last = NSUPER - 1
    with ExitStack() as ctx:
        S = lambda name: sem("e_" + name, ctx)
        T = lambda name, shape, dt=F32: sb(ctx, "e_" + name, shape, dt)
        xin = [T(f"xin{b}", [P, SUPER, D]) for b in range(2)]
        z = T("z", [P, SUPER, D])
        z_hi = [T(f"z_hi{b}", [P, KD, SUPER * P], F32R) for b in range(2)]
        z_lo = [T(f"z_lo{b}", [P, KD, SUPER * P], F32R) for b in range(2)]
        stats = T("stats", [P, SUPER, 6])
        mv = T("mv", [P, SUPER, 2])
        vare = T("vare", [P, SUPER])
        rstd = T("rstd", [P, SUPER])
        logit = T("logit", [P, SUPER, NE])
        top1 = T("top1", [P, SUPER])
        tot = T("tot", [P, SUPER])
        share = [T(f"share{b}", [P, SUPER, NE]) for b in range(2)]
        share3 = T("share3", [P, SUPER, 2 * QUAD + NE], F32R)
        shareT = T("shareT", [2 * QUAD + NE, SUPER * P], F32R)
        logitT = T("logitT", [2 * NE, SUPER * P])
        acc = [T(f"acc{b}", [P, SUPER, D]) for b in range(2)]
        h = [T(f"h{l}", [P, KH, SUPER * P]) for l in (1, 2)]
        h_hi = [T(f"h{l}_hi", [P, KH, SUPER * P], F32R) for l in (1, 2)]
        h_lo = [T(f"h{l}_lo", [P, KH, SUPER * P], F32R) for l in (1, 2)]
        up = [ps(ctx, f"e_u{l}", [P, KH, 512]) for l in (1, 2)]
        yp = ps(ctx, "e_y", [P, SUPER, D])
        misc = ps(ctx, "e_misc", [P, 2, 512])
        x_loaded = [S(f"x_loaded{b}") for b in range(2)]
        out_stored = [S(f"out_stored{b}") for b in range(2)]
        (var_ready, rstd_ready, z_ready, zT_ready, z_hi_ready, z_lo_ready, logit_ready, exp_in, exp_ready, share_ready,
         shareT_p, shareT_ready, logitT_p, logitT_ready, bias_ready, acc_ready, dve_chain) = (
            S(n) for n in ("var_ready", "rstd_ready", "z_ready", "zT_ready", "z_hi_ready", "z_lo_ready", "logit_ready", "exp_in",
                           "exp_ready", "share_ready", "shareT_p", "shareT_ready", "logitT_p", "logitT_ready", "bias_ready", "acc_ready", "dve_chain"))
        u_ready = [S(f"u{l}_ready") for l in (1, 2)]
        hi_ready = [S(f"h{l}_hi_ready") for l in (1, 2)]
        lo_ready = [S(f"h{l}_lo_ready") for l in (1, 2)]
        y_ready, y_taken = S("y_ready"), S("y_taken")
        width = lambda i: 1 if isinstance(i, int) and i == last else SUPER
        HALVES = 2
        halves = lambda i: 1 if isinstance(i, int) and i == last else HALVES

        def half_count(i, e, q):
            if isinstance(i, int) and i == last:
                return last * NE * HALVES + e + 1
            return (i * NE + e) * HALVES + q + 1


        def experts(eng, ahead, step):
            def body(i, b, k):
                for e in range(NE):
                    step(i, b, k, e)
                    if not (isinstance(i, int) and i == last):
                        ahead(i + 1, 1 - b, k + b, e)
            for e in range(NE):
                ahead(0, 0, 0, e)
            step(0, 0, 0, -1)
            body(0, 0, 0)
            body(1, 1, 0)
            turns = (NSUPER - 1) // 2
            with eng.Fori(1, turns) as k:
                body(2 * k, 0, k)
                body(2 * k + 1, 1, k)
            for i in range(2 * turns, NSUPER):
                body(i, i % 2, i // 2)

        block = ctx.enter_context(nc.Block())

        @block.sync
        def _(sp):
            def load(i, b, k):
                wait_count(sp, acc_ready, i - 1)
                if isinstance(i, int) and i == last:
                    sp.dma_start(xin[b][:, 0:1, :], row_view(v["x2_table"], i, P, 1)).then_inc(x_loaded[b], 16)
                else:
                    sp.dma_start(xin[b][:], row_view(v["x2_table"], i)).then_inc(x_loaded[b], 16)

            def store(i, b, k):
                sp.wait_ge(y_taken, half_count(i, NE - 1, halves(i) - 1))
                if isinstance(i, int) and i == last:
                    sp.dma_start(row_view(v["out"], i, TAIL, 1), acc[b][0:TAIL, 0:1, :]).then_inc(out_stored[b], 16)
                else:
                    sp.dma_start(row_view(v["out"], i), acc[b][:]).then_inc(out_stored[b], 16)

            ring(sp, NSUPER, load, stores_later(store, NSUPER))
            for b in range(2):
                sp.wait_ge(out_stored[b], 16 * (NSUPER // 2))

        @block.gpsimd
        def _(pool):
            def power(i, b, k):
                pool.wait_ge(var_ready, i + 1)
                nc.gpsimd.tensor_tensor(rstd[:], vare[:], v["eps_half"][:, 0:SUPER], ALU.pow).then_inc(rstd_ready, 1)
            ring(pool, NSUPER, power, lambda i, b, k: None)

        @block.scalar
        def _(act):
            def ahead(i, b, k, n):
                w = width(i) * P
                if n == 2:
                    act.wait_ge(zT_ready, i + 1)
                    for c in range(KD):
                        ins = nc.scalar.activation(z_hi[b][:, c, 0:w], misc[:, c, 0:w], ACT.Copy)
                    ins.then_inc(z_hi_ready, 1)
                if n == 3:
                    act.wait_ge(logitT_p, i + 1)
                    nc.scalar.activation(logitT[:, 0:w], misc[0:2 * NE, 0, 0:w], ACT.Copy).then_inc(logitT_ready, 1)
                if n == 5:
                    act.wait_ge(exp_in, i + 1)
                    nc.scalar.activation(share[b][:], logit[:], ACT.Exp).then_inc(exp_ready, 1)

            def relu(l, i, e, last_w):
                for c in range(KH):
                    act.wait_ge(u_ready[l], (i * NE + e) * KH + c + 1)
                    for o in (h[l], h_hi[l]):
                        ins = nc.scalar.activation(o[:, c, 0:last_w], up[l][:, c, 0:last_w], ACT.Relu,
                                                   bias=shift[l][:, e, c:c + 1], scale=scale[l][:, e, c:c + 1])
                    ins.then_inc(hi_ready[l], 1)

            def step(i, b, k, e):
                if e >= 0:
                    relu(1, i, e, width(i) * P)
                if e + 1 < NE:
                    relu(0, i, e + 1, width(i) * P)
                elif not (isinstance(i, int) and i == last):
                    relu(0, i + 1, 0, width(i + 1) * P)

            experts(act, ahead, step)

        @block.vector
        def _(dve):
            chain = Chain(dve, dve_chain, 8)
            nc.vector.memset(share3[:].bitcast(F32), 0.0)

            def ahead(i, b, k, n):
                w = width(i)
                if n == 0:
                    chain.round(i)
                    dve.wait_ge(x_loaded[b], 16 * k + 16)
                    for j in range(w):
                        ins = nc.vector.bn_stats(stats[:, j, :], xin[b][:, j, :])
                    chain.link(ins)
                    dve.sem_inc(v["waits_passed"], 1)
                    for j in range(w):
                        ins = nc.vector.bn_aggr(mv[:, j, :], stats[:, j, :])
                    chain.link(ins)
                    nc.vector.tensor_scalar(vare[:], mv[:, :, 1], LN_EPS, None, ALU.add).then_inc(var_ready, 1)
                if n == 1:
                    dve.wait_ge(rstd_ready, i + 1)
                    for j in range(w):
                        ins = nc.vector.tensor_scalar(z[:, j, :], xin[b][:, j, :], mv[:, j, 0:1], rstd[:, j:j + 1],
                                                      ALU.subtract, ALU.mult)
                    ins.then_inc(z_ready, 1)
                if n == 2:
                    dve.wait_ge(z_hi_ready, i + 1)
                    for c in range(KD):
                        ins = nc.vector.tensor_tensor(z_lo[b][:, c, 0:w * P], misc[:, c, 0:w * P],
                                                      z_hi[b][:, c, 0:w * P].bitcast(F32), ALU.subtract)
                    ins.then_inc(z_lo_ready, 1)
                if n == 4:
                    dve.wait_ge(logit_ready, i + 1)
                    lg = misc[:, 0, 0:w * NE].rearrange("p (j e) -> p j e", j=w)
                    chain.link(nc.vector.tensor_tensor(logit[:, 0:w], lg, v["br_row"][:].unsqueeze(1).broadcast_to([P, w, NE]), ALU.add))
                    chain.link(nc.vector.tensor_reduce(top1[:, 0:w], logit[:, 0:w], axis=AX.X, op=ALU.max))
                    nc.vector.tensor_tensor(logit[:, 0:w], logit[:, 0:w], top1[:, 0:w].unsqueeze(2).broadcast_to([P, w, NE]),
                                            ALU.subtract).then_inc(exp_in, 1)
                if n == 5:
                    dve.wait_ge(exp_ready, i + 1)
                    chain.link(nc.vector.tensor_reduce(tot[:, 0:w], share[b][:, 0:w], axis=AX.X, op=ALU.add))
                    chain.link(nc.vector.reciprocal(tot[:, 0:w], tot[:, 0:w]))
                    chain.link(nc.vector.tensor_tensor(share[b][:, 0:w], share[b][:, 0:w],
                                                       tot[:, 0:w].unsqueeze(2).broadcast_to([P, w, NE]), ALU.mult))
                    high, low_, again = (share3[:, 0:w, q * QUAD:q * QUAD + NE] for q in range(3))
                    nc.vector.tensor_copy(again, share[b][:, 0:w])
                    chain.link(nc.vector.tensor_copy(high, share[b][:, 0:w]))
                    nc.vector.tensor_tensor(low_, share[b][:, 0:w], high.bitcast(F32), ALU.subtract).then_inc(share_ready, 1)
                    chain.close()
                if n == 6:
                    dve.wait_ge(shareT_p, i + 1)
                    nc.vector.tensor_copy(shareT[:, 0:w * P], misc[0:2 * QUAD + NE, 1, 0:w * P]).then_inc(shareT_ready, 1)
                if n == 7:
                    dve.wait_ge(bias_ready, i + 1)
                    if not (isinstance(i, int) and i < 2):
                        dve.wait_ge(out_stored[b], 16 * k)
                    both = misc[:].rearrange("p q (j d) -> p (q j) d", d=D)
                    nc.vector.tensor_tensor(acc[b][:, 0:w], both[:, 0:w], xin[b][:, 0:w], ALU.add).then_inc(acc_ready, 1)

            def low(l, i, e, w):
                for c in range(KH):
                    dve.wait_ge(hi_ready[l], (i * NE + e) * KH + c + 1)
                    nc.vector.tensor_tensor(h_lo[l][:, c, 0:w], h[l][:, c, 0:w], h_hi[l][:, c, 0:w].bitcast(F32),
                                            ALU.subtract).then_inc(lo_ready[l], 1)

            def step(i, b, k, e):
                w = width(i)
                if e >= 0:
                    low(1, i, e, w * P)
                if e + 1 < NE:
                    low(0, i, e + 1, w * P)
                elif not (isinstance(i, int) and i == last):
                    low(0, i + 1, 0, width(i + 1) * P)
                if e < 0:
                    return
                dve.wait_ge(acc_ready, i + 1)
                for q in range(halves(i)):
                    dve.wait_ge(y_ready, half_count(i, e, q))
                    if e:
                        dve.wait_ge(y_taken, half_count(i, e - 1, q))
                    for j in range(q * 2, min(q * 2 + 2, w)):
                        ins = nc.vector.scalar_tensor_tensor(out=acc[b][:, j, :], in0=yp[:, j, :], scalar=share[b][:, j, e:e + 1],
                                                             in1=acc[b][:, j, :], op0=ALU.mult, op1=ALU.add)
                    ins.then_inc(y_taken, 1)

            experts(dve, ahead, step)

        @block.tensor
        def _(pe):
            def ahead(i, b, k, n):
                w = width(i)
                if n == 2:
                    pe.wait_ge(z_ready, i + 1)
                    wait_count(pe, acc_ready, i)
                    for j in range(w):
                        for c in range(KD):
                            ins = nc.tensor.transpose(misc[:, c, j * P:(j + 1) * P], z[:, j, c * P:(c + 1) * P], ident[:])
                    ins.then_inc(zT_ready, 1)
                if n == 3:
                    pe.wait_ge(z_lo_ready, i + 1)
                    terms = [(ww, zz, c) for c in range(KD) for ww, zz in ((v["Wr_a"], z_hi[b]), (v["Wr_b"], z_lo[b]))]
                    for n_, (ww, zz, c) in enumerate(terms):
                        ins = nc.tensor.matmul(misc[0:2 * NE, 0, 0:w * P], ww[:, c, :], zz[:, c, 0:w * P],
                                               start=(n_ == 0), stop=(n_ == len(terms) - 1))
                    ins.then_inc(logitT_p, 1)
                if n == 4:
                    pe.wait_ge(logitT_ready, i + 1)
                    for j in range(w):
                        ins = nc.tensor.matmul(misc[:, 0, j * NE:(j + 1) * NE], logitT[:, j * P:(j + 1) * P], v["fold"][:],
                                               start=True, stop=True)
                    ins.then_inc(logit_ready, 1)
                if n == 6:
                    pe.wait_ge(share_ready, i + 1)
                    for j in range(w):
                        ins = nc.tensor.transpose(misc[0:2 * QUAD + NE, 1, j * P:(j + 1) * P], share3[:, j, :].bitcast(F32), ident[:])
                    ins.then_inc(shareT_p, 1)
                if n == 7:
                    pe.wait_ge(shareT_ready, i + 1)
                    both = misc[:].rearrange("p q (j d) -> p (q j) d", d=D)
                    for j in range(w):
                        ins = nc.tensor.matmul(both[:, j, :], shareT[:, j * P:(j + 1) * P], v["bo3"][:], start=True, stop=True)
                    ins.then_inc(bias_ready, 1)

            def dense(l, i, e, rhs_hi, rhs_lo, name, w, chunks):
                for c in range(chunks):
                    terms = [(ww, rr, k) for k in range(KD) for ww, rr in
                             ((wh[name], rhs_hi), (wl[name], rhs_hi), (wh[name], rhs_lo))]
                    for n, (ww, rr, k) in enumerate(terms):
                        ins = nc.tensor.matmul(up[l][:, c, 0:w], ww[:, e, k, c * P:(c + 1) * P], rr[:, k, 0:w],
                                               start=(n == 0), stop=(n == len(terms) - 1))
                    ins.then_inc(u_ready[l], 1)

            def step(i, b, k, e):
                w = width(i)
                if e >= 0:
                    pe.wait_ge(lo_ready[0], (i * NE + e + 1) * KH)
                    dense(1, i, e, h_hi[0], h_lo[0], "fW2", w * P, KH)
                if e + 1 < NE:
                    if e < 0:
                        pe.wait_ge(z_lo_ready, i + 1)
                    dense(0, i, e + 1, z_hi[b], z_lo[b], "fW1", w * P, KH)
                elif not (isinstance(i, int) and i == last):
                    dense(0, i + 1, 0, z_hi[1 - b], z_lo[1 - b], "fW1", width(i + 1) * P, KH)
                if e < 0:
                    return
                pe.wait_ge(lo_ready[1], (i * NE + e + 1) * KH)
                for q in range(halves(i)):
                    if e:
                        pe.wait_ge(y_taken, half_count(i, e - 1, q))
                    elif not (isinstance(i, int) and i == 0):
                        pe.wait_ge(y_taken, (i * NE - 1) * HALVES + q + 1)
                    for j in range(q * 2, min(q * 2 + 2, w)):
                        terms = [(hh, ww, k) for k in range(KH) for hh, ww in
                                 ((h_hi[1], wh["Wo"]), (h_hi[1], wl["Wo"]), (h_lo[1], wh["Wo"]))]
                        for n, (hh, ww, c) in enumerate(terms):
                            ins = nc.tensor.matmul(yp[:, j, :], hh[:, c, j * P:(j + 1) * P], ww[:, e, c, :],
                                                   start=(n == 0), stop=(n == len(terms) - 1))
                    ins.then_inc(y_ready, 1)

            experts(pe, ahead, step)


_INS = ["x", "src", "dst", "L0_gnn_W1", "L0_gnn_att_src1", "L0_gnn_att_dst1", "L0_gnn_b1", "L0_gnn_W2", "L0_gnn_att_src2",
        "L0_gnn_att_dst2", "L0_gnn_b2", "L0_ffn_Wr", "L0_ffn_br", "L0_ffn_W1", "L0_ffn_b1", "L0_ffn_g1", "L0_ffn_be1",
        "L0_ffn_m1", "L0_ffn_v1", "L0_ffn_W2", "L0_ffn_b2", "L0_ffn_g2", "L0_ffn_be2", "L0_ffn_m2", "L0_ffn_v2",
        "L0_ffn_Wo", "L0_ffn_bo"]


def kernel(**inputs):
    import numpy as _np
    import concourse.bacc as _bacc
    from concourse import mybir as _mybir
    from concourse.bass_utils import run_bass_kernel_spmd as _run

    nc = _bacc.Bacc("TRN2", target_bir_lowering=False, num_devices=1)
    arrays, args = {}, []
    for name in _INS:
        a = _np.ascontiguousarray(inputs[name])
        arrays[f"in_{name}"] = a
        args.append(nc.dram_tensor(f"in_{name}", a.shape, _mybir.dt.from_np(a.dtype), kind="ExternalInput").ap())
    shape = inputs["x"].shape
    args.append(nc.dram_tensor("out_0", shape, _mybir.dt.float32, kind="ExternalOutput").ap())
    gnn_ffn(nc, *args)
    r = _run(nc, [arrays], core_ids=[0])
    return r.results[0]["out_0"]
```
